# Optimizing a Trainium2 kernel written in Bass

```python
import numpy as np
import jax
import jax.numpy as jnp

def _softmax(x, axis=-1):
    return jax.nn.softmax(x, axis=axis)

def _gelu(x):
    return jax.nn.gelu(x, approximate=True)

def _silu(x):
    return jax.nn.silu(x)

def _sigmoid(x):
    return jax.nn.sigmoid(x)

def _layernorm(x, axis=-1, eps=1e-05):
    m = jnp.mean(x, axis=axis, keepdims=True)
    v = jnp.var(x, axis=axis, keepdims=True)
    return (x - m) / jnp.sqrt(v + eps)

def _scatter_add(tgt, idx, src, axis=0):
    return tgt.at[idx].add(src)

def _segment_sum(src, seg, n):
    return jax.ops.segment_sum(src, seg, n)
kernel_name = 'mk_seq_postln_d2_jaxref_r4_ca66f6'

def setup_inputs(seed: int=0):
    np.random.seed(seed)
    _w = jnp.asarray

    def _L0_attn_setup():
        import jax, jax.numpy as jnp
        import numpy as np
        NUM_HEADS = 16
        WINDOW = 128

        def apply_rope(x):
            S, Dh = (x.shape[-2], x.shape[-1])
            half = Dh // 2
            inv_freq = 1.0 / 10000.0 ** (jnp.arange(half, dtype=jnp.float32) / half)
            ang = jnp.arange(S, dtype=jnp.float32)[:, None] * inv_freq[None, :]
            cos, sin = (jnp.cos(ang), jnp.sin(ang))
            x1, x2 = (x[..., :half], x[..., half:])
            return jnp.concatenate([x1 * cos - x2 * sin, x1 * sin + x2 * cos], axis=-1).astype(x.dtype)
        key = jax.random.key(seed)
        ks = jax.random.split(key, 5)
        D = 256
        B, S = (2, 512)
        w = 0.02
        return {'x': jax.random.normal(ks[0], (B, S, D), dtype=jnp.float32), 'Wq': jax.random.normal(ks[1], (D, D), dtype=jnp.float32) * w, 'bq': jnp.zeros((D,), dtype=jnp.float32), 'Wk': jax.random.normal(ks[2], (D, D), dtype=jnp.float32) * w, 'bk': jnp.zeros((D,), dtype=jnp.float32), 'Wv': jax.random.normal(ks[3], (D, D), dtype=jnp.float32) * w, 'bv': jnp.zeros((D,), dtype=jnp.float32), 'Wo': jax.random.normal(ks[4], (D, D), dtype=jnp.float32) * w, 'bo': jnp.zeros((D,), dtype=jnp.float32)}
    _L0_attn_in = _L0_attn_setup()

    def _L0_ffn_setup():
        import jax, jax.numpy as jnp
        import numpy as np
        DM, NE, ES, ESZ = (256, 16, 4, 64)
        BATCH, SEQ = (8, 512)
        key = jax.random.key(seed)
        k = jax.random.split(key, 5)
        scale = 0.02
        return {'x': jax.random.normal(k[0], (BATCH, SEQ, DM), dtype=jnp.float32), 'controller': jax.random.normal(k[1], (DM, NE, ES), dtype=jnp.float32) * scale, 'f1': jax.random.normal(k[2], (DM, NE, ES, ESZ), dtype=jnp.float32) * scale, 'f2': jax.random.normal(k[3], (NE, ES, ESZ, DM), dtype=jnp.float32) * scale, 'bias': jax.random.normal(k[4], (NE, ES, ESZ), dtype=jnp.float32) * scale}
    _L0_ffn_in = _L0_ffn_setup()

    def _L1_attn_setup():
        import jax, jax.numpy as jnp
        import numpy as np
        B, N, C = (4, 1024, 256)
        H = 16
        D = C // H
        EPS = 1e-06

        def _feature_map(x):
            return jax.nn.elu(x) + 1.0
        key = jax.random.key(seed)
        k1, k2, k3, k4 = jax.random.split(key, 4)
        x = jax.random.normal(k1, (B, N, C), dtype=jnp.float32)
        Wqkv = jax.random.normal(k2, (3 * C, C), dtype=jnp.float32) * 0.02
        Wproj = jax.random.normal(k3, (C, C), dtype=jnp.float32) * 0.02
        bproj = jax.random.normal(k4, (C,), dtype=jnp.float32) * 0.02
        return {'x': x, 'Wqkv': Wqkv, 'Wproj': Wproj, 'bproj': bproj}
    _L1_attn_in = _L1_attn_setup()

    def _L1_ffn_setup():
        import jax, jax.numpy as jnp
        import numpy as np
        B, T, D, E, H = (4, 512, 256, 4, 8)
        EPS = 1e-05

        def _uniform(k, shape, bound):
            return jax.random.uniform(k, shape, jnp.float32, -bound, bound)

        def _layernorm(x, w, b):
            mu = jnp.mean(x, axis=-1, keepdims=True)
            var = jnp.mean(jnp.square(x - mu), axis=-1, keepdims=True)
            return (x - mu) * jax.lax.rsqrt(var + EPS) * w + b
        key = jax.random.key(seed)
        ks = jax.random.split(key, 12)
        wb = np.sqrt(6.0 / D) / np.sqrt(6.0)
        wb = 1.0 / np.sqrt(D)
        return {'x': jax.random.normal(ks[0], (B, T, D), jnp.float32), 'router_prob': jax.random.uniform(ks[1], (B, T, E), jnp.float32), 'norm_w': jnp.ones((D,), jnp.float32), 'norm_b': jnp.zeros((D,), jnp.float32), 'q_w': _uniform(ks[2], (D, D), wb), 'q_b': _uniform(ks[3], (D,), wb), 'k_w': _uniform(ks[4], (D, D), wb), 'k_b': _uniform(ks[5], (D,), wb), 'v_w': _uniform(ks[6], (D, D), wb), 'v_b': _uniform(ks[7], (D,), wb), 'o_w': _uniform(ks[8], (D, D), wb), 'o_b': _uniform(ks[9], (D,), wb)}
    _L1_ffn_in = _L1_ffn_setup()
    _d = {'L0_attn_x': _L0_attn_in['x'], 'L0_attn_Wq': _L0_attn_in['Wq'], 'L0_attn_bq': _L0_attn_in['bq'], 'L0_attn_Wk': _L0_attn_in['Wk'], 'L0_attn_bk': _L0_attn_in['bk'], 'L0_attn_Wv': _L0_attn_in['Wv'], 'L0_attn_bv': _L0_attn_in['bv'], 'L0_attn_Wo': _L0_attn_in['Wo'], 'L0_attn_bo': _L0_attn_in['bo'], 'L0_ffn_controller': _L0_ffn_in['controller'], 'L0_ffn_f1': _L0_ffn_in['f1'], 'L0_ffn_f2': _L0_ffn_in['f2'], 'L0_ffn_bias': _L0_ffn_in['bias'], 'L1_attn_Wqkv': _L1_attn_in['Wqkv'], 'L1_attn_Wproj': _L1_attn_in['Wproj'], 'L1_attn_bproj': _L1_attn_in['bproj'], 'L1_ffn_router_prob': _L1_ffn_in['router_prob'], 'L1_ffn_norm_w': _L1_ffn_in['norm_w'], 'L1_ffn_norm_b': _L1_ffn_in['norm_b'], 'L1_ffn_q_w': _L1_ffn_in['q_w'], 'L1_ffn_q_b': _L1_ffn_in['q_b'], 'L1_ffn_k_w': _L1_ffn_in['k_w'], 'L1_ffn_k_b': _L1_ffn_in['k_b'], 'L1_ffn_v_w': _L1_ffn_in['v_w'], 'L1_ffn_v_b': _L1_ffn_in['v_b'], 'L1_ffn_o_w': _L1_ffn_in['o_w'], 'L1_ffn_o_b': _L1_ffn_in['o_b']}
    _x0 = _d['L0_attn_x']
    _d['L0_attn_x'] = jax.random.normal(jax.random.fold_in(jax.random.key(seed), 1), (8, 1024, 256), dtype=_x0.dtype)
    del _x0
    return _d

def reference(L0_attn_x, L0_attn_Wq, L0_attn_bq, L0_attn_Wk, L0_attn_bk, L0_attn_Wv, L0_attn_bv, L0_attn_Wo, L0_attn_bo, L0_ffn_controller, L0_ffn_f1, L0_ffn_f2, L0_ffn_bias, L1_attn_Wqkv, L1_attn_Wproj, L1_attn_bproj, L1_ffn_router_prob, L1_ffn_norm_w, L1_ffn_norm_b, L1_ffn_q_w, L1_ffn_q_b, L1_ffn_k_w, L1_ffn_k_b, L1_ffn_v_w, L1_ffn_v_b, L1_ffn_o_w, L1_ffn_o_b):

    def _L0_attn_ref(x, Wq, bq, Wk, bk, Wv, bv, Wo, bo):
        import jax, jax.numpy as jnp
        import numpy as np
        NUM_HEADS = 16
        WINDOW = 128

        def apply_rope(x):
            S, Dh = (x.shape[-2], x.shape[-1])
            half = Dh // 2
            inv_freq = 1.0 / 10000.0 ** (jnp.arange(half, dtype=jnp.float32) / half)
            ang = jnp.arange(S, dtype=jnp.float32)[:, None] * inv_freq[None, :]
            cos, sin = (jnp.cos(ang), jnp.sin(ang))
            x1, x2 = (x[..., :half], x[..., half:])
            return jnp.concatenate([x1 * cos - x2 * sin, x1 * sin + x2 * cos], axis=-1).astype(x.dtype)
        B, S, D = x.shape
        H = NUM_HEADS
        Dh = D // H

        def proj(W, b):
            y = jnp.einsum('bsd,ed->bse', x, W) + b
            return y.reshape(B, S, H, Dh).transpose(0, 2, 1, 3)
        q = apply_rope(proj(Wq, bq)) * Dh ** (-0.5)
        k = apply_rope(proj(Wk, bk))
        v = proj(Wv, bv)
        scores = jnp.einsum('bhqd,bhkd->bhqk', q, k)
        idx = jnp.arange(S)
        rel = idx[None, :] - idx[:, None]
        blocked = (rel > 0) | (rel < -WINDOW)
        scores = jnp.where(blocked[None, None], -jnp.inf, scores)
        probs = jax.nn.softmax(scores, axis=-1)
        out = jnp.einsum('bhqk,bhkd->bhqd', probs, v)
        out = out.transpose(0, 2, 1, 3).reshape(B, S, D)
        return jnp.einsum('bsd,ed->bse', out, Wo) + bo

    def _L0_ffn_ref(x, controller, f1, f2, bias):
        import jax, jax.numpy as jnp
        import numpy as np
        DM, NE, ES, ESZ = (256, 16, 4, 64)
        BATCH, SEQ = (8, 512)
        ne = controller.shape[1]
        d = x.shape[-1]
        grouped = x.reshape(x.shape[:-2] + (-1, ne, d))
        logits = jnp.einsum('...btd,des->...btes', grouped, controller)
        tie = jnp.linspace(0.0, 1e-06, ne, dtype=logits.dtype).reshape(ne, 1, 1)
        logits = logits + tie
        perm = (logits == jnp.max(logits, axis=-3, keepdims=True)).astype(x.dtype)
        sel = jnp.einsum('...btd,...btes->...besd', grouped, perm)
        inner = jax.nn.relu(jnp.einsum('...besd,desf->...besf', sel, f1) + bias)
        inter = jnp.einsum('...besf,esfd->...besd', inner, f2)
        out = jnp.einsum('...besd,...btes->...btd', inter, perm)
        return out.reshape(x.shape)

    def _L1_attn_ref(x, Wqkv, Wproj, bproj):
        import jax, jax.numpy as jnp
        import numpy as np
        B, N, C = (4, 1024, 256)
        H = 16
        D = C // H
        EPS = 1e-06

        def _feature_map(x):
            return jax.nn.elu(x) + 1.0
        b, n, c = x.shape
        qkv = jnp.einsum('bnc,fc->bnf', x, Wqkv).reshape(b, n, 3, H, D)
        qkv = jnp.transpose(qkv, (2, 0, 3, 1, 4))
        q, k, v = (qkv[0], qkv[1], qkv[2])
        q = _feature_map(q)
        k = _feature_map(k)
        kv = jnp.einsum('bhnd,bhne->bhde', k, v)
        k_sum = k.sum(axis=2)
        z = 1.0 / (jnp.einsum('bhnd,bhd->bhn', q, k_sum)[..., None] + EPS)
        out = jnp.einsum('bhnd,bhde->bhne', q, kv) * z
        out = jnp.transpose(out, (0, 2, 1, 3)).reshape(b, n, c)
        out = jnp.einsum('bnc,oc->bno', out, Wproj) + bproj
        return out

    def _L1_ffn_ref(x, router_prob, norm_w, norm_b, q_w, q_b, k_w, k_b, v_w, v_b, o_w, o_b):
        import jax, jax.numpy as jnp
        import numpy as np
        B, T, D, E, H = (4, 512, 256, 4, 8)
        EPS = 1e-05

        def _uniform(k, shape, bound):
            return jax.random.uniform(k, shape, jnp.float32, -bound, bound)

        def _layernorm(x, w, b):
            mu = jnp.mean(x, axis=-1, keepdims=True)
            var = jnp.mean(jnp.square(x - mu), axis=-1, keepdims=True)
            return (x - mu) * jax.lax.rsqrt(var + EPS) * w + b
        e_cnt = router_prob.shape[2]
        b, t, d = x.shape
        n = t // e_cnt
        h = H
        scale = d ** (-0.5)
        qs, ks_, vs = ([], [], [])
        for e in range(e_cnt):
            xe = x[:, e * n:(e + 1) * n, :]
            xn = _layernorm(xe, norm_w, norm_b)
            m = d // 2 ** e
            xm = xn[..., :m]
            qs.append(jnp.einsum('bnm,dm->bnd', xm, q_w[:, :m]) + q_b)
            ks_.append(jnp.einsum('bnm,dm->bnd', xm, k_w[:, :m]) + k_b)
            vs.append(jnp.einsum('bnm,dm->bnd', xm, v_w[:, :m]) + v_b)
        q = jnp.concatenate(qs, axis=1)
        k = jnp.concatenate(ks_, axis=1)
        v = jnp.concatenate(vs, axis=1)
        dh = d // h
        q = q.reshape(b, t, h, dh).transpose(0, 2, 1, 3)
        k = k.reshape(b, t, h, dh).transpose(0, 2, 1, 3)
        v = v.reshape(b, t, h, dh).transpose(0, 2, 1, 3)
        attn = jnp.einsum('bhqd,bhkd->bhqk', q, k) * scale
        attn = jax.nn.softmax(attn, axis=-1)
        attn_out = jnp.einsum('bhqk,bhkd->bhqd', attn, v)
        attn_out = attn_out.transpose(0, 2, 1, 3).reshape(b, t, d)
        outs = []
        for e in range(e_cnt):
            sl = slice(e * n, (e + 1) * n)
            m = d // 2 ** e
            xm = attn_out[:, sl, :m]
            out = jnp.einsum('bnm,om->bno', xm, o_w[:m, :m]) + o_b[:m]
            pad = d - m
            if pad:
                out = jnp.pad(out, ((0, 0), (0, 0), (0, pad)))
            outs.append(out + x[:, sl, :])
        return jnp.concatenate(outs, axis=1)
    x = L0_attn_x
    x = _layernorm(x + _L0_attn_ref(x, L0_attn_Wq, L0_attn_bq, L0_attn_Wk, L0_attn_bk, L0_attn_Wv, L0_attn_bv, L0_attn_Wo, L0_attn_bo), axis=-1)
    x = _layernorm(x + _L0_ffn_ref(x, L0_ffn_controller, L0_ffn_f1, L0_ffn_f2, L0_ffn_bias), axis=-1)
    x = _layernorm(x + _L1_attn_ref(x, L1_attn_Wqkv, L1_attn_Wproj, L1_attn_bproj), axis=-1)
    x = _layernorm(x + _L1_ffn_ref(x, L1_ffn_router_prob, L1_ffn_norm_w, L1_ffn_norm_b, L1_ffn_q_w, L1_ffn_q_b, L1_ffn_k_w, L1_ffn_k_b, L1_ffn_v_w, L1_ffn_v_b, L1_ffn_o_w, L1_ffn_o_b), axis=-1)
    return x

_drawn_inputs = setup_inputs


def setup_inputs(seed=0):
    import zlib

    import numpy as np

    out = dict(_drawn_inputs(seed))
    spreads = {'L0_attn_bq': (0.0, 0.8),
     'L0_attn_bk': (0.0, 0.8),
     'L0_attn_bv': (0.0, 0.1),
     'L0_attn_bo': (0.0, 0.1),
     'L1_ffn_norm_w': (1.0, 0.6),
     'L1_ffn_norm_b': (0.0, 0.8)}
    factors = {'L0_attn_Wq': 8.0,
     'L0_attn_Wk': 8.0,
     'L0_attn_Wv': 4.611,
     'L0_ffn_bias': 8.0,
     'L1_attn_Wqkv': 4.961,
     'L1_attn_Wproj': 5.053,
     'L1_attn_bproj': 3.096,
     'L1_ffn_q_w': 8.0,
     'L1_ffn_q_b': 8.0,
     'L1_ffn_k_w': 8.0,
     'L1_ffn_k_b': 64.0,
     'L1_ffn_v_w': 6.599,
     'L1_ffn_v_b': 8.0,
     'L1_ffn_o_w': 6.204,
     'L1_ffn_o_b': 15.791}
    for name, (base, spread) in spreads.items():
        noise = np.random.default_rng([zlib.crc32(name.encode()), seed]).standard_normal(out[name].shape)
        drawn = base * np.exp(spread * noise) if base else spread * noise
        out[name] = jnp.asarray(drawn.astype(out[name].dtype))
    for name, factor in factors.items():
        out[name] = (out[name] * factor).astype(out[name].dtype)
    return out
```

```python
from contextlib import ExitStack

import concourse.bass as bass
from concourse import mybir

f32 = mybir.dt.float32
f32r = mybir.dt.float32r
bf16 = mybir.dt.bfloat16
ACT = mybir.ActivationFunctionType
ALU = mybir.AluOpType
AX = mybir.AxisListType.X

P = 128
NSEQ, T, D = 8, 1024, 256
NT = T // P
LN_EPS = 1e-5


def allocators(nc, ctx, layer):
    def sb(name, shape, dtype=f32):
        return ctx.enter_context(nc.sbuf_tensor(f"{layer}_{name}", shape, dtype))

    def ps(name, shape, dtype=f32):
        return ctx.enter_context(nc.psum_tensor(f"{layer}_{name}", shape, dtype))

    def sem(name):
        return ctx.enter_context(nc.semaphore(f"{layer}_{name}"))

    return sb, ps, sem


def tokens(dram, b):
    return dram[bass.ds(b, 1), :, :].rearrange("o (t p) d -> p (o t) d", p=P)


def wait_alone(eng, sem, value):
    eng.wait_ge(sem, value)
    eng.nop(nofuse=True)


def words(ap):
    return ap.bitcast(f32)


def on_all_partitions(row, n):
    return row[0:n].partition_broadcast(P)


def each_tile(v, n=NT):
    return v[:, :].unsqueeze(1).broadcast_to([P, n, D])


class Ring:

    def __init__(self, plan, n, emptied=None):
        self.at = {key: i for i, key in enumerate(plan)}
        self.plan, self.n, self.emptied = plan, n, emptied
        assert len(self.at) == len(plan)

    def slot(self, key):
        return self.at[key] % self.n

    def count(self, b, key):
        return b * len(self.plan) + self.at[key] + 1

    def before(self, key):
        i = self.at[key] - self.n
        return self.plan[i] if i >= 0 else None

    def wait_free(self, pe, b, key):
        old = self.before(key)
        if old is not None:
            for sem, per_sequence, position in self.emptied(old):
                pe.wait_ge(sem, b * per_sequence + position)


class LayerNorm:

    def __init__(self, sb, sem, name, setup, uses, tiles=NT):
        self.setup, self.uses, self.tiles = setup, uses, tiles
        self.stats = sb(f"{name}_stats", [P, tiles, 6])
        self.mv = sb(f"{name}_mv", [P, tiles, 2])
        self.rstd = sb(f"{name}_rstd", [P, tiles])
        self.half = sb(f"{name}_half", [P, tiles])
        self.summed = sem(f"{name}_summed")
        self.aggregated = sem(f"{name}_aggregated")
        self.var_ready = sem(f"{name}_var_ready")
        self.rstd_ready = sem(f"{name}_rstd_ready")
        self.normed = sem(f"{name}_normed")

    def count(self, b, use):
        return b * self.uses + use + 1

    def statistics(self, dve, x, b, use):
        n = self.count(b, use)
        for t in range(self.tiles):
            dve.bn_stats(self.stats[:, t, :], x[:, t, :]).then_inc(self.summed, 1)
        wait_alone(dve, self.summed, n * self.tiles)
        for t in range(self.tiles):
            dve.bn_aggr(self.mv[:, t, :], self.stats[:, t, :]).then_inc(self.aggregated, 1)
        dve.wait_ge(self.aggregated, n * self.tiles)
        dve.tensor_scalar(self.mv[:, :, 1], self.mv[:, :, 1], LN_EPS, None, ALU.add).then_inc(self.var_ready, 1)

    def reciprocal_root(self, pool, b, use):
        pool.wait_ge(self.var_ready, self.count(b, use))
        pool.tensor_tensor(self.rstd[:, :], self.mv[:, :, 1], self.half[:, :], ALU.pow).then_inc(self.rstd_ready, 1)

    def normalise(self, dve, out, x, b, use):
        dve.wait_ge(self.rstd_ready, self.count(b, use))
        for t in range(self.tiles):
            dve.tensor_scalar(out[:, t, :], x[:, t, :], self.mv[:, t, 0:1], self.rstd[:, t:t + 1],
                              ALU.subtract, ALU.mult).then_inc(self.normed, 1)

    def done(self, b, use):
        return self.count(b, use) * self.tiles



class Signal:

    def __init__(self, sem, per, step=1):
        self.sem, self.per, self.step = sem, per, step

    def start(self, eng):
        eng.sem_inc(self.sem, 2 * self.per * self.step)

    def by(self, instruction):
        instruction.then_inc(self.sem, self.step)

    def wait(self, eng, block, n=None):
        eng.wait_ge(self.sem, block * (self.per * self.step) + (2 * self.per + (self.per if n is None else n)) * self.step)


def window_attention_layer(nc, x_in, y_out, wq_in, wk_in, bq_in, bk_in, wvT, bv_in, woT, bo_in, cos_in, sin_in,
                           mask_in, maskT_in, ident_in, ident16_in, scratch):
    H, DH = 16, 16
    BT = 4
    BW = BT * P
    HG = 4
    NHG = H // HG
    HR = DH // 2
    SCALE = float(DH) ** -0.5
    CH = D // P
    SHIFT_ROW = 96

    front_plan = ["xT", "q", "k", "v"]

    def nat(t):
        return [("nat", NHG * t + g) for g in range(NHG)] + [("maxT", t)]

    def tr(t):
        return [("tr", NHG * t + g) for g in range(NHG)]

    steps = [nat(0), nat(1), "xT", tr(0), nat(2), [("pv", 0)], tr(1), "q", nat(3), [("back", 0), ("pv", 1)], tr(2), "k",
             [("back", 1), ("pv", 2)], tr(3), "v", [("back", 2), ("pv", 3), ("back", 3), ("aoT", 0), ("proj", 0)]]
    att_plan = [key for s in steps if not isinstance(s, str) for key in s if key[0] != "pv"]

    with ExitStack() as ctx:
        sb, ps, sem = allocators(nc, ctx, "l0a")
        consts = sem("consts"); setup = sem("setup")
        ident = sb("ident", [P, P]); ident16 = sb("ident16", [P, P], bf16)
        mask = sb("mask", [P, 2, P], bf16)
        maskT = sb("maskT", [P, 2, P], bf16)
        wq = sb("wq", [P, CH, D]); wk = sb("wk", [P, CH, D]); wv = sb("wv", [P, CH, D]); wo = sb("wo", [P, CH, D])
        bq = sb("bq", [P, 2]); bk = sb("bk", [P, 2]); bv = sb("bv", [P, D]); bo = sb("bo", [P, D])
        cos = sb("cos", [P, T]); sin = sb("sin", [P, T])
        x = sb("x", [P, 2, BT, D])
        xT = sb("xT", [P, CH, BW])
        turned = sb("turned", [P, 4, BW])
        rot = turned[:, 0::2, :]
        hi = sb("hi", [P, 2, BW], f32r); lo = sb("lo", [P, 2, BW], f32r)
        Qs = sb("Qs", [P, 2, H, BW], f32r)
        Ks = sb("Ks", [P, 2, H // 2, P + BW], f32r)
        V = sb("V", [P, 2, BT + 1, H, 2 * DH])
        probs = sb("probs", [P, H, 2, P])
        oT = sb("oT", [P, 4, P])
        recip = sb("recip", [P, BT, H])
        ao = sb("ao", [P, BT, D]); aoT = sb("aoT", [P, CH, BW])
        rowmax = sb("rowmax", [P, BT, H])
        maxT = sb("maxT", [H, 2, P], f32r)
        ln = LayerNorm(sb, sem, "ln", setup, 1, BT)
        front_slot = ps("front", [P, 1024])
        slots = [ps(f"slot{i}", [P, 1024]) for i in range(2)]
        O = [ps(f"O{i}", [P, 4, P]) for i in range(2)]


        def signal(name, per, step=1):
            return Signal(sem(name), per, step)

        x_loaded = signal("x_loaded", 1, 16); stored = signal("stored", 1, 16)
        front = signal("front", 4); filled = signal("filled", len(att_plan))
        xT_ready = signal("xT_ready", 1); biased = signal("biased", 1)
        turned_ready = signal("turned_ready", 8); rot_ready = signal("rot_ready", 4)
        hi_ready = signal("hi_ready", 2); lo_ready = signal("lo_ready", 2)
        v_ready = signal("v_ready", 1); v_carried = signal("v_carried", 1)
        bounced = {w: signal(f"bounced_{w}", 4, 16) for w in "qk"}
        stacked = {w: signal(f"stacked_{w}", 6, 16) for w in "qk"}
        max_ready = signal("max_ready", BT * NHG); maxT_ready = signal("maxT_ready", BT)
        placed = [signal(f"placed{t}", 1, 16) for t in range(BT)]
        exp_ready = signal("exp_ready", BT * NHG); pv_done = signal("pv_done", BT)
        oT_ready = signal("oT_ready", BT); recip_ready = signal("recip_ready", BT); ao_ready = signal("ao_ready", BT)
        aoT_ready = signal("aoT_ready", 1); summed = signal("summed", 1)

        at = {key: i for i, key in enumerate(att_plan)}

        def slot(key):
            return slots[at[key] % 2]

        assert len(att_plan) % 2 == 0

        def arrived(eng, B, key):
            filled.wait(eng, B, at[key] + 1)
            return slot(key)

        def use(pe, B, key):
            i = at[key] - 2
            if i < 0:
                i, B = i + len(att_plan), B - 1
            kind, n = att_plan[i]
            read, count = {"nat": (max_ready, n + 1), "maxT": (maxT_ready, n + 1), "tr": (exp_ready, n + 1),
                           "back": (ao_ready, n + 1), "aoT": (aoT_ready, 1), "proj": (summed, 1)}[kind]
            read.wait(pe, B, count)
            return slot(key)

        def run(front_piece, attention_piece, order=steps):
            def body(b, last):
                for n in range(2):
                    B = 2 * b + n
                    for step in steps:
                        if isinstance(step, str):
                            if not (last and n == 1):
                                front_piece(step, B + 1, b + n, 1 - n)
                        else:
                            for kind, i in step:
                                attention_piece(kind, i, B, b, n)
            for piece in front_plan:
                front_piece(piece, 0, 0, 0)
            return body

        def loop(eng, body):
            with eng.Fori(0, NSEQ - 1) as b:
                body(b, False)
            body(NSEQ - 1, True)

        NCONST = 14
        NSETUP = 5
        block = ctx.enter_context(nc.Block())

        @block.sync
        def _(sp):
            for dst, src in ((ident, ident_in), (ident16, ident16_in), (cos, cos_in), (sin, sin_in), (bq, bq_in), (bk, bk_in)):
                sp.dma_start(dst[:, :], src).then_inc(consts, 16)
            for dst, src in ((mask, mask_in), (maskT, maskT_in)):
                sp.dma_start(dst[:, :, :], src.rearrange("p (a n) -> p a n", a=2)).then_inc(consts, 16)
            for dst, src in ((wq, wq_in), (wk, wk_in), (wv, wvT), (wo, woT)):
                sp.dma_start(dst[:, :, :], src.rearrange("(c p) n -> p c n", p=P)).then_inc(consts, 16)
            for dst, src in ((bv, bv_in), (bo, bo_in)):
                sp.dma_start(dst[:, :], on_all_partitions(src, D)).then_inc(consts, 16)
            for s in (x_loaded, stored, *bounced.values(), *stacked.values(), *placed):
                s.start(sp)
            sp.wait_ge(setup, NSETUP)

            def front_piece(piece, B, b, n):
                tok = BW * n
                if piece == "xT":
                    stored.wait(sp, B - 2)
                    sp.wait_ge(setup, 1)
                    x_loaded.by(sp.dma_start(x[:, n, :, :], tokens(x_in, b)[:, BT * n:BT * n + BT, :]))
                if piece in ("q", "k"):
                    w = piece
                    i = "qk".index(w)
                    lo_ready.wait(sp, B, i + 1)
                    for part, source in enumerate((hi, lo)):
                        for r in range(2):
                            rows = scratch[i, part, :, HR * r:HR * r + HR, tok:tok + BW]
                            bounced[w].by(sp.dma_start(rows, words(source[:, r, :])))
                    bounced[w].wait(sp, B)
                    pv_done.wait(sp, B - 2)
                    for parity in range(2):
                        for term, part in enumerate((0, 1, 0) if w == "q" else (0, 0, 1)):
                            first = 3 * DH * parity + DH * term
                            if w == "q":
                                src = scratch[i, part, parity::2, :, tok:tok + BW]
                                dst = Qs[first:first + DH, n, parity::2, :]
                            else:
                                skip = 0 if n else P
                                src = scratch[i, part, parity::2, :, tok - P + skip:tok + BW]
                                dst = Ks[first:first + DH, n, :, skip:]
                            stacked[w].by(sp.dma_start(words(dst), src.rearrange("h d t -> d h t")))

            def attention_piece(kind, i, B, b, n):
                if kind == "maxT":
                    maxT_ready.wait(sp, B, i + 1)
                    placed[i].by(sp.dma_start(words(Qs[SHIFT_ROW:SHIFT_ROW + 1, n, :, P * i:P * i + P]),
                                              words(maxT[:, i % 2, :])))
                if kind == "proj":
                    wait_alone(sp, ln.normed, (B + 1) * BT)
                    stored.by(sp.dma_start(tokens(y_out, b)[:, BT * n:BT * n + BT, :], x[:, n, :, :]))

            loop(sp, run(front_piece, attention_piece))
            stored.wait(sp, 2 * NSEQ - 1)

        @block.gpsimd
        def _(pool):
            for s in (biased, rot_ready, lo_ready):
                s.start(pool)
            pool.wait_ge(setup, NSETUP)
            pool.wait_ge(consts, 16 * NCONST)

            def front_piece(piece, B, b, n):
                if piece == "xT":
                    front.wait(pool, B, 1)
                    biased.by(pool.tensor_tensor(x[:, n, :, :], x[:, n, :, :], each_tile(bo, BT), ALU.add))
                if piece in ("q", "k"):
                    i = "qk".index(piece)
                    turned_ready.wait(pool, B, 4 * i + 2)
                    rot_ready.by(pool.tensor_tensor(rot[:, 0, :], turned[:, 0, :], turned[:, 1, :], ALU.subtract))
                    turned_ready.wait(pool, B, 4 * i + 4)
                    rot_ready.by(pool.tensor_tensor(rot[:, 1, :], turned[:, 2, :], turned[:, 3, :], ALU.add))
                    hi_ready.wait(pool, B, i + 1)
                    rot_ready.wait(pool, B, 2 * i + 2)
                    other = bounced["k" if i == 0 else "q"]
                    other.wait(pool, B - 1 if i == 0 else B)
                    lo_ready.by(pool.tensor_tensor(lo[:, :, :], rot[:, :, :], hi[:, :, :].bitcast(f32), ALU.subtract))

            def attention_piece(kind, i, B, b, n):
                if kind == "proj":
                    ln.reciprocal_root(pool, B, 0)

            loop(pool, run(front_piece, attention_piece))

        def back_filled(eng, B, t):
            if t < 0:
                B, t = B - 1, t + BT
            filled.wait(eng, B, at[("back", t)] + 1)

        @block.scalar
        def _(act):
            for s in (xT_ready, hi_ready, v_carried, exp_ready, oT_ready, aoT_ready):
                s.start(act)
            act.wait_ge(setup, NSETUP)
            act.wait_ge(consts, 16 * NCONST)

            def front_piece(piece, B, b, n):
                if piece == "xT":
                    front.wait(act, B, 1)
                    xT_ready.by(act.copy(xT[:, :, :], front_slot[:, :].rearrange("p (c n) -> p c n", c=CH)))
                if piece in ("q", "k"):
                    i = "qk".index(piece)
                    rot_ready.wait(act, B, 2 * i + 2)
                    other = bounced["k" if i == 0 else "q"]
                    other.wait(act, B - 1 if i == 0 else B)
                    hi_ready.by(act.copy(hi[:, :, :], rot[:, :, :]))
                if piece == "v":
                    v_ready.wait(act, B - 1)
                    pv_done.wait(act, B - 2)
                    if n:
                        v_carried.by(act.copy(V[:, 1, 0, :, :], V[:, 0, BT, :, :]))
                    else:
                        v_carried.by(act.copy(V[:, 0, 0, :, :], V[:, 1, BT, :, :]))

            def attention_piece(kind, i, B, b, n):
                if kind == "tr":
                    t, g = i // NHG, i % NHG
                    s = arrived(act, B, (kind, i))[:, :].rearrange("p (h a q) -> p h a q", h=HG, a=2)
                    pv_done.wait(act, B if t else B - 1, t if t else BT)
                    first = 0 if n or t else 1
                    exp_ready.by(act.activation(probs[:, HG * g:HG * g + HG, first:2, :], s[:, :, first:2, :],
                                                ACT.Exp, scale=SCALE))
                if kind == "pv":
                    pv_done.wait(act, B, i + 1)
                    back_filled(act, B, i - 1)
                    oT_ready.by(act.copy(oT[:, :, :], O[i % 2][:, :, :]))
                if kind == "aoT":
                    s = arrived(act, B, (kind, i))
                    aoT_ready.by(act.copy(aoT[:, :, :], s[:, :].rearrange("p (c n) -> p c n", c=CH)))

            loop(act, run(front_piece, attention_piece))

        @block.vector
        def _(dve):
            dve.memset(Qs[:, :, :, :].bitcast(f32), 0.0).then_inc(setup, 1)
            dve.memset(Ks[SHIFT_ROW:P, :, :, :].bitcast(f32), -1.0).then_inc(setup, 1)
            dve.memset(V[:, :, :, :, :], 1.0).then_inc(setup, 1)
            dve.memset(ln.half[:, :], -0.5).then_inc(setup, 1)
            dve.memset(maxT[:, :, :].bitcast(f32), 0.0).then_inc(setup, 1)
            for s in (turned_ready, v_ready, max_ready, maxT_ready, recip_ready, ao_ready, summed):
                s.start(dve)
            dve.wait_ge(consts, 16 * NCONST)
            dve.wait_ge(setup, NSETUP)

            def front_piece(piece, B, b, n):
                cols = slice(BW * n, BW * n + BW)
                if piece in ("q", "k"):
                    i = "qk".index(piece)
                    bias = (bq, bk)[i]
                    front.wait(dve, B, 2 + i)
                    hi_ready.wait(dve, B if i else B - 1, 1 if i else 2)
                    lo_ready.wait(dve, B if i else B - 1, 1 if i else 2)
                    for j, (r, table) in enumerate(((0, cos), (1, sin), (0, sin), (1, cos))):
                        turned_ready.by(dve.scalar_tensor_tensor(turned[:, j, :], front_slot[:, BW * r:BW * r + BW],
                                                                 bias[:, r:r + 1], table[:, cols], ALU.add, ALU.mult))
                if piece == "v":
                    front.wait(dve, B, 4)
                    pv_done.wait(dve, B - 2)
                    v_carried.wait(dve, B - 1)
                    for t in range(BT):
                        last = dve.tensor_tensor(V[:, n, t + 1, :, 0:DH],
                                                 front_slot[:, D * t:D * t + D].rearrange("p (h d) -> p h d", h=H),
                                                 bv[:, :].rearrange("p (h d) -> p h d", h=H), ALU.add)
                    v_ready.by(last)

            def attention_piece(kind, i, B, b, n):
                if kind == "nat":
                    t, g = i // NHG, i % NHG
                    s = arrived(dve, B, (kind, i))[:, :].rearrange("p (h k) -> p h k", h=HG)
                    first = 0 if n or t else P
                    max_ready.by(dve.reduce_max(rowmax[:, t, HG * g:HG * g + HG], s[:, :, first:2 * P], AX))
                if kind == "maxT":
                    s = arrived(dve, B, (kind, i))
                    placed[(i - 2) % BT].wait(dve, B if i >= 2 else B - 1)
                    maxT_ready.by(dve.tensor_copy(maxT[:, i % 2, :], s[0:H, 0:P]))
                if kind == "back":
                    s = arrived(dve, B, (kind, i))[:, 0:512].rearrange("p (h d) -> p h d", h=H)
                    recip_ready.by(dve.reciprocal(recip[:, i, :], s[:, :, DH]))
                    recip_ready.wait(dve, B, i + 1)
                    ao_ready.by(dve.tensor_tensor(ao[:, i, :].rearrange("p (h d) -> p h d", h=H), s[:, :, 0:DH],
                                                  recip[:, i, :].unsqueeze(2).broadcast_to([P, H, DH]), ALU.mult))
                if kind == "proj":
                    s = arrived(dve, B, (kind, i))
                    biased.wait(dve, B)
                    summed.by(dve.tensor_tensor(x[:, n, :, :], s[:, :].rearrange("p (t n) -> p t n", t=BT), x[:, n, :, :], ALU.add))
                    summed.wait(dve, B)
                    ln.statistics(dve, x[:, n, :, :], B, 0)
                    ln.normalise(dve, x[:, n, :, :], x[:, n, :, :], B, 0)

            loop(dve, run(front_piece, attention_piece))

        @block.tensor
        def _(pe):
            mm = nc.tensor.matmul
            for s in (front, filled, pv_done):
                s.start(pe)
            pe.wait_ge(setup, NSETUP)
            pe.wait_ge(consts, 16 * NCONST)

            def front_piece(piece, B, b, n):
                if piece == "xT":
                    x_loaded.wait(pe, B)
                    v_ready.wait(pe, B - 1)
                    for c in range(CH):
                        for t in range(BT):
                            last = nc.tensor.transpose(front_slot[:, BW * c + P * t:BW * c + P * t + P],
                                                       x[:, n, t, P * c:P * c + P], ident[:, :])
                if piece in ("q", "k"):
                    w = wq if piece == "q" else wk
                    if piece == "q":
                        xT_ready.wait(pe, B)
                    else:
                        turned_ready.wait(pe, B, 4)
                    for r in range(2):
                        for c in range(CH):
                            last = mm(front_slot[:, BW * r:BW * r + BW], w[:, c, P * r:P * r + P], xT[:, c, :],
                                      start=c == 0, stop=c == CH - 1)
                if piece == "v":
                    turned_ready.wait(pe, B, 8)
                    for t in range(BT):
                        for c in range(CH):
                            last = mm(front_slot[:, D * t:D * t + D], xT[:, c, P * t:P * t + P], wv[:, c, :],
                                      start=c == 0, stop=c == CH - 1)
                front.by(last)

            def attention_piece(kind, i, B, b, n):
                t, g = i // NHG, i % NHG
                if kind == "nat":
                    if i == 0:
                        stacked["q"].wait(pe, B)
                        stacked["k"].wait(pe, B)
                    s = use(pe, B, (kind, i))
                    first = 0 if n or t else 1
                    for k in range(HG // 2):
                        o = s[:, 512 * k:512 * k + 512].rearrange("p (h a n) -> p h a n", h=2, a=2)[:, :, first:2, :]
                        mm(o, ident16[:, :], mask[:, first:2, :].unsqueeze(1).broadcast_to([P, 2, 2 - first, P]),
                           start=True, stop=False, skip_group_check=True)
                        for m in range(2):
                            h = HG * g + 2 * k + m
                            last = mm(o[:, m, :, :].rearrange("p a n -> p (a n)"), Qs[0:96, n, h, P * t:P * t + P],
                                      Ks[0:96, n, h // 2, P * (t + first):P * (t + 2)], start=False, stop=True,
                                      skip_group_check=True)
                    filled.by(last)
                if kind == "maxT":
                    s = use(pe, B, (kind, i))
                    max_ready.wait(pe, B, NHG * i + NHG)
                    filled.by(nc.tensor.transpose(s[0:H, 0:P], rowmax[:, i, :], ident[:, :]))
                if kind == "tr":
                    if g == 0:
                        placed[t].wait(pe, B)
                    s = use(pe, B, (kind, i))
                    first = 0 if n or t else 1
                    for k in range(HG // 2):
                        o = s[:, 512 * k:512 * k + 512].rearrange("p (h a n) -> p h a n", h=2, a=2)
                        mm(o[:, :, first:2, :], ident16[:, :],
                           maskT[:, first:2, :].unsqueeze(1).broadcast_to([P, 2, 2 - first, P]),
                           start=True, stop=False, skip_group_check=True)
                        for m in range(2):
                            h = HG * g + 2 * k + m
                            for a in range(first, 2):
                                last = mm(o[:, m, a, :], Ks[:, n, h // 2, P * (t + a):P * (t + a + 1)],
                                          Qs[:, n, h, P * t:P * t + P], start=False, stop=True, skip_group_check=True)
                    filled.by(last)
                if kind == "pv":
                    exp_ready.wait(pe, B, NHG * i + NHG)
                    if i == 0:
                        v_ready.wait(pe, B)
                        v_carried.wait(pe, B)
                    oT_ready.wait(pe, B if i >= 2 else B - 1, (i - 2) % BT + 1)
                    first = 0 if n or i else 1
                    for gg in range(NHG):
                        for a in range(first, 2):
                            for j in range(HG):
                                h = HG * gg + j
                                last = mm(O[i % 2][32 * j:32 * j + 32, gg, :], V[:, n, i + a, h, :], probs[:, h, a, :],
                                          start=a == first, stop=a == 1, tile_position=(0, 32 * j))
                    pv_done.by(last)
                if kind == "back":
                    oT_ready.wait(pe, B, i + 1)
                    s = use(pe, B, (kind, i))
                    for gg in range(NHG):
                        last = nc.tensor.transpose(s[:, P * gg:P * gg + P], oT[:, gg, :], ident[:, :])
                    filled.by(last)
                if kind == "aoT":
                    ao_ready.wait(pe, B)
                    s = use(pe, B, (kind, i))
                    for c in range(CH):
                        for tt in range(BT):
                            last = nc.tensor.transpose(s[:, BW * c + P * tt:BW * c + P * tt + P], ao[:, tt, P * c:P * c + P],
                                                       ident[:, :])
                    filled.by(last)
                if kind == "proj":
                    aoT_ready.wait(pe, B)
                    s = use(pe, B, (kind, i))
                    for tt in range(BT):
                        for c in range(CH):
                            last = mm(s[:, D * tt:D * tt + D], aoT[:, c, P * tt:P * tt + P], wo[:, c, :],
                                      start=c == 0, stop=c == CH - 1)
                    filled.by(last)

            loop(pe, run(front_piece, attention_piece))


def token_choice_layer(nc, x_in, y_out, controller, f1_in, f2_in, f1_bias, tie_in, ident_in, scratch):
    G = 16
    E, F = 64, 64
    EH = E // 2
    TT = 2 * NT
    NG = TT * P // G
    J = P // EH
    NQ = NG // J
    CH = D // P
    TP = TT // 2
    PAIRS = EH // 2
    HB = 8
    IN = PAIRS // 2
    NC = TT // 4

    plan = [("xT", n) for n in range(2 * CH)] + [("logits", 0)]

    def selection(half):
        out = [("pT", half * TP)]
        for tp in range(TP):
            if tp + 1 < TP:
                out.append(("pT", half * TP + tp + 1))
            out.append(("sel", half * TP + tp))
        return out

    def experts(half):
        h, o = [("h", 2 * half + n) for n in range(2)], [("inter", IN * half + n) for n in range(IN)]
        return [h[0], o[0], o[1], h[1]] + o[2:]

    def combination(half):
        return [("out", NC * half + n) for n in range(NC)]

    plan += selection(0) + experts(0) + selection(1) + combination(0) + experts(1) + combination(1)

    with ExitStack() as ctx:
        sb, ps, sem = allocators(nc, ctx, "l0f")
        consts = sem("consts"); setup = sem("setup")
        ident = sb("ident", [P, P])
        ctrl = sb("ctrl", [P, CH, E])
        f1 = sb("f1", [P, CH, E, F])
        f2 = sb("f2", [P, PAIRS, D])
        b1 = sb("b1", [P, E // 2])
        tie = sb("tie", [P, G])
        sel = sb("sel", [P, CH, EH, NG])
        wide = sb("wide", [P, 2 * TT, D])
        x, inter2, y = wide[:, 0:TT, :], wide, wide[:, TT:2 * TT, :]
        hi = sb("hi", [P, TT, D], f32r); lo = sb("lo", [P, TT, D], f32r)
        turned = sb("turned", [P, TT * D])
        xT = turned[:, :].rearrange("p (c t) -> p c t", c=CH)
        total = turned[:, :].rearrange("p (t d) -> p t d", d=D)
        hidden = sb("hidden", [P, 8, 2, NG])
        inter = sb("inter", [P, 2, 4, D])
        choice = sb("choice", [P, 2, NQ, G])
        spread = sb("spread", [P, 2, NQ, J, G])
        chosen = sb("chosen", [P, 2, 2, 2, P], f32r)
        best = sb("best", [P, 2, NQ])
        ln = LayerNorm(sb, sem, "ln", setup, 1, TT)
        slots = [ps(f"slot{i}", [P, 1024]) for i in range(4)]

        f2_loaded = sem("f2_loaded")
        x_loaded = sem("x_loaded"); x_again = sem("x_again"); stored = sem("stored")
        filled = sem("filled"); xT_ready = sem("xT_ready"); hi_ready = sem("hi_ready"); lo_ready = sem("lo_ready")
        rated = sem("rated"); best_ready = sem("best_ready"); choice_ready = sem("choice_ready"); spread_ready = sem("spread_ready")
        chosen_ready = sem("chosen_ready"); sel_even = sem("sel_even"); sel_odd = sem("sel_odd")
        hidden_even = sem("hidden_even"); hidden_odd = sem("hidden_odd")
        inter_even = sem("inter_even"); inter_odd = sem("inter_odd")
        left = [[sem(f"left{h}{i}") for i in range(2)] for h in range(2)]
        back = [[sem(f"back{h}{i}") for i in range(NC)] for h in range(2)]
        summed = sem("summed")

        def emptied(key):
            kind, i = key
            return {"xT": [(xT_ready, 2 * CH, i + 1)], "logits": [(rated, 1, 1)],
                    "pT": [(chosen_ready, 4 * TP, 2 * i + 2)],
                    "sel": [(sel_even, 2 * TP, i + 1), (sel_odd, 2 * TP, i + 1)],
                    "h": [(hidden_even, 2 * PAIRS, HB * (i + 1)), (hidden_odd, 2 * PAIRS, HB * (i + 1))],
                    "inter": [(inter_even, 2 * IN, i + 1), (inter_odd, 2 * IN, i + 1)],
                    "out": [(summed, 2 * NC, i + 1)]}[kind]

        ring = Ring(plan, 4, emptied)

        def arrived(eng, b, key):
            eng.wait_ge(filled, ring.count(b, key))
            return slots[ring.slot(key)]

        NCONST = 5 + CH - 1
        NSETUP = 4
        block = ctx.enter_context(nc.Block())
        f2_rows = f2_in.rearrange("(p e) f d -> (e f) p d", e=2)

        def hidden_free(eng, b, p):
            if p >= 8:
                eng.wait_ge(filled, ring.count(b, ("inter", (p - 8) // 2)))

        def inter_free(eng, b, i):
            if i >= 2:
                half, n = (i - 2) // IN, (i - 2) % IN
                eng.wait_ge(left[half][n % 2], 16 * ((IN // 2) * b + n // 2 + 1))

        @block.sync
        def _(sp):
            sp.dma_start(ident[:, :], ident_in).then_inc(consts, 16)
            sp.dma_start(ctrl[:, :, :], controller.rearrange("(c p) e -> p c e", p=P)).then_inc(consts, 16)
            sp.dma_start(b1[:, :], f1_bias).then_inc(consts, 16)
            sp.dma_start(tie[:, :], on_all_partitions(tie_in, G)).then_inc(consts, 16)
            for c in range(CH):
                sp.dma_start(f1[:, c, :, :], f1_in.rearrange("(c p) e f -> p c e f", p=P)[:, c, :, :]).then_inc(consts, 16)

            with sp.Fori(0, NSEQ // 2) as b:
                for s in range(2):
                    sp.dma_start(wide[:, NT * s:NT * s + NT, :], tokens(x_in, 2 * b + s)).then_inc(x_loaded, 16)
                for half in range(2):
                    if half:
                        sp.wait_ge(filled, ring.count(b, ("inter", IN - 1)))
                    sp.dma_start(f2[:, :, :], f2_rows[:, PAIRS * half:PAIRS * half + PAIRS, :]).then_inc(f2_loaded, 16)
                    if half == 0:
                        wait_alone(sp, rated, b + 1)
                        for s in range(2):
                            sp.dma_start(total[:, NT * s:NT * s + NT, :], tokens(x_in, 2 * b + s)).then_inc(x_again, 16)
                    for n in range(IN):
                        i = IN * half + n
                        sp.wait_ge(inter_even, 2 * IN * b + i + 1)
                        sp.wait_ge(inter_odd, 2 * IN * b + i + 1)
                        sp.dma_start(scratch[half, :, 4 * n:4 * n + 4, :], inter[:, i % 2, :, :]).then_inc(left[half][i % 2], 16)
                    for i in range(2):
                        wait_alone(sp, left[half][i], 16 * (IN // 2) * (b + 1))
                    if half:
                        sp.wait_ge(filled, ring.count(b, ("out", NC - 1)))
                    rows = scratch[half, :, :, :].rearrange("(q j) e d -> (j e) q d", j=J)
                    for n in range(NC):
                        q = slice(NQ // NC * n, NQ // NC * (n + 1))
                        sp.dma_start(inter2[:, q, :], rows[:, q, :]).then_inc(back[half][n], 16)
                wait_alone(sp, ln.normed, ln.done(b, 0))
                for s in range(2):
                    sp.dma_start(tokens(y_out, 2 * b + s), wide[:, TT + NT * s:TT + NT * s + NT, :]).then_inc(stored, 16)
            sp.wait_ge(stored, 16 * NSEQ)

        @block.gpsimd
        def _(pool):
            pool.wait_ge(setup, NSETUP)
            pool.wait_ge(consts, 16 * NCONST)
            with pool.Fori(0, NSEQ // 2) as b:
                for n in range(2):
                    pool.wait_ge(hi_ready, 2 * b + n + 1)
                    part = slice(NT * n, NT * n + NT)
                    pool.tensor_tensor(lo[:, part, :], x[:, part, :], hi[:, part, :].bitcast(f32), ALU.subtract).then_inc(lo_ready, 1)
                pool.wait_ge(choice_ready, b + 1)
                wait_alone(pool, lo_ready, 2 * b + 2)
                for half in range(2):
                    for j in range(J):
                        if half or j:
                            wait_alone(pool, spread_ready, 2 * J * b + J * half + j)
                        rows = slice(EH * j, EH * j + EH)
                        pool.tensor_copy(spread[rows, half, :, j, :], choice[rows, half, :, :]).then_inc(spread_ready, 1)
                pool.wait_ge(spread_ready, 2 * J * (b + 1))
                ln.reciprocal_root(pool, b, 0)

        @block.scalar
        def _(act):
            act.wait_ge(setup, NSETUP)
            act.wait_ge(consts, 16 * NCONST)
            with act.Fori(0, NSEQ // 2) as b:
                act.wait_ge(x_loaded, 32 * b + 32)
                for n in range(2):
                    act.copy(hi[:, NT * n:NT * n + NT, :], x[:, NT * n:NT * n + NT, :]).then_inc(hi_ready, 1)
                for n in range(2 * CH):
                    c, s = n % CH, n // CH
                    act.copy(xT[:, c, T * s:T * s + T], arrived(act, b, ("xT", n))[:, :]).then_inc(xT_ready, 1)

                def take_choice(i):
                    if i % TP >= 2:
                        act.wait_ge(filled, ring.count(b, ("sel", i - 2)))
                    s = arrived(act, b, ("pT", i))[:, 0:2 * P].rearrange("p (t n) -> p t n", t=2)
                    for q in range(2):
                        rows = slice(64 * q, 64 * q + 64)
                        act.copy(chosen[rows, i % 2, :, q, :], s[rows, :, :]).then_inc(chosen_ready, 1)

                for half in range(2):
                    take_choice(half * TP)
                    for tp in range(TP):
                        i = half * TP + tp
                        if tp + 1 < TP:
                            take_choice(i + 1)
                        s = arrived(act, b, ("sel", i))[:, 0:512].rearrange("p (g e) -> p e g", e=EH)
                        act.copy(sel[:, 0, :, 16 * tp:16 * tp + 16], s).then_inc(sel_even, 1)
                    for key in experts(half):
                        s = arrived(act, b, key)
                        if key[0] == "h":
                            for n in range(HB):
                                p = HB * key[1] + n
                                hidden_free(act, b, p)
                                act.activation(hidden[0:64, p % 8, 0, :], s[0:64, NG * n:NG * n + NG], ACT.Relu,
                                               bias=b1[0:64, p:p + 1]).then_inc(hidden_even, 1)
                        else:
                            i = key[1]
                            inter_free(act, b, i)
                            act.copy(inter[:, i % 2, 0:2, :], s[:, 0:512].rearrange("p (e d) -> p e d", e=2)).then_inc(inter_even, 1)

        def combine(dve, b, half):
            if half == 0:
                dve.wait_ge(x_again, 32 * b + 32)
            else:
                dve.wait_ge(summed, 2 * NC * b + NC)
            for n in range(NC):
                s = arrived(dve, b, ("out", NC * half + n))[:, :].rearrange("p (t d) -> p t d", t=4)
                part = total[:, 4 * n:4 * n + 4, :]
                dve.tensor_tensor(part, s, part, ALU.add).then_inc(summed, 1)

        @block.vector
        def _(dve):
            dve.memset(spread[:, :, :, :, :], 0.0).then_inc(setup, 1)
            dve.memset(chosen[:, :, :, :, :].bitcast(f32), 0.0).then_inc(setup, 1)
            dve.memset(hidden[:, :, :, :], 0.0).then_inc(setup, 1)
            dve.memset(ln.half[:, :], -0.5).then_inc(setup, 1)
            dve.wait_ge(consts, 16 * NCONST)
            with dve.Fori(0, NSEQ // 2) as b:
                s = arrived(dve, b, ("logits", 0))[:, :].rearrange("p (h q t) -> p (h q) t", h=2, t=G)
                marks = choice[:, :, :, :].rearrange("p h q t -> p (h q) t")
                top = best[:, :, :].rearrange("p h q -> p (h q)")
                dve.tensor_tensor(marks, s, tie[:, :].unsqueeze(1).broadcast_to([P, 2 * NQ, G]), ALU.add).then_inc(rated, 1)
                dve.wait_ge(rated, b + 1)
                dve.reduce_max(top, marks, AX).then_inc(best_ready, 1)
                dve.wait_ge(best_ready, b + 1)
                dve.tensor_tensor(marks, marks, top.unsqueeze(2).broadcast_to([P, 2 * NQ, G]), ALU.is_equal)\
                    .then_inc(choice_ready, 1)
                for half in range(2):
                    for tp in range(TP):
                        i = half * TP + tp
                        s = arrived(dve, b, ("sel", i))[:, 512:1024].rearrange("p (g e) -> p e g", e=EH)
                        dve.tensor_copy(sel[:, 1, :, 16 * tp:16 * tp + 16], s).then_inc(sel_odd, 1)
                    if half:
                        combine(dve, b, 0)
                    for key in experts(half):
                        s = arrived(dve, b, key)
                        if key[0] == "h":
                            for n in range(HB):
                                p = HB * key[1] + n
                                hidden_free(dve, b, p)
                                dve.tensor_scalar(hidden[64:128, p % 8, 1, :], s[64:128, NG * n:NG * n + NG],
                                                  b1[64:128, p:p + 1], 0.0, ALU.add, ALU.max).then_inc(hidden_odd, 1)
                        else:
                            i = key[1]
                            inter_free(dve, b, i)
                            dve.tensor_copy(inter[:, i % 2, 2:4, :], s[:, 512:1024].rearrange("p (e d) -> p e d", e=2))\
                                .then_inc(inter_odd, 1)
                combine(dve, b, 1)
                dve.wait_ge(summed, 2 * NC * (b + 1))
                ln.statistics(dve, total, b, 0)
                ln.normalise(dve, y, total, b, 0)

        @block.tensor
        def _(pe):
            mm = nc.tensor.matmul
            pe.wait_ge(setup, NSETUP)
            pe.wait_ge(consts, 16 * NCONST)
            with pe.Fori(0, NSEQ // 2) as b:
                def use(key):
                    ring.wait_free(pe, b, key)
                    return slots[ring.slot(key)]

                def transpose_choice(i):
                    half, tp = i // TP, i % TP
                    s = use(("pT", i))
                    if tp == 0:
                        pe.wait_ge(spread_ready, 2 * J * b + J * (half + 1))
                    for t in range(2):
                        q = 2 * (2 * tp + t)
                        last = nc.tensor.transpose(s[:, P * t:P * t + P],
                                                   spread[:, half, q:q + 2, :, :].rearrange("p q j t -> p (q j t)"), ident[:, :])
                    last.then_inc(filled, 1)

                def select(i):
                    tp = i % TP
                    s = use(("sel", i))
                    pe.wait_ge(chosen_ready, 4 * TP * b + 2 * i + 2)
                    for c in range(CH):
                        for t in range(2):
                            o = s[:, 512 * c + 256 * t:512 * c + 256 * t + 256]
                            rhs = chosen[:, i % 2, t, :, :].rearrange("p q n -> p (q n)")
                            for part in (hi, lo):
                                last = mm(o, part[:, 2 * tp + t, P * c:P * c + P], rhs, start=part is hi, stop=part is lo)
                    last.then_inc(filled, 1)

                def expert(key):
                    s = use(key)
                    i = key[1]
                    if key[0] == "h":
                        if i % 2 == 0:
                            pe.wait_ge(sel_even, 2 * TP * b + TP * (i // 2 + 1))
                            pe.wait_ge(sel_odd, 2 * TP * b + TP * (i // 2 + 1))
                        for n in range(HB):
                            e0 = 2 * (HB * i + n)
                            for c in range(CH):
                                for k in range(2):
                                    last = mm(s[64 * k:64 * k + 64, NG * n:NG * n + NG], f1[:, c, e0 + k, :],
                                              sel[:, c, (e0 + k) % EH, :], start=c == 0, stop=c == CH - 1)
                    else:
                        for n in range(2):
                            p = 2 * i + n
                            pe.wait_ge(hidden_even, 2 * PAIRS * b + p + 1)
                            pe.wait_ge(hidden_odd, 2 * PAIRS * b + p + 1)
                            if i % IN == 0 and n == 0:
                                pe.wait_ge(f2_loaded, 16 * (2 * b + i // IN + 1))
                            for k in range(2):
                                last = mm(s[:, D * (2 * n + k):D * (2 * n + k + 1)], hidden[:, p % 8, k, :], f2[:, p % PAIRS, :],
                                          start=True, stop=True)
                    last.then_inc(filled, 1)

                def combine_on_pe(half):
                    for n in range(NC):
                        s = use(("out", NC * half + n))
                        pe.wait_ge(back[half][n], 16 * b + 16)
                        for t in range(4):
                            for k in range(2):
                                q = 2 * (4 * n + t) + k
                                last = mm(s[64 * k:64 * k + 64, D * t:D * t + D],
                                          spread[:, half, q, :, :].rearrange("p j t -> p (j t)"), inter2[:, q, :],
                                          start=True, stop=True)
                        last.then_inc(filled, 1)

                pe.wait_ge(x_loaded, 32 * b + 32)
                for n in range(2 * CH):
                    c, sq = n % CH, n // CH
                    s = use(("xT", n))
                    for t in range(NT):
                        last = nc.tensor.transpose(s[:, P * t:P * t + P], x[:, NT * sq + t, P * c:P * c + P], ident[:, :])
                    last.then_inc(filled, 1)
                s = use(("logits", 0))
                pe.wait_ge(xT_ready, 2 * CH * (b + 1))
                for half in range(2):
                    for c in range(CH):
                        by_quad = xT[:, c, :].rearrange("p (q j t) -> p q j t", j=J, t=G)
                        for j in range(J):
                            last = mm(s[EH * j:EH * j + EH, 512 * half:512 * half + 512], ctrl[:, c, EH * half:EH * half + EH],
                                      by_quad[:, :, j, :], start=c == 0, stop=c == CH - 1, tile_position=(0, EH * j))
                last.then_inc(filled, 1)
                for half in range(2):
                    if half == 0:
                        pe.wait_ge(lo_ready, 2 * b + 2)
                    for kind, i in selection(half):
                        (transpose_choice if kind == "pT" else select)(i)
                    if half:
                        combine_on_pe(0)
                    for key in experts(half):
                        expert(key)
                combine_on_pe(1)


def linear_attention_layer(nc, x_in, y_out, wqkvT, wprojT, bproj, ident_in, head_blocks_in):
    DH = 16
    HC = P // DH
    CH = D // P
    EPS = 1e-6
    W1 = P + HC
    PAIRS = NT // 2

    plan = [("xT", c) for c in range(CH)] + [("q", c) for c in range(CH)] + [("kv", g) for g in range(PAIRS)]
    plan += ["state"] + [("mix", g) for g in range(PAIRS)] + [("aoT", c) for c in range(CH)] + [("proj", g) for g in range(2)]

    with ExitStack() as ctx:
        sb, ps, sem = allocators(nc, ctx, "l1a")
        wqkv = sb("wqkv", [P, CH, 3 * D]); wproj = sb("wproj", [P, CH, D])
        bias = sb("bias", [P, D])
        ident = sb("ident", [P, P])
        head_blocks = sb("head_blocks", [P, W1])
        consts = sem("consts"); setup = sem("setup")

        class Stream:
            def __init__(self, s):
                def buf(name, shape):
                    return sb(f"{name}{s}", shape)

                def sig(name):
                    return sem(f"{name}{s}")

                self.s = s
                self.x = buf("x", [P, NT, D]); self.y = buf("y", [P, NT, D])
                self.xT = buf("xT", [P, CH, T])
                self.exp_q = buf("exp_q", [P, CH, T]); self.exp_k = buf("exp_k", [P, NT, D])
                self.qT = buf("qT", [P, CH, T]); self.k = buf("k", [P, NT, D])
                self.v1 = buf("v1", [P, NT, CH, P + 1])
                self.state = buf("state", [P, CH, W1])
                self.z = buf("z", [P, PAIRS, 2, CH, HC])
                self.ao = buf("ao", [P, NT, D]); self.aoT = buf("aoT", [P, CH, T])
                self.ln = LayerNorm(sb, sem, f"ln{s}", setup, 1)
                self.slots = [ps(f"slot{s}{i}", [P, 1024]) for i in range(2)]
                self.x_loaded = sig("x_loaded"); self.stored = sig("stored")
                self.filled = sig("filled"); self.xT_ready = sig("xT_ready"); self.v_ready = sig("v_ready")
                self.exp_ready = sig("exp_ready"); self.clipped = sig("clipped"); self.features = sig("features")
                self.state_ready = sig("state_ready"); self.den_ready = sig("den_ready"); self.z_ready = sig("z_ready")
                self.mixed = sig("mixed"); self.aoT_ready = sig("aoT_ready"); self.biased = sig("biased")
                self.summed = sig("summed")
                self.ring = Ring(plan, 2, self.emptied)

            def emptied(self, key):
                if key == "state":
                    return [(self.state_ready, 2 * CH, 2 * CH)]
                kind, i = key
                return [{"xT": (self.xT_ready, CH, i + 1), "q": (self.features, CH + PAIRS, i + 1),
                        "kv": (self.features, CH + PAIRS, CH + i + 1), "mix": (self.mixed, PAIRS, i + 1),
                        "aoT": (self.aoT_ready, CH, i + 1), "proj": (self.summed, 2, i + 1)}[kind]]

            def slot(self, key):
                return self.slots[self.ring.slot(key)]

        streams = [Stream(s) for s in range(2)]
        block = ctx.enter_context(nc.Block())

        def arrived(eng, st, b, key):
            eng.wait_ge(st.filled, st.ring.count(b, key))
            return st.slot(key)

        def run(steps, b):
            for step in steps:
                for st in streams:
                    step(st, b)

        NCONST = 5

        @block.sync
        def _(sp):
            sp.dma_start(ident[:, :], ident_in).then_inc(consts, 16)
            sp.dma_start(wqkv[:, :, :], wqkvT.rearrange("(c p) n -> p c n", p=P)).then_inc(consts, 16)
            sp.dma_start(wproj[:, :, :], wprojT.rearrange("(c p) n -> p c n", p=P)).then_inc(consts, 16)
            sp.dma_start(bias[:, :], on_all_partitions(bproj, D)).then_inc(consts, 16)
            sp.dma_start(head_blocks[:, :], head_blocks_in).then_inc(consts, 16)

            def load(st, b):
                sp.dma_start(st.x[:, :, :], tokens(x_in, 2 * b + st.s)).then_inc(st.x_loaded, 16)

            def store(st, b):
                wait_alone(sp, st.ln.normed, st.ln.done(b, 0))
                sp.dma_start(tokens(y_out, 2 * b + st.s), st.y[:, :, :]).then_inc(st.stored, 16)

            with sp.Fori(0, NSEQ // 2) as b:
                run([load, store], b)
            for st in streams:
                sp.wait_ge(st.stored, 16 * (NSEQ // 2) + 16)

        @block.gpsimd
        def _(pool):
            pool.wait_ge(setup, 4)
            pool.wait_ge(consts, 16 * NCONST)

            def clip(st, b):
                for i in range(CH + PAIRS):
                    wait_alone(pool, st.exp_ready, b * (CH + PAIRS) + i + 1)
                    part = st.exp_q[:, i, :] if i < CH else st.exp_k[:, 2 * (i - CH):2 * (i - CH) + 2, :]
                    pool.tensor_scalar(part, part, 1.0, None, ALU.min).then_inc(st.clipped, 1)

            def bias_x(st, b):
                pool.wait_ge(st.x_loaded, 16 * b + 16)
                pool.wait_ge(st.xT_ready, CH * b + CH)
                pool.tensor_tensor(st.x[:, :, :], st.x[:, :, :], each_tile(bias), ALU.add).then_inc(st.biased, 1)

            def norm(st, b):
                st.ln.reciprocal_root(pool, b, 0)

            with pool.Fori(0, NSEQ // 2) as b:
                run([clip, bias_x, norm], b)

        @block.scalar
        def _(act):
            act.wait_ge(setup, 4)
            act.wait_ge(consts, 16 * NCONST)

            def copy_xT(st, b):
                for c in range(CH):
                    act.copy(st.xT[:, c, :], arrived(act, st, b, ("xT", c))[:, :]).then_inc(st.xT_ready, 1)

            def exp_q(st, b):
                for c in range(CH):
                    act.activation(st.exp_q[:, c, :], arrived(act, st, b, ("q", c))[:, :], ACT.Exp).then_inc(st.exp_ready, 1)

            def exp_k(st, b):
                for g in range(PAIRS):
                    kv = arrived(act, st, b, ("kv", g))[:, :].rearrange("p (t n) -> p t n", t=2)
                    for t in range(2):
                        act.copy(st.v1[:, 2 * g + t, :, 0:P], kv[:, t, D:2 * D].rearrange("p (c n) -> p c n", c=CH))\
                            .then_inc(st.v_ready, 1)
                    act.activation(st.exp_k[:, 2 * g:2 * g + 2, :], kv[:, :, 0:D], ACT.Exp).then_inc(st.exp_ready, 1)

            def copy_aoT(st, b):
                for c in range(CH):
                    act.copy(st.aoT[:, c, :], arrived(act, st, b, ("aoT", c))[:, :]).then_inc(st.aoT_ready, 1)

            with act.Fori(0, NSEQ // 2) as b:
                run([copy_xT, exp_q, exp_k, copy_aoT], b)

        @block.vector
        def _(dve):
            for st in streams:
                dve.memset(st.v1[:, :, :, P:P + 1], 1.0).then_inc(setup, 1)
                dve.memset(st.ln.half[:, :], -0.5).then_inc(setup, 1)
            for st in streams:
                dve.sem_inc(st.stored, 16)
            dve.wait_ge(consts, 16 * NCONST)

            def features(st, b):
                for i in range(CH + PAIRS):
                    if i < CH:
                        x, e, o = arrived(dve, st, b, ("q", i))[:, :], st.exp_q[:, i, :], st.qT[:, i, :]
                    else:
                        g = i - CH
                        x = arrived(dve, st, b, ("kv", g))[:, :].rearrange("p (t n) -> p t n", t=2)[:, :, 0:D]
                        e, o = st.exp_k[:, 2 * g:2 * g + 2, :], st.k[:, 2 * g:2 * g + 2, :]
                    dve.wait_ge(st.clipped, b * (CH + PAIRS) + i + 1)
                    dve.scalar_tensor_tensor(o, x, 0.0, e, ALU.max, ALU.add).then_inc(st.features, 1)

            def state(st, b):
                s = arrived(dve, st, b, "state")
                for c in range(CH):
                    dve.tensor_tensor(st.state[:, c, 0:P], s[:, 512 * c:512 * c + P], head_blocks[:, 0:P], ALU.mult)\
                        .then_inc(st.state_ready, 1)
                    dve.tensor_scalar(st.state[:, c, P:W1], head_blocks[:, P:W1], s[:, 512 * c + P:512 * c + P + 1], None,
                                      ALU.mult).then_inc(st.state_ready, 1)

            def mix(st, b):
                for g in range(PAIRS):
                    s = arrived(dve, st, b, ("mix", g))[:, :].rearrange("p (t n) -> p t n", t=2)[:, :, 0:CH * W1]\
                        .rearrange("p t (c n) -> p t c n", c=CH)
                    z = st.z[:, g, :, :, :]
                    dve.tensor_scalar(z, s[:, :, :, P:W1], EPS, None, ALU.add).then_inc(st.den_ready, 1)
                    dve.wait_ge(st.den_ready, PAIRS * b + g + 1)
                    dve.reciprocal(z, z).then_inc(st.z_ready, 1)
                    dve.wait_ge(st.z_ready, PAIRS * b + g + 1)
                    for t in range(2):
                        for c in range(CH):
                            ins = dve.tensor_tensor(
                                st.ao[:, 2 * g + t, P * c:P * c + P].rearrange("p (h n) -> p h n", h=HC),
                                s[:, t, c, 0:P].rearrange("p (h n) -> p h n", h=HC),
                                z[:, t, c, :].unsqueeze(2).broadcast_to([P, HC, DH]), ALU.mult)
                    ins.then_inc(st.mixed, 1)

            def residual(st, b):
                for g in range(2):
                    s = arrived(dve, st, b, ("proj", g))[:, :].rearrange("p (t n) -> p t n", t=4)
                    dve.wait_ge(st.biased, b + 1)
                    part = st.x[:, 4 * g:4 * g + 4, :]
                    dve.tensor_tensor(part, s, part, ALU.add).then_inc(st.summed, 1)
                dve.wait_ge(st.summed, 2 * b + 2)
                st.ln.statistics(dve, st.x, b, 0)

            def norm(st, b):
                dve.wait_ge(st.stored, 16 * b + 16)
                st.ln.normalise(dve, st.y, st.x, b, 0)

            with dve.Fori(0, NSEQ // 2) as b:
                run([features, state, mix, residual, norm], b)

        @block.tensor
        def _(pe):
            mm = nc.tensor.matmul
            pe.wait_ge(setup, 4)
            pe.wait_ge(consts, 16 * NCONST)

            def use(st, b, key):
                st.ring.wait_free(pe, b, key)
                return st.slot(key)

            def transpose_x(st, b):
                pe.wait_ge(st.x_loaded, 16 * b + 16)
                for c in range(CH):
                    s = use(st, b, ("xT", c))
                    for t in range(NT):
                        last = nc.tensor.transpose(s[:, P * t:P * t + P], st.x[:, t, P * c:P * c + P], ident[:, :])
                    last.then_inc(st.filled, 1)

            def project_q(st, b):
                pe.wait_ge(st.xT_ready, CH * b + CH)
                for c in range(CH):
                    s = use(st, b, ("q", c))
                    for half in range(2):
                        cols = slice(512 * half, 512 * half + 512)
                        for k in range(CH):
                            last = mm(s[:, cols], wqkv[:, k, P * c:P * c + P], st.xT[:, k, cols], start=k == 0, stop=k == CH - 1)
                    last.then_inc(st.filled, 1)

            def project_kv(st, b):
                for g in range(PAIRS):
                    s = use(st, b, ("kv", g))
                    for t in range(2):
                        tok = P * (2 * g + t)
                        for k in range(CH):
                            last = mm(s[:, 512 * t:512 * t + 512], st.xT[:, k, tok:tok + P], wqkv[:, k, D:3 * D],
                                      start=k == 0, stop=k == CH - 1)
                    last.then_inc(st.filled, 1)

            def sum_state(st, b):
                s = use(st, b, "state")
                pe.wait_ge(st.v_ready, NT * b + NT)
                pe.wait_ge(st.features, (b + 1) * (CH + PAIRS))
                for c in range(CH):
                    for t in range(NT):
                        last = mm(s[:, 512 * c:512 * c + P + 1], st.k[:, t, P * c:P * c + P], st.v1[:, t, c, :],
                                  start=t == 0, stop=t == NT - 1)
                last.then_inc(st.filled, 1)

            def mix(st, b):
                pe.wait_ge(st.state_ready, (b + 1) * 2 * CH)
                for g in range(PAIRS):
                    s = use(st, b, ("mix", g))
                    for t in range(2):
                        tok = P * (2 * g + t)
                        for c in range(CH):
                            at = 512 * t + W1 * c
                            last = mm(s[:, at:at + W1], st.qT[:, c, tok:tok + P], st.state[:, c, :], start=True, stop=True)
                    last.then_inc(st.filled, 1)

            def transpose_ao(st, b):
                pe.wait_ge(st.mixed, PAIRS * (b + 1))
                for c in range(CH):
                    s = use(st, b, ("aoT", c))
                    for t in range(NT):
                        last = nc.tensor.transpose(s[:, P * t:P * t + P], st.ao[:, t, P * c:P * c + P], ident[:, :])
                    last.then_inc(st.filled, 1)

            def project_out(st, b):
                pe.wait_ge(st.aoT_ready, CH * (b + 1))
                for g in range(2):
                    s = use(st, b, ("proj", g))
                    for t in range(4):
                        tok = P * (4 * g + t)
                        for k in range(CH):
                            last = mm(s[:, D * t:D * t + D], st.aoT[:, k, tok:tok + P], wproj[:, k, :], start=k == 0, stop=k == CH - 1)
                    last.then_inc(st.filled, 1)

            with pe.Fori(0, NSEQ // 2) as b:
                run([transpose_x, project_q, project_kv, sum_state, mix, transpose_ao, project_out], b)
def nested_width_attention_layer(nc, x_in, y_out, q_wT, q_b, k_wT, k_b, v_wT, v_b, o_wT, o_b, norm_w, norm_b, ident_in):
    H, DH = 8, 32
    NE = 4
    QW = T // NE
    SCALE = float(D) ** -0.5
    width = [D >> e for e in range(NE)]
    BATCHES = [[(h, 0) for h in range(4)], [(h, 0) for h in range(4, 8)], [(h, 1) for h in range(4)],
               [(0, 2), (1, 2), (0, 3)]]
    UNITS = [u for batch in BATCHES for u in batch]
    FIRST = [sum(len(b) for b in BATCHES[:i]) for i in range(len(BATCHES))]
    NB = len(BATCHES)

    plan = [("xT0", 0), ("xT1", 0), ("k", 0), ("k", 1), ("q", 0), ("q", 1), ("v", 0), ("v", 1)]
    def nat(i):
        return [("nat", FIRST[i] + u, t) for u in range(len(BATCHES[i])) for t in range(2)] + [("mT", i)]
    def tr(i):
        return [("tr", FIRST[i] + u, half) for u in range(len(BATCHES[i])) for half in range(2)]
    plan += nat(0) + nat(1) + tr(0) + nat(2) + tr(1) + nat(3) + tr(2) + tr(3) + [("out", 0)]
    ring = Ring(plan, 3)
    NPLAN = len(plan)
    NU = 2 * len(UNITS)

    with ExitStack() as ctx:
        sb, ps, sem = allocators(nc, ctx, "l1f")
        consts = sem("consts"); setup = sem("setup")
        x = sb("x", [P, NT, D]); xn = sb("xn", [P, NT, D])
        xT = [sb("xT0", [P, T]), sb("xT1", [P, QW])]
        hi_k = sb("hi_k", [P, 2, T], f32r); lo_k = sb("lo_k", [P, 2, T], f32r)
        hi_q = sb("hi_q", [P, T + QW], f32r); lo_q = sb("lo_q", [P, T + QW], f32r)
        Qs = sb("Qs", [P, len(UNITS), QW], f32r)
        Ks = sb("Ks", [P, H, T], f32r)
        V = sb("V", [P, NT, D])
        probs = sb("probs", [P, 2, 4, NT * QW])
        recip = sb("recip", [P, 2, QW])
        aoT = [sb("aoT0", [P, T]), sb("aoT1", [P, QW])]
        wq = sb("wq", [P, 2, D]); wk = sb("wk", [P, 2, D]); wv = sb("wv", [P, 2, D]); wo = sb("wo", [P, 2, D])
        qb = sb("qb", [P, 2]); kb = sb("kb", [P, 2]); vb = sb("vb", [P, D]); nw = sb("nw", [P, D]); nb = sb("nb", [P, D])
        ob = sb("ob", [P, NE, D])
        ident = sb("ident", [P, P])
        ones = sb("ones", [P, DH])
        rowmax = sb("rowmax", [P, 2 * len(UNITS)])
        maxT = sb("maxT", [8, 2, P], f32r)
        ln = LayerNorm(sb, sem, "ln", setup, 2)
        slots = [ps(f"slot{i}", [P, 1024]) for i in range(3)]
        OS = [ps(f"os{i}", [P, 2, QW]) for i in range(2)]

        x_loaded = sem("x_loaded"); stored = sem("stored")
        scaled = sem("scaled"); xn_ready = sem("xn_ready"); xT0_ready = sem("xT0_ready"); xT1_ready = sem("xT1_ready")
        doubled = sem("doubled"); x2_ready = sem("x2_ready"); summed = sem("summed"); recip_ready = sem("recip_ready")
        hi_ready = sem("hi_ready"); lo_ready = sem("lo_ready"); v_ready = sem("v_ready")
        stacked = sem("stacked")
        max_done = sem("max_done"); maxT_ready = sem("maxT_ready"); max_placed = [sem(f"max_placed{i}") for i in range(NB)]
        exp_done = sem("exp_done"); pv_done = sem("pv_done"); ao_ready = sem("ao_ready")
        filled = sem("filled")

        def emptied(key):
            kind = key[0]
            if kind == "nat":
                return [(max_done, NU, 2 * key[1] + key[2] + 1)]
            if kind == "tr":
                return [(exp_done, NU, 2 * key[1] + key[2] + 1)]
            i = key[1]
            return [{"xT0": (xT0_ready, 3, 3), "xT1": (xT1_ready, 1, 1), "out": (summed, NE, NE),
                     "k": (lo_ready, 4, i + 1), "q": (lo_ready, 4, i + 3), "v": (v_ready, 2, i + 1),
                     "mT": (maxT_ready, NB, i + 1)}[kind]]

        ring.emptied = emptied

        def slot(key):
            return slots[ring.slot(key)]

        NSTACK = 3 * (H + len(UNITS))
        block = ctx.enter_context(nc.Block())

        @block.sync
        def _(sp):
            for w, src in ((wq, q_wT), (wk, k_wT), (wv, v_wT), (wo, o_wT)):
                sp.dma_start(w[:, :, :], src.rearrange("(c p) n -> p c n", p=P)).then_inc(consts, 16)
            for v, src in ((qb, q_b), (kb, k_b)):
                sp.dma_start(v[:, :], src).then_inc(consts, 16)
            for v, src in ((vb, v_b), (nw, norm_w), (nb, norm_b)):
                sp.dma_start(v[:, :], on_all_partitions(src, D)).then_inc(consts, 16)
            sp.wait_ge(setup, 1)
            for e in range(NE):
                sp.dma_start(ob[:, e, 0:width[e]], on_all_partitions(o_b, width[e])).then_inc(consts, 16)
            sp.dma_start(ident[:, :], ident_in).then_inc(consts, 16)
            with sp.Fori(0, NSEQ) as b:
                sp.dma_start(x[:, :, :], tokens(x_in, b)).then_inc(x_loaded, 16)
                for h in range(H):
                    c, p0 = h // 4, DH * (h % 4)
                    if h % 4 == 0:
                        sp.wait_ge(lo_ready, b * 4 + c + 1)
                    for r, part in enumerate((hi_k, hi_k, lo_k)):
                        sp.dma_start(words(Ks[DH * r:DH * r + DH, h, :]), words(part[p0:p0 + DH, c, :])).then_inc(stacked, 16)
                for u, (h, e) in enumerate(UNITS):
                    if u in (0, 4):
                        sp.wait_ge(lo_ready, b * 4 + 3 + (u == 4))
                    p0, col = DH * (h % 4), QW * e + (T if h >= 4 else 0)
                    for r, part in enumerate((hi_q, lo_q, hi_q)):
                        sp.dma_start(words(Qs[DH * r:DH * r + DH, u, :]), words(part[p0:p0 + DH, col:col + QW])).then_inc(stacked, 16)
                for i in range(NB):
                    n = len(BATCHES[i])
                    sp.wait_ge(maxT_ready, b * NB + i + 1)
                    sp.dma_start(words(Qs[3 * DH:3 * DH + 1, FIRST[i]:FIRST[i] + n, :]).rearrange("o u (t q) -> o (u t) q", q=P),
                                 words(maxT[0:2 * n, i % 2, :])).then_inc(max_placed[i], 16)
                wait_alone(sp, ln.normed, ln.done(b, 1))
                sp.dma_start(tokens(y_out, b), xn[:, :, :]).then_inc(stored, 16)
            sp.wait_ge(stored, 16 * NSEQ + 16)

        @block.gpsimd
        def _(pool):
            pool.wait_ge(setup, 6)
            pool.wait_ge(consts, 16 * 14)
            with pool.Fori(0, NSEQ) as b:
                ln.reciprocal_root(pool, b, 0)
                pool.wait_ge(ln.normed, ln.done(b, 0))
                pool.tensor_tensor(xn[:, :, :], xn[:, :, :], each_tile(nw), ALU.mult).then_inc(scaled, 1)
                pool.wait_ge(scaled, b + 1)
                pool.tensor_tensor(xn[:, :, :], xn[:, :, :], each_tile(nb), ALU.add).then_inc(xn_ready, 1)
                pool.tensor_tensor(x[:, :, :], x[:, :, :], x[:, :, :], ALU.add).then_inc(doubled, 1)
                pool.wait_ge(doubled, b + 1)
                for e in range(NE):
                    pool.tensor_tensor(x[:, 2 * e:2 * e + 2, :], x[:, 2 * e:2 * e + 2, :],
                                       ob[:, e:e + 1, :].broadcast_to([P, 2, D]), ALU.add).then_inc(x2_ready, 1)
                ln.reciprocal_root(pool, b, 1)

        @block.scalar
        def _(act):
            act.wait_ge(setup, 6)
            act.wait_ge(consts, 16 * 14)
            with act.Fori(0, NSEQ) as b:
                act.wait_ge(filled, ring.count(b, ("xT0", 0)))
                s = slot(("xT0", 0))
                act.copy(xT[0][:, 0:512], s[:, 0:512]).then_inc(xT0_ready, 1)
                act.copy(xT[0][0:64, 512:768], s[0:64, 512:768]).then_inc(xT0_ready, 1)
                act.copy(xT[0][0:32, 768:1024], s[0:32, 768:1024]).then_inc(xT0_ready, 1)
                for what, hi, bias in (("k", hi_k, kb), ("q", hi_q, qb)):
                    for c in range(2):
                        n = T if what == "k" or c == 0 else QW
                        dst = hi[:, c, :] if what == "k" else hi[:, T * c:T * c + n]
                        act.wait_ge(filled, ring.count(b, (what, c)))
                        act.activation(dst, slot((what, c))[:, 0:n], ACT.Identity, bias=bias[:, c:c + 1])\
                            .then_inc(hi_ready, 1)
                for i, batch in enumerate(BATCHES):
                    if i >= 2:
                        act.wait_ge(pv_done, b * NB + i - 1)
                    for u in range(len(batch)):
                        for half in range(2):
                            key = ("tr", FIRST[i] + u, half)
                            act.wait_ge(filled, ring.count(b, key))
                            act.activation(probs[:, i % 2, u, 1024 * half:1024 * half + 1024],
                                           slot(key)[:, :], ACT.Exp, scale=SCALE)\
                                .then_inc(exp_done, 1)

        @block.vector
        def _(dve):
            dve.memset(ob[:, :, :], 0.0).then_inc(setup, 1)
            dve.memset(ones[:, :], 1.0).then_inc(setup, 1)
            dve.memset(Qs[96:128, :, :].bitcast(f32), 0.0).then_inc(setup, 1)
            dve.memset(Ks[96:128, :, :].bitcast(f32), -1.0).then_inc(setup, 1)
            dve.memset(xT[0][:, :], 0.0).then_inc(setup, 1)
            dve.memset(ln.half[:, :], -0.5).then_inc(setup, 1)
            dve.wait_ge(setup, 6)
            dve.wait_ge(consts, 16 * 14)
            dve.sem_inc(stored, 16)
            with dve.Fori(0, NSEQ) as b:
                dve.wait_ge(x_loaded, 16 * b + 16)
                dve.wait_ge(stored, 16 * b + 16)
                ln.statistics(dve, x, b, 0)
                ln.normalise(dve, xn, x, b, 0)
                dve.wait_ge(filled, ring.count(b, ("xT1", 0)))
                dve.tensor_copy(xT[1][:, :], slot(("xT1", 0))[:, 0:QW]).then_inc(xT1_ready, 1)
                n_lo = 0
                for what, hi, lo, bias in (("k", hi_k, lo_k, kb), ("q", hi_q, lo_q, qb)):
                    for c in range(2):
                        n = T if what == "k" or c == 0 else QW
                        at = (lambda t: t[:, c, :]) if what == "k" else (lambda t: t[:, T * c:T * c + n])
                        n_lo += 1
                        dve.wait_ge(hi_ready, b * 4 + n_lo)
                        dve.scalar_tensor_tensor(at(lo), slot((what, c))[:, 0:n], bias[:, c:c + 1],
                                                 at(hi), ALU.add, ALU.subtract).then_inc(lo_ready, 1)
                for g in range(2):
                    dve.wait_ge(filled, ring.count(b, ("v", g)))
                    dve.tensor_tensor(V[:, 4 * g:4 * g + 4, :],
                                      slot(("v", g))[:, :].rearrange("p (t n) -> p t n", t=4),
                                      each_tile(vb, 4), ALU.add).then_inc(v_ready, 1)

                def maxima(i):
                    for u in range(FIRST[i], FIRST[i] + len(BATCHES[i])):
                        for t in range(2):
                            dve.wait_ge(filled, ring.count(b, ("nat", u, t)))
                            dve.reduce_max(rowmax[:, 2 * u + t:2 * u + t + 1], slot(("nat", u, t))[:, :],
                                           AX).then_inc(max_done, 1)
                    n = 2 * len(BATCHES[i])
                    dve.wait_ge(filled, ring.count(b, ("mT", i)))
                    if i >= 2:
                        dve.wait_ge(max_placed[i - 2], 16 * b + 16)
                    dve.tensor_copy(maxT[0:n, i % 2, :], slot(("mT", i))[0:n, 0:P]).then_inc(maxT_ready, 1)

                def norms(i):
                    dve.wait_ge(pv_done, b * NB + i + 1)
                    os = OS[i % 2]
                    rows = DH * len(BATCHES[i])
                    dve.reciprocal(recip[0:rows, i % 2, :], os[0:rows, 1, :]).then_inc(recip_ready, 1)
                    dve.wait_ge(recip_ready, b * NB + i + 1)
                    if i < 3:
                        c, e = (1, 0) if i == 1 else (0, i // 2)
                        dve.tensor_tensor(aoT[c][:, QW * e:QW * e + QW], os[:, 0, :], recip[:, i % 2, :], ALU.mult)\
                            .then_inc(ao_ready, 1)
                    else:
                        dve.tensor_tensor(aoT[0][0:64, 2 * QW:3 * QW], os[0:64, 0, :], recip[0:64, i % 2, :], ALU.mult)\
                            .then_inc(ao_ready, 1)
                        dve.tensor_tensor(aoT[0][0:32, 3 * QW:4 * QW], os[64:96, 0, :], recip[64:96, i % 2, :],
                                          ALU.mult).then_inc(ao_ready, 1)

                maxima(0); maxima(1); maxima(2); norms(0); maxima(3); norms(1); norms(2); norms(3)
                dve.wait_ge(filled, ring.count(b, ("out", 0)))
                dve.wait_ge(x2_ready, NE * b + NE)
                s = slot(("out", 0))
                at = 0
                for e in range(NE):
                    w = width[e]
                    o = s[:, at:at + 2 * w].rearrange("p (t n) -> p t n", t=2)
                    at += 2 * w
                    dve.tensor_tensor(x[:, 2 * e:2 * e + 2, 0:w], o, x[:, 2 * e:2 * e + 2, 0:w], ALU.add).then_inc(summed, 1)
                dve.wait_ge(summed, NE * b + NE)
                ln.statistics(dve, x, b, 1)
                ln.normalise(dve, xn, x, b, 1)

        @block.tensor
        def _(pe):
            pe.wait_ge(setup, 6)
            pe.wait_ge(consts, 16 * 14)
            with pe.Fori(0, NSEQ) as b:
                mm = nc.tensor.matmul

                def use(key):
                    ring.wait_free(pe, b, key)
                    return slot(key)

                pe.wait_ge(xn_ready, b + 1)
                s = use(("xT0", 0))
                for t in range(NT):
                    last = nc.tensor.transpose(s[:, P * t:P * t + P], xn[:, t, 0:P], ident[:, :])
                last.then_inc(filled, 1)
                s = use(("xT1", 0))
                for t in range(2):
                    last = nc.tensor.transpose(s[:, P * t:P * t + P], xn[:, t, P:D], ident[:, :])
                last.then_inc(filled, 1)
                pe.wait_ge(xT0_ready, 3 * b + 3)
                pe.wait_ge(xT1_ready, b + 1)
                for what, w in (("k", wk), ("q", wq)):
                    for c in range(2):
                        s = use((what, c))
                        cols = slice(P * c, P * c + P)
                        mm(s[:, 0:QW], w[:, 0, cols], xT[0][:, 0:QW], start=True, stop=False)
                        last = mm(s[:, 0:QW], w[:, 1, cols], xT[1][:, :], start=False, stop=True)
                        if what == "k" or c == 0:
                            mm(s[:, QW:2 * QW], w[:, 0, cols], xT[0][:, QW:2 * QW], start=True, stop=True)
                            last = mm(s[:, 2 * QW:T], w[:, 0, cols], xT[0][:, 2 * QW:T], start=True, stop=True)
                        last.then_inc(filled, 1)
                for g in range(2):
                    s = use(("v", g))
                    for t in range(4):
                        tok = 4 * g + t
                        o = s[:, D * t:D * t + D]
                        last = mm(o, xT[0][:, P * tok:P * tok + P], wv[:, 0, :], start=True, stop=tok >= 2)
                        if tok < 2:
                            last = mm(o, xT[1][:, P * tok:P * tok + P], wv[:, 1, :], start=False, stop=True)
                    last.then_inc(filled, 1)
                pe.wait_ge(stacked, 16 * (b * NSTACK + NSTACK))

                def natural(i):
                    for u in range(FIRST[i], FIRST[i] + len(BATCHES[i])):
                        h = UNITS[u][0]
                        for t in range(2):
                            s = use(("nat", u, t))
                            for half in range(2):
                                last = mm(s[:, 512 * half:512 * half + 512], Qs[0:96, u, P * t:P * t + P],
                                          Ks[0:96, h, 512 * half:512 * half + 512], start=True, stop=True)
                            last.then_inc(filled, 1)
                    s = use(("mT", i))
                    n = 2 * len(BATCHES[i])
                    pe.wait_ge(max_done, 2 * len(UNITS) * b + 2 * FIRST[i] + n)
                    nc.tensor.transpose(s[0:n, 0:P], rowmax[:, 2 * FIRST[i]:2 * FIRST[i] + n], ident[:, :])\
                        .then_inc(filled, 1)

                def transposed(i):
                    pe.wait_ge(max_placed[i], 16 * b + 16)
                    for u in range(FIRST[i], FIRST[i] + len(BATCHES[i])):
                        h = UNITS[u][0]
                        for half in range(2):
                            s = use(("tr", u, half))
                            for j in range(4):
                                kt = 4 * half + j
                                last = mm(s[:, QW * j:QW * j + QW], Ks[:, h, P * kt:P * kt + P], Qs[:, u, :],
                                          start=True, stop=True)
                            last.then_inc(filled, 1)

                def values(i):
                    n = len(BATCHES[i])
                    pe.wait_ge(exp_done, 2 * (b * len(UNITS) + FIRST[i] + n))
                    if i >= 2:
                        pe.wait_ge(ao_ready, (NB + 1) * b + i - 1)
                    os = OS[i % 2]
                    for kt in range(NT):
                        for what in range(2):
                            for u in range(n):
                                h = BATCHES[i][u][0]
                                lhsT = ones[:, :] if what else V[:, kt, DH * h:DH * h + DH]
                                last = mm(os[DH * u:DH * u + DH, what, :], lhsT, probs[:, i % 2, u, QW * kt:QW * kt + QW],
                                          start=kt == 0 and what == 0, stop=kt == NT - 1, skip_group_check=True,
                                          tile_position=(0, DH * u))
                    last.then_inc(pv_done, 1)

                pe.wait_ge(v_ready, 2 * b + 2)
                natural(0); natural(1); transposed(0); natural(2)
                values(0); transposed(1); natural(3); values(1); transposed(2); values(2); transposed(3)
                values(3)
                s = use(("out", 0))
                pe.wait_ge(ao_ready, (NB + 1) * b + NB + 1)
                at = 0
                for e in range(NE):
                    w = width[e]
                    for t in (2 * e, 2 * e + 1):
                        k = min(w, P)
                        last = mm(s[:, at:at + w], aoT[0][0:k, P * t:P * t + P], wo[0:k, 0, 0:w], start=True, stop=w <= P)
                        if w > P:
                            last = mm(s[:, at:at + w], aoT[1][:, P * t:P * t + P], wo[:, 1, 0:w], start=False, stop=True)
                        at += w
                last.then_inc(filled, 1)



def four_layers(nc, x, wq, wk, bq, bk, wv, bv, wo, bo, cos, sin, mask, maskT, ident, ident16,
                controller, f1, f2, f1_bias, tie, wqkv, wproj, bproj, head_blocks,
                q_w, q_b, k_w, k_b, v_w, v_b, o_w, o_b, norm_w, norm_b, out):
    def dram(name, shape):
        return nc.dram_tensor(name, shape, f32, kind="Internal").ap()

    x1, x2, x3 = (dram(f"x{i}", (NSEQ, T, D)) for i in (1, 2, 3))
    window_attention_layer(nc, x, x1, wq, wk, bq, bk, wv, bv, wo, bo, cos, sin, mask, maskT, ident, ident16,
                           dram("qk_rows", (2, 2, 16, 16, T)))
    token_choice_layer(nc, x1, x2, controller, f1, f2, f1_bias, tie, ident, dram("expert_outputs", (2, 128, 32, D)))
    linear_attention_layer(nc, x2, x3, wqkv, wproj, bproj, ident, head_blocks)
    nested_width_attention_layer(nc, x3, out, q_w, q_b, k_w, k_b, v_w, v_b, o_w, o_b, norm_w, norm_b, ident)


def shape_constants():
    import numpy as np

    half, blocked = 8, -1e30
    inv_freq = (np.float32(1.0) / np.float32(10000.0) ** (np.arange(half, dtype=np.float32) / np.float32(half))).astype(np.float32)
    ang = np.arange(T, dtype=np.float32)[:, None] * inv_freq[None, :]
    i = np.arange(P)
    before = lambda key, query: np.where(key >= query, 0.0, blocked)
    own = lambda key, query: np.where(key <= query, 0.0, blocked)
    heads = np.zeros((P, P + 8), np.float32)
    heads[:, :P] = i[:, None] // 16 == i[None, :] // 16
    heads[:, P:] = i[:, None] // 16 == np.arange(8)[None, :]
    bf = mybir.dt.np(bf16)
    return {
        "cos": np.ascontiguousarray(np.tile(np.cos(ang).astype(np.float32).T, (16, 1))),
        "sin": np.ascontiguousarray(np.tile(np.sin(ang).astype(np.float32).T, (16, 1))),
        "mask": np.concatenate([before(i[None, :], i[:, None]), own(i[None, :], i[:, None])], 1).astype(bf),
        "maskT": np.concatenate([before(i[:, None], i[None, :]), own(i[:, None], i[None, :])], 1).astype(bf),
        "ident": np.eye(P, dtype=np.float32), "ident16": np.eye(P, dtype=np.float32).astype(bf),
        "tie": np.linspace(0.0, 1e-6, 16, dtype=np.float32), "heads": heads,
    }


def kernel(**inputs):
    import numpy as np
    import concourse.bacc as bacc
    from concourse.bass_utils import run_bass_kernel_spmd as run

    a = {k: np.asarray(v) for k, v in inputs.items()}
    c = shape_constants()
    order = np.arange(D).reshape(16, 2, 8).transpose(1, 0, 2).reshape(D)
    column = lambda v: v.reshape(-1, P).T
    wqkv = a["L1_attn_Wqkv"].T
    args = [
        a["L0_attn_x"], a["L0_attn_Wq"][order].T, a["L0_attn_Wk"][order].T, column(a["L0_attn_bq"][order]),
        column(a["L0_attn_bk"][order]), a["L0_attn_Wv"].T, a["L0_attn_bv"], a["L0_attn_Wo"].T, a["L0_attn_bo"],
        c["cos"], c["sin"], c["mask"], c["maskT"], c["ident"], c["ident16"],
        a["L0_ffn_controller"].reshape(D, 64), a["L0_ffn_f1"].reshape(D, 64, 64), a["L0_ffn_f2"].reshape(64, 64, D),
        column(a["L0_ffn_bias"]), c["tie"],
        wqkv, a["L1_attn_Wproj"].T, a["L1_attn_bproj"], c["heads"],
        a["L1_ffn_q_w"].T, column(a["L1_ffn_q_b"]), a["L1_ffn_k_w"].T, column(a["L1_ffn_k_b"]), a["L1_ffn_v_w"].T,
        a["L1_ffn_v_b"], a["L1_ffn_o_w"].T, a["L1_ffn_o_b"], a["L1_ffn_norm_w"], a["L1_ffn_norm_b"],
    ]
    nc = bacc.Bacc("TRN2", target_bir_lowering=False, num_devices=1)
    arrays, aps = {}, []
    for i, v in enumerate(args):
        v = np.ascontiguousarray(v)
        arrays[f"in_{i}_dram"] = v
        aps.append(nc.dram_tensor(f"in_{i}_dram", v.shape, mybir.dt.from_np(v.dtype), kind="ExternalInput").ap())
    out = nc.dram_tensor("out_dram", (NSEQ, T, D), f32, kind="ExternalOutput").ap()
    four_layers(nc, *aps, out)
    r = run(nc, [arrays], core_ids=[0])
    return r.results[0]["out_dram"]
```

```python
from contextlib import ExitStack

import concourse.bass as bass
from concourse import mybir

f32 = mybir.dt.float32
f32r = mybir.dt.float32r
bf16 = mybir.dt.bfloat16
ACT = mybir.ActivationFunctionType
ALU = mybir.AluOpType
AX = mybir.AxisListType.X

P = 128
NSEQ, T, D = 8, 1024, 256
NT = T // P
LN_EPS = 1e-5


def allocators(nc, ctx, layer):
    def sb(name, shape, dtype=f32):
        return ctx.enter_context(nc.sbuf_tensor(f"{layer}_{name}", shape, dtype))

    def ps(name, shape, dtype=f32):
        return ctx.enter_context(nc.psum_tensor(f"{layer}_{name}", shape, dtype))

    def sem(name):
        return ctx.enter_context(nc.semaphore(f"{layer}_{name}"))

    return sb, ps, sem


def tokens(dram, b):
    return dram[bass.ds(b, 1), :, :].rearrange("o (t p) d -> p (o t) d", p=P)


def alone(eng):
    eng.nop(nofuse=True)


def wait_alone(eng, sem, value):
    eng.wait_ge(sem, value)
    alone(eng)


def words(ap):
    return ap.bitcast(f32)


def on_all_partitions(row, n):
    return row[0:n].partition_broadcast(P)


def each_tile(v, n=NT):
    return v[:, :].unsqueeze(1).broadcast_to([P, n, D])


class Signal:

    def __init__(self, sem, per, step=1):
        self.sem, self.per, self.step = sem, per, step

    def start(self, eng):
        eng.sem_inc(self.sem, 2 * self.per * self.step)

    def by(self, instruction):
        instruction.then_inc(self.sem, self.step)

    def wait(self, eng, block, n=None):
        eng.wait_ge(self.sem, block * (self.per * self.step) + (2 * self.per + (self.per if n is None else n)) * self.step)


class Ring:

    def __init__(self, plan, n, emptied=None):
        self.at = {key: i for i, key in enumerate(plan)}
        self.plan, self.n, self.emptied = plan, n, emptied
        assert len(self.at) == len(plan)

    def slot(self, key):
        return self.at[key] % self.n

    def count(self, b, key):
        return b * len(self.plan) + self.at[key] + 1

    def before(self, key):
        i = self.at[key] - self.n
        return self.plan[i] if i >= 0 else None

    def wait_free(self, pe, b, key):
        old = self.before(key)
        if old is not None:
            for sem, per_sequence, position in self.emptied(old):
                pe.wait_ge(sem, b * per_sequence + position)


class LayerNorm:

    def __init__(self, sb, sem, name, setup, uses, tiles=NT):
        self.setup, self.uses, self.tiles = setup, uses, tiles
        self.stats = sb(f"{name}_stats", [P, tiles, 6])
        self.mv = sb(f"{name}_mv", [P, tiles, 2])
        self.rstd = sb(f"{name}_rstd", [P, tiles])
        self.half = sb(f"{name}_half", [P, tiles])
        self.summed = sem(f"{name}_summed")
        self.aggregated = sem(f"{name}_aggregated")
        self.var_ready = sem(f"{name}_var_ready")
        self.rstd_ready = sem(f"{name}_rstd_ready")
        self.normed = sem(f"{name}_normed")

    def count(self, b, use):
        return b * self.uses + use + 1

    def statistics(self, dve, x, b, use):
        n = self.count(b, use)
        for t in range(self.tiles):
            dve.bn_stats(self.stats[:, t, :], x[:, t, :]).then_inc(self.summed, 1)
        wait_alone(dve, self.summed, n * self.tiles)
        for t in range(self.tiles):
            dve.bn_aggr(self.mv[:, t, :], self.stats[:, t, :]).then_inc(self.aggregated, 1)
        dve.wait_ge(self.aggregated, n * self.tiles)
        dve.tensor_scalar(self.mv[:, :, 1], self.mv[:, :, 1], LN_EPS, None, ALU.add).then_inc(self.var_ready, 1)

    def reciprocal_root(self, pool, b, use):
        pool.wait_ge(self.var_ready, self.count(b, use))
        pool.tensor_tensor(self.rstd[:, :], self.mv[:, :, 1], self.half[:, :], ALU.pow).then_inc(self.rstd_ready, 1)

    def normalise(self, eng, out, x, b, use):
        wait_alone(eng, self.rstd_ready, self.count(b, use))
        for t in range(self.tiles):
            eng.tensor_scalar(out[:, t, :], x[:, t, :], self.mv[:, t, 0:1], self.rstd[:, t:t + 1],
                              ALU.subtract, ALU.mult).then_inc(self.normed, 1)

    def done(self, b, use):
        return self.count(b, use) * self.tiles



def window_attention_layer(nc, x_in, y_out, wq_in, wk_in, bq_in, bk_in, wvT, bv_in, woT, bo_in, cos_in, sin_in,
                           mask_in, maskT_in, ident_in, ident16_in, scratch):
    H, DH = 16, 16
    BT = 4
    BW = BT * P
    HG = 4
    NHG = H // HG
    HR = DH // 2
    SCALE = float(DH) ** -0.5
    CH = D // P
    SHIFT_ROW = 96

    front_plan = ["xT", "q", "k", "v"]

    def nat(t):
        return [("nat", NHG * t + g) for g in range(NHG)] + [("maxT", t)]

    def tr(t):
        return [("tr", NHG * t + g) for g in range(NHG)]

    steps = [nat(0), nat(1), "xT", tr(0), nat(2), [("pv", 0)], tr(1), "q", nat(3), [("back", 0), ("pv", 1)], tr(2), "k",
             [("back", 1), ("pv", 2)], tr(3), "v", [("back", 2), ("pv", 3), ("back", 3), ("aoT", 0), ("proj", 0)]]
    att_plan = [key for s in steps if not isinstance(s, str) for key in s if key[0] != "pv"]

    with ExitStack() as ctx:
        sb, ps, sem = allocators(nc, ctx, "l0a")
        consts = sem("consts"); setup = sem("setup")
        ident = sb("ident", [P, P]); ident16 = sb("ident16", [P, P], bf16)
        mask = sb("mask", [P, 2, P], bf16)
        maskT = sb("maskT", [P, 2, P], bf16)
        wq = sb("wq", [P, CH, D]); wk = sb("wk", [P, CH, D]); wv = sb("wv", [P, CH, D]); wo = sb("wo", [P, CH, D])
        bq = sb("bq", [P, 2]); bk = sb("bk", [P, 2]); bv = sb("bv", [P, D]); bo = sb("bo", [P, D])
        cos = sb("cos", [P, T]); sin = sb("sin", [P, T])
        x = sb("x", [P, 2, BT, D])
        xT = sb("xT", [P, CH, BW])
        turned = sb("turned", [P, 4, BW])
        rot = turned[:, 0::2, :]
        hi = sb("hi", [P, 2, BW], f32r); lo = sb("lo", [P, 2, BW], f32r)
        Qs = sb("Qs", [P, 2, H, BW], f32r)
        Ks = sb("Ks", [P, 2, H // 2, P + BW], f32r)
        V = sb("V", [P, 2, BT + 1, H, 2 * DH])
        probs = sb("probs", [P, H, 2, P])
        oT = sb("oT", [P, 4, P])
        recip = sb("recip", [P, BT, H])
        ao = sb("ao", [P, BT, D]); aoT = sb("aoT", [P, CH, BW])
        rowmax = sb("rowmax", [P, BT, H])
        maxT = sb("maxT", [H, 2, P], f32r)
        ln = LayerNorm(sb, sem, "ln", setup, 1, BT)
        front_slot = ps("front", [P, 1024])
        slots = [ps(f"slot{i}", [P, 1024]) for i in range(2)]
        O = [ps(f"O{i}", [P, 4, P]) for i in range(2)]


        def signal(name, per, step=1):
            return Signal(sem(name), per, step)

        x_loaded = signal("x_loaded", 1, 16); stored = signal("stored", 1, 16)
        front = signal("front", 4); filled = signal("filled", len(att_plan))
        xT_ready = signal("xT_ready", 1); biased = signal("biased", 1)
        turned_ready = signal("turned_ready", 8); rot_ready = signal("rot_ready", 4)
        hi_ready = signal("hi_ready", 2); lo_ready = signal("lo_ready", 2)
        v_ready = signal("v_ready", 1); v_carried = signal("v_carried", 1)
        bounced = {w: signal(f"bounced_{w}", 4, 16) for w in "qk"}
        stacked = {w: signal(f"stacked_{w}", 6, 16) for w in "qk"}
        max_ready = signal("max_ready", BT * NHG); maxT_ready = signal("maxT_ready", BT)
        placed = [signal(f"placed{t}", BT // 2, 16) for t in range(2)]
        exp_ready = signal("exp_ready", BT * NHG); pv_done = signal("pv_done", BT)
        oT_ready = signal("oT_ready", BT); recip_ready = signal("recip_ready", BT); ao_ready = signal("ao_ready", BT)
        aoT_ready = signal("aoT_ready", 1); summed = signal("summed", 1)

        at = {key: i for i, key in enumerate(att_plan)}

        def slot(key):
            return slots[at[key] % 2]

        assert len(att_plan) % 2 == 0

        def arrived(eng, B, key):
            filled.wait(eng, B, at[key] + 1)
            return slot(key)

        def use(pe, B, key):
            i = at[key] - 2
            if i < 0:
                i, B = i + len(att_plan), B - 1
            kind, n = att_plan[i]
            read, count = {"nat": (max_ready, n + 1), "maxT": (maxT_ready, n + 1), "tr": (exp_ready, n + 1),
                           "back": (ao_ready, n + 1), "aoT": (aoT_ready, 1), "proj": (summed, 1)}[kind]
            read.wait(pe, B, count)
            return slot(key)

        def run(front_piece, attention_piece, order=steps):
            def body(b, last):
                for n in range(2):
                    B = 2 * b + n
                    for step in steps:
                        if isinstance(step, str):
                            if not (last and n == 1):
                                front_piece(step, B + 1, b + n, 1 - n)
                        else:
                            for kind, i in step:
                                attention_piece(kind, i, B, b, n)
            for piece in front_plan:
                front_piece(piece, 0, 0, 0)
            return body

        def loop(eng, body):
            with eng.Fori(0, NSEQ - 1) as b:
                body(b, False)
            body(NSEQ - 1, True)

        NCONST = 14
        NSETUP = 5
        block = ctx.enter_context(nc.Block())

        @block.sync
        def _(sp):
            for dst, src in ((ident, ident_in), (ident16, ident16_in), (cos, cos_in), (sin, sin_in), (bq, bq_in), (bk, bk_in)):
                sp.dma_start(dst[:, :], src).then_inc(consts, 16)
            for dst, src in ((mask, mask_in), (maskT, maskT_in)):
                sp.dma_start(dst[:, :, :], src.rearrange("p (a n) -> p a n", a=2)).then_inc(consts, 16)
            for dst, src in ((wq, wq_in), (wk, wk_in), (wv, wvT), (wo, woT)):
                sp.dma_start(dst[:, :, :], src.rearrange("(c p) n -> p c n", p=P)).then_inc(consts, 16)
            for dst, src in ((bv, bv_in), (bo, bo_in)):
                sp.dma_start(dst[:, :], on_all_partitions(src, D)).then_inc(consts, 16)
            for s in (x_loaded, stored, *bounced.values(), *stacked.values(), *placed):
                s.start(sp)
            sp.wait_ge(setup, NSETUP)

            def front_piece(piece, B, b, n):
                tok = BW * n
                if piece == "xT":
                    stored.wait(sp, B - 2)
                    alone(sp)
                    x_loaded.by(sp.dma_start(x[:, n, :, :], tokens(x_in, b)[:, BT * n:BT * n + BT, :]))
                if piece in ("q", "k"):
                    w = piece
                    i = "qk".index(w)
                    lo_ready.wait(sp, B, i + 1)
                    for part, source in enumerate((hi, lo)):
                        for r in range(2):
                            rows = scratch[i, part, :, HR * r:HR * r + HR, tok:tok + BW]
                            bounced[w].by(sp.dma_start(rows, words(source[:, r, :])))
                    bounced[w].wait(sp, B)
                    pv_done.wait(sp, B - 2)
                    for parity in range(2):
                        for term, part in enumerate((0, 1, 0) if w == "q" else (0, 0, 1)):
                            first = 3 * DH * parity + DH * term
                            if w == "q":
                                src = scratch[i, part, parity::2, :, tok:tok + BW]
                                dst = Qs[first:first + DH, n, parity::2, :]
                            else:
                                skip = 0 if n else P
                                src = scratch[i, part, parity::2, :, tok - P + skip:tok + BW]
                                dst = Ks[first:first + DH, n, :, skip:]
                            stacked[w].by(sp.dma_start(words(dst), src.rearrange("h d t -> d h t")))

            def attention_piece(kind, i, B, b, n):
                if kind == "maxT":
                    maxT_ready.wait(sp, B, i + 1)
                    placed[i % 2].by(sp.dma_start(words(Qs[SHIFT_ROW:SHIFT_ROW + 1, n, :, P * i:P * i + P]),
                                              words(maxT[:, i % 2, :])))
                if kind == "proj":
                    wait_alone(sp, ln.normed, (B + 1) * BT)
                    stored.by(sp.dma_start(tokens(y_out, b)[:, BT * n:BT * n + BT, :], x[:, n, :, :]))

            loop(sp, run(front_piece, attention_piece))
            stored.wait(sp, 2 * NSEQ - 1)

        @block.gpsimd
        def _(pool):
            for s in (biased, rot_ready, lo_ready):
                s.start(pool)
            pool.wait_ge(setup, NSETUP)
            pool.wait_ge(consts, 16 * NCONST)

            def front_piece(piece, B, b, n):
                if piece == "xT":
                    front.wait(pool, B, 1)
                    biased.by(pool.tensor_tensor(x[:, n, :, :], x[:, n, :, :], each_tile(bo, BT), ALU.add))
                if piece in ("q", "k"):
                    i = "qk".index(piece)
                    turned_ready.wait(pool, B, 4 * i + 2)
                    rot_ready.by(pool.tensor_tensor(rot[:, 0, :], turned[:, 0, :], turned[:, 1, :], ALU.subtract))
                    turned_ready.wait(pool, B, 4 * i + 4)
                    rot_ready.by(pool.tensor_tensor(rot[:, 1, :], turned[:, 2, :], turned[:, 3, :], ALU.add))
                    hi_ready.wait(pool, B, i + 1)
                    rot_ready.wait(pool, B, 2 * i + 2)
                    other = bounced["k" if i == 0 else "q"]
                    other.wait(pool, B - 1 if i == 0 else B)
                    lo_ready.by(pool.tensor_tensor(lo[:, :, :], rot[:, :, :], hi[:, :, :].bitcast(f32), ALU.subtract))

            def attention_piece(kind, i, B, b, n):
                if kind == "proj":
                    ln.reciprocal_root(pool, B, 0)

            loop(pool, run(front_piece, attention_piece))

        def back_filled(eng, B, t):
            if t < 0:
                B, t = B - 1, t + BT
            filled.wait(eng, B, at[("back", t)] + 1)

        @block.scalar
        def _(act):
            for s in (xT_ready, hi_ready, v_carried, exp_ready, oT_ready, aoT_ready):
                s.start(act)
            act.wait_ge(setup, NSETUP)
            act.wait_ge(consts, 16 * NCONST)

            def front_piece(piece, B, b, n):
                if piece == "xT":
                    front.wait(act, B, 1)
                    xT_ready.by(act.copy(xT[:, :, :], front_slot[:, :].rearrange("p (c n) -> p c n", c=CH)))
                if piece in ("q", "k"):
                    i = "qk".index(piece)
                    rot_ready.wait(act, B, 2 * i + 2)
                    other = bounced["k" if i == 0 else "q"]
                    other.wait(act, B - 1 if i == 0 else B)
                    hi_ready.by(act.copy(hi[:, :, :], rot[:, :, :]))
                if piece == "v":
                    v_ready.wait(act, B - 1)
                    pv_done.wait(act, B - 2)
                    if n:
                        v_carried.by(act.copy(V[:, 1, 0, :, :], V[:, 0, BT, :, :]))
                    else:
                        v_carried.by(act.copy(V[:, 0, 0, :, :], V[:, 1, BT, :, :]))

            def attention_piece(kind, i, B, b, n):
                if kind == "tr":
                    t, g = i // NHG, i % NHG
                    s = arrived(act, B, (kind, i))[:, :].rearrange("p (h a q) -> p h a q", h=HG, a=2)
                    pv_done.wait(act, B if t else B - 1, t if t else BT)
                    first = 0 if n or t else 1
                    exp_ready.by(act.activation(probs[:, HG * g:HG * g + HG, first:2, :], s[:, :, first:2, :],
                                                ACT.Exp, scale=SCALE))
                if kind == "pv":
                    pv_done.wait(act, B, i + 1)
                    back_filled(act, B, i - 1)
                    oT_ready.by(act.copy(oT[:, :, :], O[i % 2][:, :, :]))
                if kind == "aoT":
                    s = arrived(act, B, (kind, i))
                    aoT_ready.by(act.copy(aoT[:, :, :], s[:, :].rearrange("p (c n) -> p c n", c=CH)))

            loop(act, run(front_piece, attention_piece))

        @block.vector
        def _(dve):
            dve.memset(Qs[:, :, :, :].bitcast(f32), 0.0).then_inc(setup, 1)
            dve.memset(Ks[SHIFT_ROW:P, :, :, :].bitcast(f32), -1.0).then_inc(setup, 1)
            dve.memset(V[:, :, :, :, :], 1.0).then_inc(setup, 1)
            dve.memset(ln.half[:, :], -0.5).then_inc(setup, 1)
            dve.memset(maxT[:, :, :].bitcast(f32), 0.0).then_inc(setup, 1)
            for s in (turned_ready, v_ready, max_ready, maxT_ready, recip_ready, ao_ready, summed):
                s.start(dve)
            dve.wait_ge(consts, 16 * NCONST)
            dve.wait_ge(setup, NSETUP)

            def front_piece(piece, B, b, n):
                cols = slice(BW * n, BW * n + BW)
                if piece in ("q", "k"):
                    i = "qk".index(piece)
                    bias = (bq, bk)[i]
                    front.wait(dve, B, 2 + i)
                    hi_ready.wait(dve, B if i else B - 1, 1 if i else 2)
                    lo_ready.wait(dve, B if i else B - 1, 1 if i else 2)
                    for j, (r, table) in enumerate(((0, cos), (1, sin), (0, sin), (1, cos))):
                        turned_ready.by(dve.scalar_tensor_tensor(turned[:, j, :], front_slot[:, BW * r:BW * r + BW],
                                                                 bias[:, r:r + 1], table[:, cols], ALU.add, ALU.mult))
                if piece == "v":
                    front.wait(dve, B, 4)
                    pv_done.wait(dve, B - 2)
                    v_carried.wait(dve, B - 1)
                    for t in range(BT):
                        last = dve.tensor_tensor(V[:, n, t + 1, :, 0:DH],
                                                 front_slot[:, D * t:D * t + D].rearrange("p (h d) -> p h d", h=H),
                                                 bv[:, :].rearrange("p (h d) -> p h d", h=H), ALU.add)
                    v_ready.by(last)

            def attention_piece(kind, i, B, b, n):
                if kind == "nat":
                    t, g = i // NHG, i % NHG
                    s = arrived(dve, B, (kind, i))[:, :].rearrange("p (h k) -> p h k", h=HG)
                    first = 0 if n or t else P
                    max_ready.by(dve.reduce_max(rowmax[:, t, HG * g:HG * g + HG], s[:, :, first:2 * P], AX))
                if kind == "maxT":
                    s = arrived(dve, B, (kind, i))
                    placed[i % 2].wait(dve, B - (i < 2), (i - 2) % BT // 2 + 1)
                    maxT_ready.by(dve.tensor_copy(maxT[:, i % 2, :], s[0:H, 0:P]))
                if kind == "back":
                    s = arrived(dve, B, (kind, i))[:, 0:512].rearrange("p (h d) -> p h d", h=H)
                    recip_ready.by(dve.reciprocal(recip[:, i, :], s[:, :, DH]))
                    recip_ready.wait(dve, B, i + 1)
                    ao_ready.by(dve.tensor_tensor(ao[:, i, :].rearrange("p (h d) -> p h d", h=H), s[:, :, 0:DH],
                                                  recip[:, i, :].unsqueeze(2).broadcast_to([P, H, DH]), ALU.mult))
                if kind == "proj":
                    s = arrived(dve, B, (kind, i))
                    biased.wait(dve, B)
                    summed.by(dve.tensor_tensor(x[:, n, :, :], s[:, :].rearrange("p (t n) -> p t n", t=BT), x[:, n, :, :], ALU.add))
                    summed.wait(dve, B)
                    ln.statistics(dve, x[:, n, :, :], B, 0)
                    ln.normalise(dve, x[:, n, :, :], x[:, n, :, :], B, 0)

            loop(dve, run(front_piece, attention_piece))

        @block.tensor
        def _(pe):
            mm = nc.tensor.matmul
            for s in (front, filled, pv_done):
                s.start(pe)
            pe.wait_ge(setup, NSETUP)
            pe.wait_ge(consts, 16 * NCONST)

            def front_piece(piece, B, b, n):
                if piece == "xT":
                    x_loaded.wait(pe, B)
                    v_ready.wait(pe, B - 1)
                    for c in range(CH):
                        for t in range(BT):
                            last = nc.tensor.transpose(front_slot[:, BW * c + P * t:BW * c + P * t + P],
                                                       x[:, n, t, P * c:P * c + P], ident[:, :])
                if piece in ("q", "k"):
                    w = wq if piece == "q" else wk
                    if piece == "q":
                        xT_ready.wait(pe, B)
                    else:
                        turned_ready.wait(pe, B, 4)
                    for r in range(2):
                        for c in range(CH):
                            last = mm(front_slot[:, BW * r:BW * r + BW], w[:, c, P * r:P * r + P], xT[:, c, :],
                                      start=c == 0, stop=c == CH - 1)
                if piece == "v":
                    turned_ready.wait(pe, B, 8)
                    for t in range(BT):
                        for c in range(CH):
                            last = mm(front_slot[:, D * t:D * t + D], xT[:, c, P * t:P * t + P], wv[:, c, :],
                                      start=c == 0, stop=c == CH - 1)
                front.by(last)

            def attention_piece(kind, i, B, b, n):
                t, g = i // NHG, i % NHG
                if kind == "nat":
                    if i == 0:
                        stacked["q"].wait(pe, B)
                        stacked["k"].wait(pe, B)
                    s = use(pe, B, (kind, i))
                    first = 0 if n or t else 1
                    for k in range(HG // 2):
                        o = s[:, 512 * k:512 * k + 512].rearrange("p (h a n) -> p h a n", h=2, a=2)[:, :, first:2, :]
                        mm(o, ident16[:, :], mask[:, first:2, :].unsqueeze(1).broadcast_to([P, 2, 2 - first, P]),
                           start=True, stop=False, skip_group_check=True)
                        for m in range(2):
                            h = HG * g + 2 * k + m
                            last = mm(o[:, m, :, :].rearrange("p a n -> p (a n)"), Qs[0:96, n, h, P * t:P * t + P],
                                      Ks[0:96, n, h // 2, P * (t + first):P * (t + 2)], start=False, stop=True,
                                      skip_group_check=True)
                    filled.by(last)
                if kind == "maxT":
                    s = use(pe, B, (kind, i))
                    max_ready.wait(pe, B, NHG * i + NHG)
                    filled.by(nc.tensor.transpose(s[0:H, 0:P], rowmax[:, i, :], ident[:, :]))
                if kind == "tr":
                    if g == 0:
                        placed[t % 2].wait(pe, B, t // 2 + 1)
                    s = use(pe, B, (kind, i))
                    first = 0 if n or t else 1
                    for k in range(HG // 2):
                        o = s[:, 512 * k:512 * k + 512].rearrange("p (h a n) -> p h a n", h=2, a=2)
                        mm(o[:, :, first:2, :], ident16[:, :],
                           maskT[:, first:2, :].unsqueeze(1).broadcast_to([P, 2, 2 - first, P]),
                           start=True, stop=False, skip_group_check=True)
                        for m in range(2):
                            h = HG * g + 2 * k + m
                            for a in range(first, 2):
                                last = mm(o[:, m, a, :], Ks[:, n, h // 2, P * (t + a):P * (t + a + 1)],
                                          Qs[:, n, h, P * t:P * t + P], start=False, stop=True, skip_group_check=True)
                    filled.by(last)
                if kind == "pv":
                    exp_ready.wait(pe, B, NHG * i + NHG)
                    if i == 0:
                        v_ready.wait(pe, B)
                        v_carried.wait(pe, B)
                    oT_ready.wait(pe, B if i >= 2 else B - 1, (i - 2) % BT + 1)
                    first = 0 if n or i else 1
                    for gg in range(NHG):
                        for a in range(first, 2):
                            for j in range(HG):
                                h = HG * gg + j
                                last = mm(O[i % 2][32 * j:32 * j + 32, gg, :], V[:, n, i + a, h, :], probs[:, h, a, :],
                                          start=a == first, stop=a == 1, tile_position=(0, 32 * j))
                    pv_done.by(last)
                if kind == "back":
                    oT_ready.wait(pe, B, i + 1)
                    s = use(pe, B, (kind, i))
                    for gg in range(NHG):
                        last = nc.tensor.transpose(s[:, P * gg:P * gg + P], oT[:, gg, :], ident[:, :])
                    filled.by(last)
                if kind == "aoT":
                    ao_ready.wait(pe, B)
                    s = use(pe, B, (kind, i))
                    for c in range(CH):
                        for tt in range(BT):
                            last = nc.tensor.transpose(s[:, BW * c + P * tt:BW * c + P * tt + P], ao[:, tt, P * c:P * c + P],
                                                       ident[:, :])
                    filled.by(last)
                if kind == "proj":
                    aoT_ready.wait(pe, B)
                    s = use(pe, B, (kind, i))
                    for tt in range(BT):
                        for c in range(CH):
                            last = mm(s[:, D * tt:D * tt + D], aoT[:, c, P * tt:P * tt + P], wo[:, c, :],
                                      start=c == 0, stop=c == CH - 1)
                    filled.by(last)

            loop(pe, run(front_piece, attention_piece))


def token_choice_layer(nc, x_in, y_out, controller, f1_in, f2_in, f1_bias, tie_in, ident_in, scratch):
    G = 16
    E, F = 64, 64
    EH = E // 2
    TT = 2 * NT
    NG = TT * P // G
    J = P // EH
    NQ = NG // J
    CH = D // P
    TP = TT // 2
    PAIRS = EH // 2
    HB = 8
    IN = PAIRS // 2
    NC = TT // 4

    plan = [("xT", n) for n in range(2 * CH)] + [("logits", 0)]

    def selection(half):
        out = [("pT", half * TP)]
        for tp in range(TP):
            if tp + 1 < TP:
                out.append(("pT", half * TP + tp + 1))
            out.append(("sel", half * TP + tp))
        return out

    def experts(half):
        h, o = [("h", 2 * half + n) for n in range(2)], [("inter", IN * half + n) for n in range(IN)]
        return [h[0], o[0], o[1], h[1]] + o[2:]

    def combination(half):
        return [("out", NC * half + n) for n in range(NC)]

    plan += selection(0) + experts(0) + selection(1) + combination(0) + experts(1) + combination(1)

    with ExitStack() as ctx:
        sb, ps, sem = allocators(nc, ctx, "l0f")
        consts = sem("consts"); setup = sem("setup")
        ident = sb("ident", [P, P])
        ctrl = sb("ctrl", [P, CH, E])
        f1 = sb("f1", [P, CH, E, F])
        f2 = sb("f2", [P, PAIRS, D])
        b1 = sb("b1", [P, E // 2])
        tie = sb("tie", [P, G])
        sel = sb("sel", [P, CH, EH, NG])
        wide = sb("wide", [P, 2 * TT, D])
        x, inter2, y = wide[:, 0:TT, :], wide, wide[:, TT:2 * TT, :]
        hi = sb("hi", [P, TT, D], f32r); lo = sb("lo", [P, TT, D], f32r)
        turned = sb("turned", [P, TT * D])
        xT = turned[:, :].rearrange("p (c t) -> p c t", c=CH)
        total = turned[:, :].rearrange("p (t d) -> p t d", d=D)
        hidden = sb("hidden", [P, 8, 2, NG])
        inter = sb("inter", [P, 2, 4, D])
        choice = sb("choice", [P, 2, NQ, G])
        spread = sb("spread", [P, 2, NQ, J, G])
        chosen = sb("chosen", [P, 2, 2, 2, P], f32r)
        best = sb("best", [P, 2, NQ])
        ln = LayerNorm(sb, sem, "ln", setup, 1, TT)
        slots = [ps(f"slot{i}", [P, 1024]) for i in range(4)]

        f2_loaded = sem("f2_loaded")
        x_loaded = sem("x_loaded"); x_again = sem("x_again"); stored = sem("stored")
        filled = sem("filled"); xT_ready = sem("xT_ready"); hi_ready = sem("hi_ready"); lo_ready = sem("lo_ready")
        rated = sem("rated"); best_ready = sem("best_ready"); choice_ready = sem("choice_ready"); spread_ready = sem("spread_ready")
        chosen_ready = sem("chosen_ready"); sel_even = sem("sel_even"); sel_odd = sem("sel_odd")
        hidden_even = sem("hidden_even"); hidden_odd = sem("hidden_odd")
        inter_even = sem("inter_even"); inter_odd = sem("inter_odd")
        left = [[sem(f"left{h}{i}") for i in range(2)] for h in range(2)]
        back = [[sem(f"back{h}{i}") for i in range(NC)] for h in range(2)]
        summed = sem("summed")

        def emptied(key):
            kind, i = key
            return {"xT": [(xT_ready, 2 * CH, i + 1)], "logits": [(rated, 1, 1)],
                    "pT": [(chosen_ready, 4 * TP, 2 * i + 2)],
                    "sel": [(sel_even, 2 * TP, i + 1), (sel_odd, 2 * TP, i + 1)],
                    "h": [(hidden_even, 2 * PAIRS, HB * (i + 1)), (hidden_odd, 2 * PAIRS, HB * (i + 1))],
                    "inter": [(inter_even, 2 * IN, i + 1), (inter_odd, 2 * IN, i + 1)],
                    "out": [(summed, 2 * NC, i + 1)]}[kind]

        ring = Ring(plan, 4, emptied)

        def arrived(eng, b, key):
            eng.wait_ge(filled, ring.count(b, key))
            return slots[ring.slot(key)]

        NCONST = 5 + CH - 1
        NSETUP = 4
        block = ctx.enter_context(nc.Block())
        f2_rows = f2_in.rearrange("(p e) f d -> (e f) p d", e=2)

        def hidden_free(eng, b, p):
            if p >= 8:
                eng.wait_ge(filled, ring.count(b, ("inter", (p - 8) // 2)))

        def inter_free(eng, b, i):
            if i >= 2:
                half, n = (i - 2) // IN, (i - 2) % IN
                eng.wait_ge(left[half][n % 2], 16 * ((IN // 2) * b + n // 2 + 1))

        @block.sync
        def _(sp):
            sp.dma_start(ident[:, :], ident_in).then_inc(consts, 16)
            sp.dma_start(ctrl[:, :, :], controller.rearrange("(c p) e -> p c e", p=P)).then_inc(consts, 16)
            sp.dma_start(b1[:, :], f1_bias).then_inc(consts, 16)
            sp.dma_start(tie[:, :], on_all_partitions(tie_in, G)).then_inc(consts, 16)
            for c in range(CH):
                sp.dma_start(f1[:, c, :, :], f1_in.rearrange("(c p) e f -> p c e f", p=P)[:, c, :, :]).then_inc(consts, 16)

            with sp.Fori(0, NSEQ // 2) as b:
                for s in range(2):
                    sp.dma_start(wide[:, NT * s:NT * s + NT, :], tokens(x_in, 2 * b + s)).then_inc(x_loaded, 16)
                for half in range(2):
                    if half:
                        sp.wait_ge(filled, ring.count(b, ("inter", IN - 1)))
                    sp.dma_start(f2[:, :, :], f2_rows[:, PAIRS * half:PAIRS * half + PAIRS, :]).then_inc(f2_loaded, 16)
                    if half == 0:
                        wait_alone(sp, rated, b + 1)
                        for s in range(2):
                            sp.dma_start(total[:, NT * s:NT * s + NT, :], tokens(x_in, 2 * b + s)).then_inc(x_again, 16)
                    for n in range(IN):
                        i = IN * half + n
                        sp.wait_ge(inter_even, 2 * IN * b + i + 1)
                        sp.wait_ge(inter_odd, 2 * IN * b + i + 1)
                        sp.dma_start(scratch[half, :, 4 * n:4 * n + 4, :], inter[:, i % 2, :, :]).then_inc(left[half][i % 2], 16)
                    for i in range(2):
                        wait_alone(sp, left[half][i], 16 * (IN // 2) * (b + 1))
                    if half:
                        sp.wait_ge(filled, ring.count(b, ("out", NC - 1)))
                    rows = scratch[half, :, :, :].rearrange("(q j) e d -> (j e) q d", j=J)
                    for n in range(NC):
                        q = slice(NQ // NC * n, NQ // NC * (n + 1))
                        sp.dma_start(inter2[:, q, :], rows[:, q, :]).then_inc(back[half][n], 16)
                wait_alone(sp, ln.normed, ln.done(b, 0))
                for s in range(2):
                    sp.dma_start(tokens(y_out, 2 * b + s), wide[:, TT + NT * s:TT + NT * s + NT, :]).then_inc(stored, 16)
            sp.wait_ge(stored, 16 * NSEQ)

        @block.gpsimd
        def _(pool):
            pool.wait_ge(setup, NSETUP)
            pool.wait_ge(consts, 16 * NCONST)
            with pool.Fori(0, NSEQ // 2) as b:
                for n in range(2):
                    pool.wait_ge(hi_ready, 2 * b + n + 1)
                    part = slice(NT * n, NT * n + NT)
                    pool.tensor_tensor(lo[:, part, :], x[:, part, :], hi[:, part, :].bitcast(f32), ALU.subtract).then_inc(lo_ready, 1)
                pool.wait_ge(choice_ready, b + 1)
                wait_alone(pool, lo_ready, 2 * b + 2)
                for half in range(2):
                    for j in range(J):
                        if half or j:
                            wait_alone(pool, spread_ready, 2 * J * b + J * half + j)
                        rows = slice(EH * j, EH * j + EH)
                        pool.tensor_copy(spread[rows, half, :, j, :], choice[rows, half, :, :]).then_inc(spread_ready, 1)
                pool.wait_ge(spread_ready, 2 * J * (b + 1))
                ln.reciprocal_root(pool, b, 0)

        @block.scalar
        def _(act):
            act.wait_ge(setup, NSETUP)
            act.wait_ge(consts, 16 * NCONST)
            with act.Fori(0, NSEQ // 2) as b:
                act.wait_ge(x_loaded, 32 * b + 32)
                for n in range(2):
                    act.copy(hi[:, NT * n:NT * n + NT, :], x[:, NT * n:NT * n + NT, :]).then_inc(hi_ready, 1)
                for n in range(2 * CH):
                    c, s = n % CH, n // CH
                    act.copy(xT[:, c, T * s:T * s + T], arrived(act, b, ("xT", n))[:, :]).then_inc(xT_ready, 1)

                def take_choice(i):
                    if i % TP >= 2:
                        act.wait_ge(filled, ring.count(b, ("sel", i - 2)))
                    s = arrived(act, b, ("pT", i))[:, 0:2 * P].rearrange("p (t n) -> p t n", t=2)
                    for q in range(2):
                        rows = slice(64 * q, 64 * q + 64)
                        act.copy(chosen[rows, i % 2, :, q, :], s[rows, :, :]).then_inc(chosen_ready, 1)

                for half in range(2):
                    take_choice(half * TP)
                    for tp in range(TP):
                        i = half * TP + tp
                        if tp + 1 < TP:
                            take_choice(i + 1)
                        s = arrived(act, b, ("sel", i))[:, 0:512].rearrange("p (g e) -> p e g", e=EH)
                        act.copy(sel[:, 0, :, 16 * tp:16 * tp + 16], s).then_inc(sel_even, 1)
                    for key in experts(half):
                        s = arrived(act, b, key)
                        if key[0] == "h":
                            for n in range(HB):
                                p = HB * key[1] + n
                                hidden_free(act, b, p)
                                act.activation(hidden[0:64, p % 8, 0, :], s[0:64, NG * n:NG * n + NG], ACT.Relu,
                                               bias=b1[0:64, p:p + 1]).then_inc(hidden_even, 1)
                        else:
                            i = key[1]
                            inter_free(act, b, i)
                            act.copy(inter[:, i % 2, 0:2, :], s[:, 0:512].rearrange("p (e d) -> p e d", e=2)).then_inc(inter_even, 1)

        def combine(dve, b, half):
            if half == 0:
                dve.wait_ge(x_again, 32 * b + 32)
            else:
                dve.wait_ge(summed, 2 * NC * b + NC)
            for n in range(NC):
                s = arrived(dve, b, ("out", NC * half + n))[:, :].rearrange("p (t d) -> p t d", t=4)
                part = total[:, 4 * n:4 * n + 4, :]
                dve.tensor_tensor(part, s, part, ALU.add).then_inc(summed, 1)

        @block.vector
        def _(dve):
            dve.memset(spread[:, :, :, :, :], 0.0).then_inc(setup, 1)
            dve.memset(chosen[:, :, :, :, :].bitcast(f32), 0.0).then_inc(setup, 1)
            dve.memset(hidden[:, :, :, :], 0.0).then_inc(setup, 1)
            dve.memset(ln.half[:, :], -0.5).then_inc(setup, 1)
            dve.wait_ge(consts, 16 * NCONST)
            with dve.Fori(0, NSEQ // 2) as b:
                s = arrived(dve, b, ("logits", 0))[:, :].rearrange("p (h q t) -> p (h q) t", h=2, t=G)
                marks = choice[:, :, :, :].rearrange("p h q t -> p (h q) t")
                top = best[:, :, :].rearrange("p h q -> p (h q)")
                dve.tensor_tensor(marks, s, tie[:, :].unsqueeze(1).broadcast_to([P, 2 * NQ, G]), ALU.add).then_inc(rated, 1)
                dve.wait_ge(rated, b + 1)
                dve.reduce_max(top, marks, AX).then_inc(best_ready, 1)
                dve.wait_ge(best_ready, b + 1)
                dve.tensor_tensor(marks, marks, top.unsqueeze(2).broadcast_to([P, 2 * NQ, G]), ALU.is_equal)\
                    .then_inc(choice_ready, 1)
                for half in range(2):
                    for tp in range(TP):
                        i = half * TP + tp
                        s = arrived(dve, b, ("sel", i))[:, 512:1024].rearrange("p (g e) -> p e g", e=EH)
                        dve.tensor_copy(sel[:, 1, :, 16 * tp:16 * tp + 16], s).then_inc(sel_odd, 1)
                    if half:
                        combine(dve, b, 0)
                    for key in experts(half):
                        s = arrived(dve, b, key)
                        if key[0] == "h":
                            for n in range(HB):
                                p = HB * key[1] + n
                                hidden_free(dve, b, p)
                                dve.tensor_scalar(hidden[64:128, p % 8, 1, :], s[64:128, NG * n:NG * n + NG],
                                                  b1[64:128, p:p + 1], 0.0, ALU.add, ALU.max).then_inc(hidden_odd, 1)
                        else:
                            i = key[1]
                            inter_free(dve, b, i)
                            dve.tensor_copy(inter[:, i % 2, 2:4, :], s[:, 512:1024].rearrange("p (e d) -> p e d", e=2))\
                                .then_inc(inter_odd, 1)
                combine(dve, b, 1)
                dve.wait_ge(summed, 2 * NC * (b + 1))
                ln.statistics(dve, total, b, 0)
                ln.normalise(dve, y, total, b, 0)

        @block.tensor
        def _(pe):
            mm = nc.tensor.matmul
            pe.wait_ge(setup, NSETUP)
            pe.wait_ge(consts, 16 * NCONST)
            with pe.Fori(0, NSEQ // 2) as b:
                def use(key):
                    ring.wait_free(pe, b, key)
                    return slots[ring.slot(key)]

                def transpose_choice(i):
                    half, tp = i // TP, i % TP
                    s = use(("pT", i))
                    if tp == 0:
                        pe.wait_ge(spread_ready, 2 * J * b + J * (half + 1))
                    for t in range(2):
                        q = 2 * (2 * tp + t)
                        last = nc.tensor.transpose(s[:, P * t:P * t + P],
                                                   spread[:, half, q:q + 2, :, :].rearrange("p q j t -> p (q j t)"), ident[:, :])
                    last.then_inc(filled, 1)

                def select(i):
                    tp = i % TP
                    s = use(("sel", i))
                    pe.wait_ge(chosen_ready, 4 * TP * b + 2 * i + 2)
                    for c in range(CH):
                        for t in range(2):
                            o = s[:, 512 * c + 256 * t:512 * c + 256 * t + 256]
                            rhs = chosen[:, i % 2, t, :, :].rearrange("p q n -> p (q n)")
                            for part in (hi, lo):
                                last = mm(o, part[:, 2 * tp + t, P * c:P * c + P], rhs, start=part is hi, stop=part is lo)
                    last.then_inc(filled, 1)

                def expert(key):
                    s = use(key)
                    i = key[1]
                    if key[0] == "h":
                        if i % 2 == 0:
                            pe.wait_ge(sel_even, 2 * TP * b + TP * (i // 2 + 1))
                            pe.wait_ge(sel_odd, 2 * TP * b + TP * (i // 2 + 1))
                        for n in range(HB):
                            e0 = 2 * (HB * i + n)
                            for c in range(CH):
                                for k in range(2):
                                    last = mm(s[64 * k:64 * k + 64, NG * n:NG * n + NG], f1[:, c, e0 + k, :],
                                              sel[:, c, (e0 + k) % EH, :], start=c == 0, stop=c == CH - 1)
                    else:
                        for n in range(2):
                            p = 2 * i + n
                            pe.wait_ge(hidden_even, 2 * PAIRS * b + p + 1)
                            pe.wait_ge(hidden_odd, 2 * PAIRS * b + p + 1)
                            if i % IN == 0 and n == 0:
                                pe.wait_ge(f2_loaded, 16 * (2 * b + i // IN + 1))
                            for k in range(2):
                                last = mm(s[:, D * (2 * n + k):D * (2 * n + k + 1)], hidden[:, p % 8, k, :], f2[:, p % PAIRS, :],
                                          start=True, stop=True)
                    last.then_inc(filled, 1)

                def combine_on_pe(half):
                    for n in range(NC):
                        s = use(("out", NC * half + n))
                        pe.wait_ge(back[half][n], 16 * b + 16)
                        for t in range(4):
                            for k in range(2):
                                q = 2 * (4 * n + t) + k
                                last = mm(s[64 * k:64 * k + 64, D * t:D * t + D],
                                          spread[:, half, q, :, :].rearrange("p j t -> p (j t)"), inter2[:, q, :],
                                          start=True, stop=True)
                        last.then_inc(filled, 1)

                pe.wait_ge(x_loaded, 32 * b + 32)
                for n in range(2 * CH):
                    c, sq = n % CH, n // CH
                    s = use(("xT", n))
                    for t in range(NT):
                        last = nc.tensor.transpose(s[:, P * t:P * t + P], x[:, NT * sq + t, P * c:P * c + P], ident[:, :])
                    last.then_inc(filled, 1)
                s = use(("logits", 0))
                pe.wait_ge(xT_ready, 2 * CH * (b + 1))
                for half in range(2):
                    for c in range(CH):
                        by_quad = xT[:, c, :].rearrange("p (q j t) -> p q j t", j=J, t=G)
                        for j in range(J):
                            last = mm(s[EH * j:EH * j + EH, 512 * half:512 * half + 512], ctrl[:, c, EH * half:EH * half + EH],
                                      by_quad[:, :, j, :], start=c == 0, stop=c == CH - 1, tile_position=(0, EH * j))
                last.then_inc(filled, 1)
                for half in range(2):
                    if half == 0:
                        pe.wait_ge(lo_ready, 2 * b + 2)
                    for kind, i in selection(half):
                        (transpose_choice if kind == "pT" else select)(i)
                    if half:
                        combine_on_pe(0)
                    for key in experts(half):
                        expert(key)
                combine_on_pe(1)


def linear_attention_layer(nc, x_in, y_out, wqkvT, wprojT, bproj, ident_in, head_blocks_in):
    DH = 16
    HC = P // DH
    CH = D // P
    EPS = 1e-6
    W1 = P + HC
    PAIRS = NT // 2

    plan = [("xT", c) for c in range(CH)] + [("q", c) for c in range(CH)] + [("kv", g) for g in range(PAIRS)]
    plan += ["state"] + [("mix", g) for g in range(PAIRS)] + [("aoT", c) for c in range(CH)] + [("proj", g) for g in range(2)]

    with ExitStack() as ctx:
        sb, ps, sem = allocators(nc, ctx, "l1a")
        wqkv = sb("wqkv", [P, CH, 3 * D]); wproj = sb("wproj", [P, CH, D])
        bias = sb("bias", [P, D])
        ident = sb("ident", [P, P])
        head_blocks = sb("head_blocks", [P, W1])
        consts = sem("consts"); setup = sem("setup")

        class Stream:
            def __init__(self, s):
                def buf(name, shape):
                    return sb(f"{name}{s}", shape)

                def sig(name):
                    return sem(f"{name}{s}")

                self.s = s
                self.x = buf("x", [P, NT, D]); self.y = buf("y", [P, NT, D])
                self.xT = buf("xT", [P, CH, T])
                self.exp_q = buf("exp_q", [P, CH, T]); self.exp_k = buf("exp_k", [P, NT, D])
                self.qT = buf("qT", [P, CH, T]); self.k = buf("k", [P, NT, D])
                self.v1 = buf("v1", [P, NT, CH, P + 1])
                self.state = buf("state", [P, CH, W1])
                self.z = buf("z", [P, PAIRS, 2, CH, HC])
                self.ao = buf("ao", [P, NT, D]); self.aoT = buf("aoT", [P, CH, T])
                self.ln = LayerNorm(sb, sem, f"ln{s}", setup, 1)
                self.slots = [ps(f"slot{s}{i}", [P, 1024]) for i in range(2)]
                self.x_loaded = sig("x_loaded"); self.stored = sig("stored")
                self.filled = sig("filled"); self.xT_ready = sig("xT_ready"); self.v_ready = sig("v_ready")
                self.exp_ready = sig("exp_ready"); self.clipped = sig("clipped"); self.features = sig("features")
                self.state_ready = sig("state_ready"); self.den_ready = sig("den_ready"); self.z_ready = sig("z_ready")
                self.mixed = sig("mixed"); self.aoT_ready = sig("aoT_ready"); self.biased = sig("biased")
                self.summed = sig("summed")
                self.ring = Ring(plan, 2, self.emptied)

            def emptied(self, key):
                if key == "state":
                    return [(self.state_ready, 2 * CH, 2 * CH)]
                kind, i = key
                return [{"xT": (self.xT_ready, CH, i + 1), "q": (self.features, CH + PAIRS, i + 1),
                        "kv": (self.features, CH + PAIRS, CH + i + 1), "mix": (self.mixed, PAIRS, i + 1),
                        "aoT": (self.aoT_ready, CH, i + 1), "proj": (self.summed, 2, i + 1)}[kind]]

            def slot(self, key):
                return self.slots[self.ring.slot(key)]

        streams = [Stream(s) for s in range(2)]
        block = ctx.enter_context(nc.Block())

        def arrived(eng, st, b, key):
            eng.wait_ge(st.filled, st.ring.count(b, key))
            return st.slot(key)

        def run(steps, b):
            for step in steps:
                for st in streams:
                    step(st, b)

        NCONST = 5

        @block.sync
        def _(sp):
            sp.dma_start(ident[:, :], ident_in).then_inc(consts, 16)
            sp.dma_start(wqkv[:, :, :], wqkvT.rearrange("(c p) n -> p c n", p=P)).then_inc(consts, 16)
            sp.dma_start(wproj[:, :, :], wprojT.rearrange("(c p) n -> p c n", p=P)).then_inc(consts, 16)
            sp.dma_start(bias[:, :], on_all_partitions(bproj, D)).then_inc(consts, 16)
            sp.dma_start(head_blocks[:, :], head_blocks_in).then_inc(consts, 16)

            def load(st, b):
                sp.dma_start(st.x[:, :, :], tokens(x_in, 2 * b + st.s)).then_inc(st.x_loaded, 16)

            def store(st, b):
                wait_alone(sp, st.ln.normed, st.ln.done(b, 0))
                sp.dma_start(tokens(y_out, 2 * b + st.s), st.y[:, :, :]).then_inc(st.stored, 16)

            with sp.Fori(0, NSEQ // 2) as b:
                run([load, store], b)
            for st in streams:
                sp.wait_ge(st.stored, 16 * (NSEQ // 2) + 16)

        @block.gpsimd
        def _(pool):
            pool.wait_ge(setup, 4)
            pool.wait_ge(consts, 16 * NCONST)

            def clip(st, b):
                for i in range(CH + PAIRS):
                    wait_alone(pool, st.exp_ready, b * (CH + PAIRS) + i + 1)
                    part = st.exp_q[:, i, :] if i < CH else st.exp_k[:, 2 * (i - CH):2 * (i - CH) + 2, :]
                    pool.tensor_scalar(part, part, 1.0, None, ALU.min).then_inc(st.clipped, 1)

            def bias_x(st, b):
                pool.wait_ge(st.x_loaded, 16 * b + 16)
                pool.wait_ge(st.xT_ready, CH * b + CH)
                pool.tensor_tensor(st.x[:, :, :], st.x[:, :, :], each_tile(bias), ALU.add).then_inc(st.biased, 1)

            def norm(st, b):
                st.ln.reciprocal_root(pool, b, 0)

            with pool.Fori(0, NSEQ // 2) as b:
                run([clip, bias_x, norm], b)

        @block.scalar
        def _(act):
            act.wait_ge(setup, 4)
            act.wait_ge(consts, 16 * NCONST)

            def copy_xT(st, b):
                for c in range(CH):
                    act.copy(st.xT[:, c, :], arrived(act, st, b, ("xT", c))[:, :]).then_inc(st.xT_ready, 1)

            def exp_q(st, b):
                for c in range(CH):
                    act.activation(st.exp_q[:, c, :], arrived(act, st, b, ("q", c))[:, :], ACT.Exp).then_inc(st.exp_ready, 1)

            def exp_k(st, b):
                for g in range(PAIRS):
                    kv = arrived(act, st, b, ("kv", g))[:, :].rearrange("p (t n) -> p t n", t=2)
                    for t in range(2):
                        act.copy(st.v1[:, 2 * g + t, :, 0:P], kv[:, t, D:2 * D].rearrange("p (c n) -> p c n", c=CH))\
                            .then_inc(st.v_ready, 1)
                    act.activation(st.exp_k[:, 2 * g:2 * g + 2, :], kv[:, :, 0:D], ACT.Exp).then_inc(st.exp_ready, 1)

            def copy_aoT(st, b):
                for c in range(CH):
                    act.copy(st.aoT[:, c, :], arrived(act, st, b, ("aoT", c))[:, :]).then_inc(st.aoT_ready, 1)

            with act.Fori(0, NSEQ // 2) as b:
                run([copy_xT, exp_q, exp_k, copy_aoT], b)

        @block.vector
        def _(dve):
            for st in streams:
                dve.memset(st.v1[:, :, :, P:P + 1], 1.0).then_inc(setup, 1)
                dve.memset(st.ln.half[:, :], -0.5).then_inc(setup, 1)
            for st in streams:
                dve.sem_inc(st.stored, 16)
            dve.wait_ge(consts, 16 * NCONST)

            def features(st, b):
                for i in range(CH + PAIRS):
                    if i < CH:
                        x, e, o = arrived(dve, st, b, ("q", i))[:, :], st.exp_q[:, i, :], st.qT[:, i, :]
                    else:
                        g = i - CH
                        x = arrived(dve, st, b, ("kv", g))[:, :].rearrange("p (t n) -> p t n", t=2)[:, :, 0:D]
                        e, o = st.exp_k[:, 2 * g:2 * g + 2, :], st.k[:, 2 * g:2 * g + 2, :]
                    dve.wait_ge(st.clipped, b * (CH + PAIRS) + i + 1)
                    dve.scalar_tensor_tensor(o, x, 0.0, e, ALU.max, ALU.add).then_inc(st.features, 1)

            def state(st, b):
                s = arrived(dve, st, b, "state")
                for c in range(CH):
                    dve.tensor_tensor(st.state[:, c, 0:P], s[:, 512 * c:512 * c + P], head_blocks[:, 0:P], ALU.mult)\
                        .then_inc(st.state_ready, 1)
                    dve.tensor_scalar(st.state[:, c, P:W1], head_blocks[:, P:W1], s[:, 512 * c + P:512 * c + P + 1], None,
                                      ALU.mult).then_inc(st.state_ready, 1)

            def mix(st, b):
                for g in range(PAIRS):
                    s = arrived(dve, st, b, ("mix", g))[:, :].rearrange("p (t n) -> p t n", t=2)[:, :, 0:CH * W1]\
                        .rearrange("p t (c n) -> p t c n", c=CH)
                    z = st.z[:, g, :, :, :]
                    dve.tensor_scalar(z, s[:, :, :, P:W1], EPS, None, ALU.add).then_inc(st.den_ready, 1)
                    dve.wait_ge(st.den_ready, PAIRS * b + g + 1)
                    dve.reciprocal(z, z).then_inc(st.z_ready, 1)
                    dve.wait_ge(st.z_ready, PAIRS * b + g + 1)
                    for t in range(2):
                        for c in range(CH):
                            ins = dve.tensor_tensor(
                                st.ao[:, 2 * g + t, P * c:P * c + P].rearrange("p (h n) -> p h n", h=HC),
                                s[:, t, c, 0:P].rearrange("p (h n) -> p h n", h=HC),
                                z[:, t, c, :].unsqueeze(2).broadcast_to([P, HC, DH]), ALU.mult)
                    ins.then_inc(st.mixed, 1)

            def residual(st, b):
                for g in range(2):
                    s = arrived(dve, st, b, ("proj", g))[:, :].rearrange("p (t n) -> p t n", t=4)
                    dve.wait_ge(st.biased, b + 1)
                    part = st.x[:, 4 * g:4 * g + 4, :]
                    dve.tensor_tensor(part, s, part, ALU.add).then_inc(st.summed, 1)
                dve.wait_ge(st.summed, 2 * b + 2)
                st.ln.statistics(dve, st.x, b, 0)

            def norm(st, b):
                dve.wait_ge(st.stored, 16 * b + 16)
                st.ln.normalise(dve, st.y, st.x, b, 0)

            with dve.Fori(0, NSEQ // 2) as b:
                run([features, state, mix, residual, norm], b)

        @block.tensor
        def _(pe):
            mm = nc.tensor.matmul
            pe.wait_ge(setup, 4)
            pe.wait_ge(consts, 16 * NCONST)

            def use(st, b, key):
                st.ring.wait_free(pe, b, key)
                return st.slot(key)

            def transpose_x(st, b):
                pe.wait_ge(st.x_loaded, 16 * b + 16)
                for c in range(CH):
                    s = use(st, b, ("xT", c))
                    for t in range(NT):
                        last = nc.tensor.transpose(s[:, P * t:P * t + P], st.x[:, t, P * c:P * c + P], ident[:, :])
                    last.then_inc(st.filled, 1)

            def project_q(st, b):
                pe.wait_ge(st.xT_ready, CH * b + CH)
                for c in range(CH):
                    s = use(st, b, ("q", c))
                    for half in range(2):
                        cols = slice(512 * half, 512 * half + 512)
                        for k in range(CH):
                            last = mm(s[:, cols], wqkv[:, k, P * c:P * c + P], st.xT[:, k, cols], start=k == 0, stop=k == CH - 1)
                    last.then_inc(st.filled, 1)

            def project_kv(st, b):
                for g in range(PAIRS):
                    s = use(st, b, ("kv", g))
                    for t in range(2):
                        tok = P * (2 * g + t)
                        for k in range(CH):
                            last = mm(s[:, 512 * t:512 * t + 512], st.xT[:, k, tok:tok + P], wqkv[:, k, D:3 * D],
                                      start=k == 0, stop=k == CH - 1)
                    last.then_inc(st.filled, 1)

            def sum_state(st, b):
                s = use(st, b, "state")
                pe.wait_ge(st.v_ready, NT * b + NT)
                pe.wait_ge(st.features, (b + 1) * (CH + PAIRS))
                for c in range(CH):
                    for t in range(NT):
                        last = mm(s[:, 512 * c:512 * c + P + 1], st.k[:, t, P * c:P * c + P], st.v1[:, t, c, :],
                                  start=t == 0, stop=t == NT - 1)
                last.then_inc(st.filled, 1)

            def mix(st, b):
                pe.wait_ge(st.state_ready, (b + 1) * 2 * CH)
                for g in range(PAIRS):
                    s = use(st, b, ("mix", g))
                    for t in range(2):
                        tok = P * (2 * g + t)
                        for c in range(CH):
                            at = 512 * t + W1 * c
                            last = mm(s[:, at:at + W1], st.qT[:, c, tok:tok + P], st.state[:, c, :], start=True, stop=True)
                    last.then_inc(st.filled, 1)

            def transpose_ao(st, b):
                pe.wait_ge(st.mixed, PAIRS * (b + 1))
                for c in range(CH):
                    s = use(st, b, ("aoT", c))
                    for t in range(NT):
                        last = nc.tensor.transpose(s[:, P * t:P * t + P], st.ao[:, t, P * c:P * c + P], ident[:, :])
                    last.then_inc(st.filled, 1)

            def project_out(st, b):
                pe.wait_ge(st.aoT_ready, CH * (b + 1))
                for g in range(2):
                    s = use(st, b, ("proj", g))
                    for t in range(4):
                        tok = P * (4 * g + t)
                        for k in range(CH):
                            last = mm(s[:, D * t:D * t + D], st.aoT[:, k, tok:tok + P], wproj[:, k, :], start=k == 0, stop=k == CH - 1)
                    last.then_inc(st.filled, 1)

            with pe.Fori(0, NSEQ // 2) as b:
                run([transpose_x, project_q, project_kv, sum_state, mix, transpose_ao, project_out], b)
def nested_width_attention_layer(nc, x_in, y_out, q_wT, q_b, k_wT, k_b, v_wT, v_b, o_wT, o_b, norm_w, norm_b, ident_in, scratch):
    H, DH = 8, 32
    NE = 4
    QW = T // NE
    SCALE = float(D) ** -0.5
    width = [D >> e for e in range(NE)]
    BATCHES = [[(h, 0) for h in range(4)], [(h, 0) for h in range(4, 8)], [(h, 1) for h in range(4)],
               [(0, 2), (1, 2), (0, 3)]]
    UNITS = [u for batch in BATCHES for u in batch]
    FIRST = [sum(len(b) for b in BATCHES[:i]) for i in range(len(BATCHES))]
    NB = len(BATCHES)

    USED = {(c, "k"): T for c in range(2)} | {(0, "q"): T, (1, "q"): QW}
    PROJECTIONS = [("k", 0), ("q", 0), ("k", 1), ("q", 1)]

    def nat(i):
        return [("nat", FIRST[i] + u, t) for u in range(len(BATCHES[i])) for t in range(2)]

    def tr(i):
        return [("tr", FIRST[i] + u, half) for half in range(2) for u in range(len(BATCHES[i]))]

    def pv(i, half):
        return [("pv", i, NT // 2 * half + j) for j in range(NT // 2)]

    def ahead(steps):
        return [("ahead",) + s for s in steps]

    def merged(*streams):
        keyed = [((j + 0.5) / len(s), i, step) for i, s in enumerate(streams) for j, step in enumerate(s)]
        return [step for _, _, step in sorted(keyed, key=lambda k: k[:2])]

    front = [("xT", 0), ("xT", 1), ("xT", 2), ("load",), ("k", 0), ("q", 0), ("k", 1), ("q", 1), ("v", 0), ("v", 1), ("statistics",), ("rest of q",), ("normalise",)]
    steps = [("again",)]
    steps += merged(tr(1)[:4], nat(3)[:2], pv(0, 1), ahead(front[:4]))
    steps += merged(tr(1)[4:], nat(3)[2:], pv(1, 0), ahead(front[4:6]))
    steps += merged(tr(2)[:4], pv(1, 1), ahead(front[6:9])) + [("mT", 3)]
    steps += merged(tr(2)[4:], pv(2, 0), ahead(front[9:12]), ahead(nat(0)[:4]))
    steps += merged(tr(3)[:3], ahead(nat(0)[4:]), pv(2, 1)) + ahead(front[12:13])
    steps += merged(tr(3)[3:], ahead(nat(1)[:4])) + ahead([("mT", 0)]) + pv(3, 0) + ahead(front[13:])
    steps += ahead(nat(1)[4:6]) + pv(3, 1) + ahead(nat(1)[6:]) + [("out", 0), ("out", 1)] + ahead([("mT", 1)])
    steps += merged(ahead(tr(0)[:4]), ahead(nat(2)[:2])) + [("finish",)]
    steps += ahead(merged(tr(0)[4:], nat(2)[2:5])) + ahead(merged(nat(2)[5:], pv(0, 0)) + [("mT", 2)])
    lead = [s[1:] for s in steps if s[0] == "ahead"]

    unslotted = ("statistics", "normalise", "load", "again", "pv", "rest of q", "finish")
    plan = [s for s in steps if s[0] not in unslotted and s[1] not in unslotted]
    NSLOT = 3
    assert len(plan) % NSLOT == 0
    assert all(key[0] == "ahead" for key in plan[-NSLOT:])
    at = {key: i for i, key in enumerate(plan)}
    lead_at = {key[1:]: i for i, key in enumerate(k for k in plan if k[0] == "ahead")}
    rest_at = {key: i for i, key in enumerate(k for k in plan if k[0] != "ahead")}
    max_at = {s[1:]: i for i, s in enumerate(nat(0) + nat(1) + nat(2) + nat(3))}
    exp_at = {s[1:]: i for i, s in enumerate(tr(0) + tr(1) + tr(2) + tr(3))}

    with ExitStack() as ctx:
        sb, ps, sem = allocators(nc, ctx, "l1f")
        consts = sem("consts"); setup = sem("setup")
        xn = sb("xn", [P, NT, D])
        total = sb("total", [P, NT, D])
        xT = [sb("xT0", [P, T]), sb("xT1", [P, QW])]
        hi = sb("hi", [P, 2, T], f32r); lo = sb("lo", [P, 2, T], f32r)
        Qs = sb("Qs", [P, 2, len(UNITS), QW], f32r)
        Ks = sb("Ks", [P, 2, H, T], f32r)
        V = sb("V", [P, 2, NT, D])
        probs = sb("probs", [P, 2, 4, NT // 2 * QW])
        recip = sb("recip", [P, 2, QW])
        aoT = [sb("aoT0", [P, T]), sb("aoT1", [P, QW])]
        wq = sb("wq", [P, 2, D]); wk = sb("wk", [P, 2, D]); wv = sb("wv", [P, 2, D]); wo = sb("wo", [P, 2, D])
        qb = sb("qb", [P, 2]); kb = sb("kb", [P, 2]); vb = sb("vb", [P, D]); nw = sb("nw", [P, 2]); nb = sb("nb", [P, 2])
        ob = sb("ob", [P, NE, D])
        ident = sb("ident", [P, P])
        ones = sb("ones", [P, DH])
        rowmax = sb("rowmax", [P, 2 * len(UNITS)])
        maxT = sb("maxT", [8, 2, P], f32r)
        first_ln = LayerNorm(sb, sem, "first", setup, 1)
        own_ln = LayerNorm(sb, sem, "own", setup, 1)
        slots = [ps(f"slot{i}", [P, 1024]) for i in range(NSLOT)]
        OS = [ps(f"os{i}", [P, 2, QW]) for i in range(2)]
        SHIFT_ROW = 3 * DH

        def signal(name, per, step=1):
            return Signal(sem(name), per, step)

        x_loaded = signal("x_loaded", 1, 16); x_again = signal("x_again", 1, 16); stored = signal("stored", 1, 16)
        doubled = sem("doubled"); x2_ready = signal("x2_ready", NE)
        xT_ready = [signal(f"xT{i}_ready", n) for i, n in enumerate((1, 2, 1))]
        lead_filled = signal("lead_filled", len(lead_at)); filled = signal("filled", len(rest_at))
        hi_ready = signal("hi_ready", 4); lo_ready = signal("lo_ready", 4); v_ready = signal("v_ready", 2)
        bounced = {p: signal(f"bounced_{p[0]}{p[1]}", 2, 16) for p in PROJECTIONS}
        stacked = [signal(f"stacked{c}", 6, 16) for c in range(2)]
        rest_stacked = signal("rest_stacked", 9, 16)
        max_done = signal("max_done", len(max_at)); maxT_ready = signal("maxT_ready", NB)
        placed = [signal(f"placed{i}", NB // 2, 16) for i in range(2)]
        exp_done = signal("exp_done", len(exp_at)); pv_done = signal("pv_done", 2 * NB)
        recip_ready = signal("recip_ready", NB); ao_ready = signal("ao_ready", NB + 1)
        summed = signal("summed", NE)

        def arrived(eng, B, key, is_ahead):
            if is_ahead:
                lead_filled.wait(eng, B, lead_at[key] + 1)
                return slots[at[("ahead",) + key] % NSLOT]
            filled.wait(eng, B, rest_at[key] + 1)
            return slots[at[key] % NSLOT]

        def runs(key, is_ahead):
            return {"alone": key[0] == "ahead", None: key[0] != "ahead"}.get(is_ahead, True)

        def use(pe, B, key, is_ahead):
            i = at[("ahead",) + key if is_ahead else key]
            R = B - 1 if is_ahead else B
            here = [j for j in range(i) if j % NSLOT == i % NSLOT and runs(plan[j], is_ahead)]
            if here:
                old = here[-1]
            elif is_ahead == "alone":
                return slots[i % NSLOT]
            else:
                old, R = len(plan) - NSLOT + i % NSLOT, R - 1
            was = plan[old]
            if was[0] == "ahead":
                was, R = was[1:], R + 1
            kind = was[0]
            read, count = {"nat": lambda: (max_done, max_at[was[1:]] + 1), "tr": lambda: (exp_done, exp_at[was[1:]] + 1),
                           "mT": lambda: (maxT_ready, was[1] + 1), "out": lambda: (summed, (1, NE)[was[1]]),
                           "xT": lambda: (xT_ready[was[1]], None), "v": lambda: (v_ready, was[1] + 1),
                           "k": lambda: (lo_ready, 2 * was[1] + 1), "q": lambda: (lo_ready, 2 * was[1] + 2)}[kind]()
            read.wait(pe, R, count)
            return slots[i % NSLOT]

        def loop(eng, piece):
            def body(b, last):
                for n in range(2):
                    for step in steps:
                        if step[0] == "ahead":
                            if not (last and n == 1):
                                piece(step[1:], 2 * b + n + 1, 1 - n, not last, True)
                        else:
                            piece(step, 2 * b + n, n, True, None if last and n == 1 else False)

            for step in lead:
                piece(step, 0, 0, True, "alone")
            with eng.Fori(0, NSEQ // 2 - 1) as b:
                body(b, False)
            body(NSEQ // 2 - 1, True)

        NCONST = 14
        NSETUP = 8
        block = ctx.enter_context(nc.Block())

        @block.sync
        def _(sp):
            sp.dma_start(xn[:, :, :], tokens(x_in, 0)).then_inc(x_loaded.sem, 16)
            for w, src in ((wk, k_wT), (wq, q_wT), (wv, v_wT), (wo, o_wT)):
                sp.dma_start(w[:, :, :], src.rearrange("(c p) n -> p c n", p=P)).then_inc(consts, 16)
            for v, src in ((qb, q_b), (kb, k_b), (nw, norm_w), (nb, norm_b), (ident, ident_in)):
                sp.dma_start(v[:, :], src).then_inc(consts, 16)
            sp.dma_start(vb[:, :], on_all_partitions(v_b, D)).then_inc(consts, 16)
            sp.wait_ge(setup, NSETUP)
            for e in range(NE):
                sp.dma_start(ob[:, e, 0:width[e]], on_all_partitions(o_b, width[e])).then_inc(consts, 16)
            for s in (x_again, stored, x_loaded, *bounced.values(), *stacked, rest_stacked):
                s.start(sp)

            def piece(step, B, parity, next_too, is_ahead):
                kind = step[0]
                if kind == "load" and next_too:
                    for r in xT_ready:
                        r.wait(sp, B)
                    alone(sp)
                    x_loaded.by(sp.dma_start(xn[:, :, :], tokens(x_in, B + 1)))
                if kind == "again":
                    stored.wait(sp, B - 1)
                    alone(sp)
                    x_again.by(sp.dma_start(total[:, :, :], tokens(x_in, B)))
                if kind in ("k", "q"):
                    p = step
                    j, c = "kq".index(kind), step[1]
                    used = USED[(c, kind)]
                    stacked[c].wait(sp, B - 1)
                    if p == ("q", 0):
                        rest_stacked.wait(sp, B - 1)
                    alone(sp)
                    lo_ready.wait(sp, B, PROJECTIONS.index(p) + 1)
                    for part, source in enumerate((hi, lo)):
                        bounced[p].by(sp.dma_start(scratch[j, part, P * c:P * c + P, 0:used], words(source[:, j, 0:used])))
                    bounced[p].wait(sp, B)
                    exp_done.wait(sp, B - 2)
                    alone(sp)
                    for r in range(3):
                        rows = slice(DH * r, DH * r + DH)
                        if kind == "k":
                            src = scratch[0, (0, 0, 1)[r], P * c:P * c + P, :]
                            stacked[c].by(sp.dma_start(words(Ks[rows, parity, 4 * c:4 * c + 4, :]),
                                                       src.rearrange("(h d) t -> d h t", d=DH)))
                        else:
                            src = scratch[1, (0, 1, 0)[r], P * c:P * c + P, :]
                            u = FIRST[c]
                            stacked[c].by(sp.dma_start(words(Qs[rows, parity, u:u + 4, :]),
                                                       src[:, 0:QW].rearrange("(h d) t -> d h t", d=DH)))
                if kind == "rest of q":
                    for u, n, e in ((8, 4, 1), (12, 2, 2), (14, 1, 3)):
                        for r in range(3):
                            src = scratch[1, (0, 1, 0)[r], 0:DH * n, QW * e:QW * e + QW]
                            rest_stacked.by(sp.dma_start(words(Qs[DH * r:DH * r + DH, parity, u:u + n, :]),
                                                         src.rearrange("(h d) t -> d h t", d=DH)))
                if kind == "mT":
                    i = step[1]
                    maxT_ready.wait(sp, B, i + 1)
                    n = len(BATCHES[i])
                    placed[i % 2].by(sp.dma_start(
                        words(Qs[SHIFT_ROW:SHIFT_ROW + 1, parity, FIRST[i]:FIRST[i] + n, :])
                        .rearrange("o u (t q) -> o (u t) q", q=P), words(maxT[0:2 * n, i % 2, :])))
                if kind == "finish":
                    wait_alone(sp, own_ln.normed, own_ln.done(B, 0))
                    stored.by(sp.dma_start(tokens(y_out, B), total[:, :, :]))

            for s in placed:
                s.start(sp)
            loop(sp, piece)
            stored.wait(sp, NSEQ - 1)

        @block.gpsimd
        def _(pool):
            x2_ready.start(pool)
            pool.memset(Ks[96:128, 1, :, :].bitcast(f32), -1.0).then_inc(setup, 1)
            pool.wait_ge(setup, NSETUP)
            pool.wait_ge(consts, 16 * NCONST)

            def piece(step, B, parity, next_too, is_ahead):
                if step[0] == "statistics" and next_too:
                    first_ln.reciprocal_root(pool, B + 1, 0)
                if step[0] == "again":
                    x_again.wait(pool, B)
                    pool.tensor_tensor(total[:, :, :], total[:, :, :], total[:, :, :], ALU.add).then_inc(doubled, 1)
                    pool.wait_ge(doubled, B + 1)
                    for e in range(NE):
                        x2_ready.by(pool.tensor_tensor(total[:, 2 * e:2 * e + 2, :], total[:, 2 * e:2 * e + 2, :],
                                                       ob[:, e:e + 1, :].broadcast_to([P, 2, D]), ALU.add))
                if step[0] == "finish":
                    own_ln.reciprocal_root(pool, B, 0)
                    own_ln.normalise(pool, total, total, B, 0)

            first_ln.reciprocal_root(pool, 0, 0)
            loop(pool, piece)

        @block.scalar
        def _(act):
            for s in (xT_ready[0], xT_ready[1], hi_ready, exp_done):
                s.start(act)
            act.wait_ge(setup, NSETUP)
            act.wait_ge(consts, 16 * NCONST)

            def piece(step, B, parity, next_too, is_ahead):
                kind = step[0]
                if kind == "xT" and step[1] < 2:
                    s = arrived(act, B, step, is_ahead)
                    v_ready.wait(act, B - 1)
                    for rows, to, col in (((P, 0, 0), ) if step[1] == 0 else ((64, 512, 0), (32, 768, 256))):
                        n = 512 if rows == P else 256
                        xT_ready[step[1]].by(act.activation(xT[0][0:rows, to:to + n], s[0:rows, col:col + n], ACT.Identity,
                                                            bias=nb[0:rows, 0:1], scale=nw[0:rows, 0:1]))
                if kind in ("k", "q"):
                    c = step[1]
                    used = USED[(c, kind)]
                    bias = kb if kind == "k" else qb
                    s = arrived(act, B, step, is_ahead)
                    before = (kind, 1 - c)
                    bounced[before].wait(act, B - (c == 0))
                    hi_ready.by(act.activation(hi[:, "kq".index(kind), 0:used], s[:, 0:used], ACT.Identity,
                                               bias=bias[:, c:c + 1]))
                if kind == "tr":
                    _, u, half = step
                    i = max(i for i in range(NB) if FIRST[i] <= u)
                    s = arrived(act, B, step, is_ahead)
                    if u == FIRST[i]:
                        if i:
                            pv_done.wait(act, B, 2 * (i - 1) + half + 1)
                        else:
                            pv_done.wait(act, B - 1, 2 * (NB - 1) + half + 1)
                    exp_done.by(act.activation(probs[:, half, u - FIRST[i], :], s[:, :], ACT.Exp, scale=SCALE))

            loop(act, piece)

        @block.vector
        def _(dve):
            for s in (xT_ready[2], lo_ready, v_ready, max_done, maxT_ready, recip_ready, ao_ready, summed):
                s.start(dve)
            dve.memset(ob[:, :, :], 0.0).then_inc(setup, 1)
            dve.memset(ones[:, :], 1.0).then_inc(setup, 1)
            dve.memset(first_ln.half[:, :], -0.5).then_inc(setup, 1)
            dve.memset(own_ln.half[:, :], -0.5).then_inc(setup, 1)
            dve.memset(xT[0][:, :], 0.0).then_inc(setup, 1)
            dve.memset(Qs[96:128, :, :, :].bitcast(f32), 0.0).then_inc(setup, 1)
            dve.memset(Ks[96:128, 0, :, :].bitcast(f32), -1.0).then_inc(setup, 1)
            dve.wait_ge(setup, NSETUP)
            dve.wait_ge(consts, 16 * NCONST)

            def statistics(B):
                x_loaded.wait(dve, B)
                first_ln.statistics(dve, xn, B, 0)

            def norms(B, i):
                pv_done.wait(dve, B, 2 * i + 2)
                os = OS[i % 2]
                rows = DH * len(BATCHES[i])
                recip_ready.by(dve.reciprocal(recip[0:rows, i % 2, :], os[0:rows, 1, :]))
                recip_ready.wait(dve, B, i + 1)
                for dst, rows in (((aoT[i % 2][:, QW * (i // 2):QW * (i // 2) + QW], slice(0, P)),) if i < 3 else
                                  ((aoT[0][0:64, 2 * QW:3 * QW], slice(0, 64)), (aoT[0][0:32, 3 * QW:4 * QW], slice(64, 96)))):
                    ao_ready.by(dve.tensor_tensor(dst, os[rows, 0, :], recip[rows, i % 2, :], ALU.mult))

            def piece(step, B, parity, next_too, is_ahead):
                kind = step[0]
                if kind == "statistics" and next_too:
                    statistics(B + 1)
                if kind == "normalise" and next_too:
                    first_ln.normalise(dve, xn, xn, B + 1, 0)
                if step == ("xT", 2):
                    s = arrived(dve, B, step, is_ahead)
                    v_ready.wait(dve, B - 1)
                    xT_ready[2].by(dve.tensor_scalar(xT[1][:, :], s[:, 0:QW], nw[:, 1:2], nb[:, 1:2], ALU.mult, ALU.add))
                if kind in ("k", "q"):
                    c = step[1]
                    used = USED[(c, kind)]
                    bias = kb if kind == "k" else qb
                    j = "kq".index(kind)
                    before = (kind, 1 - c)
                    bounced[before].wait(dve, B - (c == 0))
                    hi_ready.wait(dve, B, PROJECTIONS.index(step) + 1)
                    s = slots[at[("ahead",) + step] % NSLOT]
                    lo_ready.by(dve.scalar_tensor_tensor(lo[:, j, 0:used], s[:, 0:used], bias[:, c:c + 1],
                                                         hi[:, j, 0:used], ALU.add, ALU.subtract))
                if kind == "v":
                    g = step[1]
                    s = arrived(dve, B, step, is_ahead)
                    v_ready.by(dve.tensor_tensor(V[:, parity, 4 * g:4 * g + 4, :],
                                                 s[:, :].rearrange("p (t n) -> p t n", t=4), each_tile(vb, 4), ALU.add))
                if kind == "nat":
                    _, u, t = step
                    s = arrived(dve, B, step, is_ahead)
                    max_done.by(dve.reduce_max(rowmax[:, 2 * u + t:2 * u + t + 1], s[:, :], AX))
                if kind == "mT":
                    i = step[1]
                    n = 2 * len(BATCHES[i])
                    s = arrived(dve, B, step, is_ahead)
                    placed[i % 2].wait(dve, B - (i < 2), (i + 2) % NB // 2 + 1)
                    maxT_ready.by(dve.tensor_copy(maxT[0:n, i % 2, :], s[0:n, 0:P]))
                if kind == "pv" and step[2] == NT - 1:
                    norms(B, step[1])
                if step == ("out", 0):
                    s = arrived(dve, B, step, is_ahead)
                    x2_ready.wait(dve, B)
                    summed.by(dve.tensor_tensor(total[:, 0:2, :], s[:, 0:2 * D].rearrange("p (t n) -> p t n", t=2),
                                                total[:, 0:2, :], ALU.add))
                if step == ("out", 1):
                    s = arrived(dve, B, step, is_ahead)
                    col = 0
                    for e in range(1, NE):
                        w = width[e]
                        o = s[:, col:col + 2 * w].rearrange("p (t n) -> p t n", t=2)
                        col += 2 * w
                        summed.by(dve.tensor_tensor(total[:, 2 * e:2 * e + 2, 0:w], o, total[:, 2 * e:2 * e + 2, 0:w], ALU.add))
                if kind == "finish":
                    summed.wait(dve, B)
                    own_ln.statistics(dve, total, B, 0)

            statistics(0)
            first_ln.normalise(dve, xn, xn, 0, 0)
            loop(dve, piece)

        @block.tensor
        def _(pe):
            for s in (lead_filled, filled, pv_done):
                s.start(pe)
            pe.wait_ge(setup, NSETUP)
            pe.wait_ge(consts, 16 * NCONST)
            mm = nc.tensor.matmul

            def piece(step, B, parity, next_too, is_ahead):
                kind = step[0]
                if kind != "pv" and kind in unslotted:
                    return
                if kind == "pv":
                    _, i, kt = step
                    n = len(BATCHES[i])
                    half, j = divmod(kt, NT // 2)
                    if j == 0:
                        exp_done.wait(pe, B, 2 * FIRST[i] + n * (half + 1))
                    if kt == 0:
                        ao_ready.wait(pe, B - (i < 2), (3, NB + 1, 1, 2)[i])
                        v_ready.wait(pe, B)
                    os = OS[i % 2]
                    for what in range(2):
                        for u in range(n):
                            h = BATCHES[i][u][0]
                            lhsT = ones[:, :] if what else V[:, parity, kt, DH * h:DH * h + DH]
                            last = mm(os[DH * u:DH * u + DH, what, :], lhsT, probs[:, half, u, QW * j:QW * j + QW],
                                      start=kt == 0 and what == 0, stop=kt == NT - 1, skip_group_check=True,
                                      tile_position=(0, DH * u))
                    if j == NT // 2 - 1:
                        pv_done.by(last)
                    return
                s = use(pe, B, step, is_ahead)
                if kind == "xT":
                    if step[1] == 0:
                        pe.wait_ge(first_ln.normed, first_ln.done(B, 0))
                    first, n, c = ((0, 4, 0), (4, 4, 0), (0, 2, 1))[step[1]]
                    for t in range(n):
                        last = nc.tensor.transpose(s[:, P * t:P * t + P], xn[:, first + t, P * c:P * c + P], ident[:, :])
                if kind in ("k", "q"):
                    c = step[1]
                    w = wk if kind == "k" else wq
                    if step == ("k", 0):
                        for r in xT_ready:
                            r.wait(pe, B)
                    cols = slice(P * c, P * c + P)
                    mm(s[:, 0:QW], w[:, 0, cols], xT[0][:, 0:QW], start=True, stop=False)
                    last = mm(s[:, 0:QW], w[:, 1, cols], xT[1][:, :], start=False, stop=True)
                    if kind == "k" or c == 0:
                        mm(s[:, QW:2 * QW], w[:, 0, cols], xT[0][:, QW:2 * QW], start=True, stop=True)
                        last = mm(s[:, 2 * QW:T], w[:, 0, cols], xT[0][:, 2 * QW:T], start=True, stop=True)
                if kind == "v":
                    for t in range(4):
                        tok = 4 * step[1] + t
                        o = s[:, D * t:D * t + D]
                        last = mm(o, xT[0][:, P * tok:P * tok + P], wv[:, 0, :], start=True, stop=tok >= 2)
                        if tok < 2:
                            last = mm(o, xT[1][:, P * tok:P * tok + P], wv[:, 1, :], start=False, stop=True)
                if kind == "nat":
                    _, u, t = step
                    if u == 0 and t == 0:
                        stacked[0].wait(pe, B)
                    if u == FIRST[1] and t == 0:
                        stacked[1].wait(pe, B)
                    if u == FIRST[2] and t == 0:
                        rest_stacked.wait(pe, B)
                    for half in range(2):
                        last = mm(s[:, 512 * half:512 * half + 512], Qs[0:96, parity, u, P * t:P * t + P],
                                  Ks[0:96, parity, UNITS[u][0], 512 * half:512 * half + 512], start=True, stop=True)
                if kind == "mT":
                    i = step[1]
                    n = 2 * len(BATCHES[i])
                    max_done.wait(pe, B, 2 * FIRST[i] + n)
                    last = nc.tensor.transpose(s[0:n, 0:P], rowmax[:, 2 * FIRST[i]:2 * FIRST[i] + n], ident[:, :])
                if kind == "tr":
                    _, u, half = step
                    if half == 0 and u in FIRST:
                        i = FIRST.index(u)
                        placed[i % 2].wait(pe, B, i // 2 + 1)
                    for j in range(4):
                        kt = 4 * half + j
                        last = mm(s[:, QW * j:QW * j + QW], Ks[:, parity, UNITS[u][0], P * kt:P * kt + P], Qs[:, parity, u, :],
                                  start=True, stop=True)
                if kind == "out":
                    if step[1] == 0:
                        ao_ready.wait(pe, B)
                    col = 0
                    for e in ((0,), range(1, NE))[step[1]]:
                        w = width[e]
                        for t in (2 * e, 2 * e + 1):
                            k = min(w, P)
                            last = mm(s[:, col:col + w], aoT[0][0:k, P * t:P * t + P], wo[0:k, 0, 0:w], start=True, stop=w <= P)
                            if w > P:
                                last = mm(s[:, col:col + w], aoT[1][:, P * t:P * t + P], wo[:, 1, 0:w], start=False, stop=True)
                            col += w
                (lead_filled if is_ahead else filled).by(last)

            loop(pe, piece)


def four_layers(nc, x, wq, wk, bq, bk, wv, bv, wo, bo, cos, sin, mask, maskT, ident, ident16,
                controller, f1, f2, f1_bias, tie, wqkv, wproj, bproj, head_blocks,
                q_w, q_b, k_w, k_b, v_w, v_b, o_w, o_b, norm_w, norm_b, out):
    def dram(name, shape):
        return nc.dram_tensor(name, shape, f32, kind="Internal").ap()

    x1, x2, x3 = (dram(f"x{i}", (NSEQ, T, D)) for i in (1, 2, 3))
    window_attention_layer(nc, x, x1, wq, wk, bq, bk, wv, bv, wo, bo, cos, sin, mask, maskT, ident, ident16,
                           dram("qk_rows", (2, 2, 16, 16, T)))
    token_choice_layer(nc, x1, x2, controller, f1, f2, f1_bias, tie, ident, dram("expert_outputs", (2, 128, 32, D)))
    linear_attention_layer(nc, x2, x3, wqkv, wproj, bproj, ident, head_blocks)
    nested_width_attention_layer(nc, x3, out, q_w, q_b, k_w, k_b, v_w, v_b, o_w, o_b, norm_w, norm_b, ident, dram("kq_rows", (2, 2, D, T)))


def shape_constants():
    import numpy as np

    half, blocked = 8, -1e30
    inv_freq = (np.float32(1.0) / np.float32(10000.0) ** (np.arange(half, dtype=np.float32) / np.float32(half))).astype(np.float32)
    ang = np.arange(T, dtype=np.float32)[:, None] * inv_freq[None, :]
    i = np.arange(P)
    before = lambda key, query: np.where(key >= query, 0.0, blocked)
    own = lambda key, query: np.where(key <= query, 0.0, blocked)
    heads = np.zeros((P, P + 8), np.float32)
    heads[:, :P] = i[:, None] // 16 == i[None, :] // 16
    heads[:, P:] = i[:, None] // 16 == np.arange(8)[None, :]
    bf = mybir.dt.np(bf16)
    return {
        "cos": np.ascontiguousarray(np.tile(np.cos(ang).astype(np.float32).T, (16, 1))),
        "sin": np.ascontiguousarray(np.tile(np.sin(ang).astype(np.float32).T, (16, 1))),
        "mask": np.concatenate([before(i[None, :], i[:, None]), own(i[None, :], i[:, None])], 1).astype(bf),
        "maskT": np.concatenate([before(i[:, None], i[None, :]), own(i[:, None], i[None, :])], 1).astype(bf),
        "ident": np.eye(P, dtype=np.float32), "ident16": np.eye(P, dtype=np.float32).astype(bf),
        "tie": np.linspace(0.0, 1e-6, 16, dtype=np.float32), "heads": heads,
    }


def kernel(**inputs):
    import numpy as np
    import concourse.bacc as bacc
    from concourse.bass_utils import run_bass_kernel_spmd as run

    a = {k: np.asarray(v) for k, v in inputs.items()}
    c = shape_constants()
    order = np.arange(D).reshape(16, 2, 8).transpose(1, 0, 2).reshape(D)
    column = lambda v: v.reshape(-1, P).T
    wqkv = a["L1_attn_Wqkv"].T
    args = [
        a["L0_attn_x"], a["L0_attn_Wq"][order].T, a["L0_attn_Wk"][order].T, column(a["L0_attn_bq"][order]),
        column(a["L0_attn_bk"][order]), a["L0_attn_Wv"].T, a["L0_attn_bv"], a["L0_attn_Wo"].T, a["L0_attn_bo"],
        c["cos"], c["sin"], c["mask"], c["maskT"], c["ident"], c["ident16"],
        a["L0_ffn_controller"].reshape(D, 64), a["L0_ffn_f1"].reshape(D, 64, 64), a["L0_ffn_f2"].reshape(64, 64, D),
        column(a["L0_ffn_bias"]), c["tie"],
        wqkv, a["L1_attn_Wproj"].T, a["L1_attn_bproj"], c["heads"],
        a["L1_ffn_q_w"].T, column(a["L1_ffn_q_b"]), a["L1_ffn_k_w"].T, column(a["L1_ffn_k_b"]), a["L1_ffn_v_w"].T,
        a["L1_ffn_v_b"], a["L1_ffn_o_w"].T, a["L1_ffn_o_b"], column(a["L1_ffn_norm_w"]), column(a["L1_ffn_norm_b"]),
    ]
    nc = bacc.Bacc("TRN2", target_bir_lowering=False, num_devices=1)
    arrays, aps = {}, []
    for i, v in enumerate(args):
        v = np.ascontiguousarray(v)
        arrays[f"in_{i}_dram"] = v
        aps.append(nc.dram_tensor(f"in_{i}_dram", v.shape, mybir.dt.from_np(v.dtype), kind="ExternalInput").ap())
    out = nc.dram_tensor("out_dram", (NSEQ, T, D), f32, kind="ExternalOutput").ap()
    four_layers(nc, *aps, out)
    r = run(nc, [arrays], core_ids=[0])
    return r.results[0]["out_dram"]
```

```python
from contextlib import ExitStack

import concourse.bass as bass
from concourse import mybir

f32 = mybir.dt.float32
f32r = mybir.dt.float32r
bf16 = mybir.dt.bfloat16
ACT = mybir.ActivationFunctionType
ALU = mybir.AluOpType
AX = mybir.AxisListType.X

P = 128
NSEQ, T, D = 8, 1024, 256
NT = T // P
LN_EPS = 1e-5


def allocators(nc, ctx, layer):
    def sb(name, shape, dtype=f32):
        return ctx.enter_context(nc.sbuf_tensor(f"{layer}_{name}", shape, dtype))

    def ps(name, shape, dtype=f32):
        return ctx.enter_context(nc.psum_tensor(f"{layer}_{name}", shape, dtype))

    def sem(name):
        return ctx.enter_context(nc.semaphore(f"{layer}_{name}"))

    return sb, ps, sem


def tokens(dram, b):
    return dram[bass.ds(b, 1), :, :].rearrange("o (t p) d -> p (o t) d", p=P)


def alone(eng):
    eng.nop(nofuse=True)


def wait_alone(eng, sem, value):
    eng.wait_ge(sem, value)
    alone(eng)


def words(ap):
    return ap.bitcast(f32)


def on_all_partitions(row, n):
    return row[0:n].partition_broadcast(P)


def each_tile(v, n=NT):
    return v[:, :].unsqueeze(1).broadcast_to([P, n, D])


class Signal:

    def __init__(self, sem, per, step=1):
        self.sem, self.per, self.step = sem, per, step

    def start(self, eng):
        eng.sem_inc(self.sem, 2 * self.per * self.step)

    def by(self, instruction):
        instruction.then_inc(self.sem, self.step)

    def wait(self, eng, block, n=None):
        eng.wait_ge(self.sem, block * (self.per * self.step) + (2 * self.per + (self.per if n is None else n)) * self.step)


class Ring:

    def __init__(self, plan, n, emptied=None):
        self.at = {key: i for i, key in enumerate(plan)}
        self.plan, self.n, self.emptied = plan, n, emptied
        assert len(self.at) == len(plan)

    def slot(self, key):
        return self.at[key] % self.n

    def count(self, b, key):
        return b * len(self.plan) + self.at[key] + 1

    def before(self, key):
        i = self.at[key] - self.n
        return self.plan[i] if i >= 0 else None

    def wait_free(self, pe, b, key):
        old = self.before(key)
        if old is not None:
            for sem, per_sequence, position in self.emptied(old):
                pe.wait_ge(sem, b * per_sequence + position)


def merged(*streams):
    keyed = [((j + 0.5) / len(s), i, step) for i, s in enumerate(streams) for j, step in enumerate(s)]
    return [step for _, _, step in sorted(keyed, key=lambda k: k[:2])]


def ahead(steps):
    return [("ahead",) + s for s in steps]


class Pipeline:

    def __init__(self, steps, unslotted, slots):
        self.steps, self.unslotted, self.slots = steps, unslotted, slots
        self.lead = [s[1:] for s in steps if s[0] == "ahead"]
        self.plan = [s for s in steps if s[0] not in unslotted and s[1] not in unslotted]
        assert len(self.plan) % len(slots) == 0
        assert all(key[0] == "ahead" for key in self.plan[-len(slots):])
        self.at = {key: i for i, key in enumerate(self.plan)}
        self.lead_at = {key[1:]: i for i, key in enumerate(k for k in self.plan if k[0] == "ahead")}
        self.rest_at = {key: i for i, key in enumerate(k for k in self.plan if k[0] != "ahead")}

    def signals(self, lead_filled, filled, reader):
        self.lead_filled, self.filled, self.reader = lead_filled, filled, reader

    def slot(self, key):
        return self.slots[self.at[key if key in self.at else ("ahead",) + key] % len(self.slots)]

    def arrived(self, eng, B, key):
        if key in self.lead_at:
            self.lead_filled.wait(eng, B, self.lead_at[key] + 1)
        else:
            self.filled.wait(eng, B, self.rest_at[key] + 1)
        return self.slot(key)

    def use(self, pe, B, key, when):
        n = len(self.slots)
        is_ahead = key in self.lead_at
        i = self.at[("ahead",) + key if is_ahead else key]
        R = B - 1 if is_ahead else B
        here = [j for j in range(i) if j % n == i % n
                and {"alone": self.plan[j][0] == "ahead", "last": self.plan[j][0] != "ahead"}.get(when, True)]
        if here:
            old = here[-1]
        elif when == "alone":
            return self.slots[i % n]
        else:
            old, R = len(self.plan) - n + i % n, R - 1
        was = self.plan[old]
        if was[0] == "ahead":
            was, R = was[1:], R + 1
        signal, count = self.reader(was)
        signal.wait(pe, R, count)
        return self.slots[i % n]

    def put(self, key, instruction):
        (self.lead_filled if key in self.lead_at else self.filled).by(instruction)

    def loop(self, eng, pairs, piece):
        def body(b, last):
            for n in range(2):
                when = "last" if last and n == 1 else "both"
                for step in self.steps:
                    if step[0] != "ahead":
                        piece(step, 2 * b + n, b, n, when, True)
                    elif when != "last":
                        piece(step[1:], 2 * b + n + 1, b + n, 1 - n, when, not last)

        for step in self.lead:
            piece(step, 0, 0, 0, "alone", True)
        with eng.Fori(0, pairs - 1) as b:
            body(b, False)
        body(pairs - 1, True)


class LayerNorm:

    def __init__(self, sb, sem, name, setup, uses, tiles=NT):
        self.setup, self.uses, self.tiles = setup, uses, tiles
        self.stats = sb(f"{name}_stats", [P, tiles, 6])
        self.mv = sb(f"{name}_mv", [P, tiles, 2])
        self.rstd = sb(f"{name}_rstd", [P, tiles])
        self.half = sb(f"{name}_half", [P, tiles])
        self.summed = sem(f"{name}_summed")
        self.aggregated = sem(f"{name}_aggregated")
        self.var_ready = sem(f"{name}_var_ready")
        self.rstd_ready = sem(f"{name}_rstd_ready")
        self.normed = sem(f"{name}_normed")

    def count(self, b, use):
        return b * self.uses + use + 1

    def statistics(self, dve, x, b, use):
        n = self.count(b, use)
        for t in range(self.tiles):
            dve.bn_stats(self.stats[:, t, :], x[:, t, :]).then_inc(self.summed, 1)
        wait_alone(dve, self.summed, n * self.tiles)
        for t in range(self.tiles):
            dve.bn_aggr(self.mv[:, t, :], self.stats[:, t, :]).then_inc(self.aggregated, 1)
        dve.wait_ge(self.aggregated, n * self.tiles)
        dve.tensor_scalar(self.mv[:, :, 1], self.mv[:, :, 1], LN_EPS, None, ALU.add).then_inc(self.var_ready, 1)

    def reciprocal_root(self, pool, b, use):
        pool.wait_ge(self.var_ready, self.count(b, use))
        pool.tensor_tensor(self.rstd[:, :], self.mv[:, :, 1], self.half[:, :], ALU.pow).then_inc(self.rstd_ready, 1)

    def normalise(self, eng, out, x, b, use):
        wait_alone(eng, self.rstd_ready, self.count(b, use))
        for t in range(self.tiles):
            eng.tensor_scalar(out[:, t, :], x[:, t, :], self.mv[:, t, 0:1], self.rstd[:, t:t + 1],
                              ALU.subtract, ALU.mult).then_inc(self.normed, 1)

    def done(self, b, use):
        return self.count(b, use) * self.tiles



def window_attention_layer(nc, x_in, y_out, wq_in, wk_in, bq_in, bk_in, wvT, bv_in, woT, bo_in, cos_in, sin_in,
                           mask_in, maskT_in, ident_in, ident16_in, scratch):
    H, DH = 16, 16
    BT = 4
    BW = BT * P
    HG = 4
    NHG = H // HG
    HR = DH // 2
    SCALE = float(DH) ** -0.5
    CH = D // P
    SHIFT_ROW = 96

    def nat(t):
        return [("nat", NHG * t + g) for g in range(NHG)]

    def tr(t):
        return [("tr", NHG * t + g) for g in range(NHG)]

    def pv(t):
        return [("pv", NHG * t + g) for g in range(NHG)]

    steps = merged(pv(0)[:2], tr(1)[:2], nat(3)[:2], ahead([("xT", 0), ("xT", 1), ("q", 0)]))
    steps += merged(pv(0)[2:], tr(1)[2:], nat(3)[2:]) + ahead([("split q", 0)]) + [("maxT", 3), ("back", 0)]
    steps += ahead([("k", 0)]) + merged(pv(1)[:2], tr(2)[:2], ahead([("split k", 0)])) + merged(pv(1)[2:], tr(2)[2:], ahead([("bias", 0), ("load", 0), ("v", 0)]))
    steps += merged(pv(2)[:3], tr(3)[:3], [("back", 1)]) + pv(2)[3:] + [("aoT", 0)] + tr(3)[3:] + ahead(nat(0)[:1])
    steps += [("back", 2)] + ahead(nat(0)[1:]) + ahead(nat(1)[:1])
    steps += merged(pv(3), ahead(nat(1)[1:3])) + ahead([("maxT", 0)] + nat(1)[3:]) + [("back", 3)] + ahead(nat(2)[:1])
    steps += [("aoT", 1)] + ahead(tr(0)[:1]) + [("proj", 0)] + ahead([("maxT", 1)] + merged(tr(0)[1:], nat(2)[1:]))
    steps += [("statistics", 0)] + ahead([("maxT", 2)]) + [("normalise", 0)]
    unslotted = ("split q", "split k", "bias", "load", "pv", "statistics", "normalise")

    with ExitStack() as ctx:
        sb, ps, sem = allocators(nc, ctx, "l0a")
        consts = sem("consts"); setup = sem("setup"); cleared = sem("cleared"); cleared_too = sem("cleared_too")
        ident = sb("ident", [P, P]); ident16 = sb("ident16", [P, P], bf16)
        mask = sb("mask", [P, 2, P], bf16)
        maskT = sb("maskT", [P, 2, P], bf16)
        wq = sb("wq", [P, CH, D]); wk = sb("wk", [P, CH, D]); wv = sb("wv", [P, CH, D]); wo = sb("wo", [P, CH, D])
        bq = sb("bq", [P, 2]); bk = sb("bk", [P, 2]); bv = sb("bv", [P, D]); bo = sb("bo", [P, D])
        cos = sb("cos", [P, T]); sin = sb("sin", [P, T])
        x = sb("x", [P, BT, D])
        total = sb("total", [P, 2, BT, D])
        xT = sb("xT", [P, CH, BW])
        turned = sb("turned", [P, 4, BW])
        rot = turned[:, 0::2, :]
        hi = sb("hi", [P, 2, BW], f32r); lo = sb("lo", [P, 2, BW], f32r)
        Qs = sb("Qs", [P, 2, H, BW], f32r)
        Ks = sb("Ks", [P, 2, H // 2, P + BW], f32r)
        V = sb("V", [P, 2, BT + 1, H, 2 * DH])
        probs = sb("probs", [P, H, 2, P])
        oT = sb("oT", [P, 4, P])
        recip = sb("recip", [P, BT, H])
        ao = sb("ao", [P, BT, D]); aoT = sb("aoT", [P, CH, BW])
        rowmax = sb("rowmax", [P, BT, H])
        maxT = sb("maxT", [H, 2, P], f32r)
        ln = LayerNorm(sb, sem, "ln", setup, 1, BT)
        pipeline = Pipeline(steps, unslotted, [ps(f"slot{i}", [P, 1024]) for i in range(3)])
        arrived = pipeline.arrived
        O = [ps(f"O{i}", [P, 4, P]) for i in range(2)]


        def signal(name, per, step=1):
            return Signal(sem(name), per, step)

        x_loaded = signal("x_loaded", 1, 16); stored = signal("stored", 1, 16)
        lead_filled = signal("lead_filled", len(pipeline.lead_at)); filled = signal("filled", len(pipeline.rest_at))
        xT_ready = signal("xT_ready", CH); biased = signal("biased", 1)
        turned_ready = signal("turned_ready", 8); rot_ready = signal("rot_ready", 4)
        hi_ready = signal("hi_ready", 2); lo_ready = signal("lo_ready", 2)
        v_ready = signal("v_ready", 1); v_carried = signal("v_carried", 1)
        bounced = {w: signal(f"bounced_{w}", 4, 16) for w in "qk"}
        stacked = {w: signal(f"stacked_{w}", 6, 16) for w in "qk"}
        max_ready = signal("max_ready", BT * NHG); maxT_ready = signal("maxT_ready", BT)
        placed = [signal(f"placed{t}", BT // 2, 16) for t in range(2)]
        exp_ready = signal("exp_ready", BT * NHG); pv_done = signal("pv_done", BT * NHG)
        oT_ready = signal("oT_ready", BT); recip_ready = signal("recip_ready", BT); ao_ready = signal("ao_ready", BT)
        aoT_ready = signal("aoT_ready", 2); summed = signal("summed", 1)

        def reader(key):
            kind, n = key
            return {"nat": (max_ready, n + 1), "maxT": (maxT_ready, n + 1), "tr": (exp_ready, n + 1),
                    "back": (ao_ready, n + 1), "aoT": (aoT_ready, n + 1), "proj": (summed, 1),
                    "xT": (xT_ready, n + 1), "q": (turned_ready, 4), "k": (turned_ready, 8), "v": (v_ready, 1)}[kind]

        pipeline.signals(lead_filled, filled, reader)

        NCONST = 14
        NSETUP = 3
        block = ctx.enter_context(nc.Block())

        @block.sync
        def _(sp):
            sp.dma_start(x[:, :, :], tokens(x_in, 0)[:, 0:BT, :]).then_inc(x_loaded.sem, 16)
            for dst, src in ((ident, ident_in), (ident16, ident16_in), (cos, cos_in), (sin, sin_in), (bq, bq_in), (bk, bk_in)):
                sp.dma_start(dst[:, :], src).then_inc(consts, 16)
            for dst, src in ((mask, mask_in), (maskT, maskT_in)):
                sp.dma_start(dst[:, :, :], src.rearrange("p (a n) -> p a n", a=2)).then_inc(consts, 16)
            for dst, src in ((wq, wq_in), (wk, wk_in), (wv, wvT), (wo, woT)):
                sp.dma_start(dst[:, :, :], src.rearrange("(c p) n -> p c n", p=P)).then_inc(consts, 16)
            for dst, src in ((bv, bv_in), (bo, bo_in)):
                sp.dma_start(dst[:, :], on_all_partitions(src, D)).then_inc(consts, 16)
            for s in (x_loaded, stored, *bounced.values(), *stacked.values(), *placed):
                s.start(sp)
            sp.wait_ge(cleared, 1); sp.wait_ge(cleared_too, 2)

            def block_of(dram, b, n):
                return tokens(dram, b)[:, BT * n:BT * n + BT, :]

            def piece(step, B, b, n, when, next_too):
                kind, i = step
                tok = BW * n
                if kind == "load" and next_too:
                    xT_ready.wait(sp, B)
                    alone(sp)
                    biased.wait(sp, B)
                    alone(sp)
                    x_loaded.by(sp.dma_start(x[:, :, :], block_of(x_in, b + n, 1 - n)))
                if kind in ("split q", "split k"):
                    w = kind[-1]
                    i = "qk".index(w)
                    lo_ready.wait(sp, B, i + 1)
                    for part, source in enumerate((hi, lo)):
                        for r in range(2):
                            rows = scratch[i, part, :, HR * r:HR * r + HR, tok:tok + BW]
                            bounced[w].by(sp.dma_start(rows, words(source[:, r, :])))
                    bounced[w].wait(sp, B)
                    pv_done.wait(sp, B - 2)
                    for parity in range(2):
                        for term, part in enumerate((0, 1, 0) if w == "q" else (0, 0, 1)):
                            first = 3 * DH * parity + DH * term
                            if w == "q":
                                src = scratch[i, part, parity::2, :, tok:tok + BW]
                                dst = Qs[first:first + DH, n, parity::2, :]
                            else:
                                skip = 0 if n else P
                                src = scratch[i, part, parity::2, :, tok - P + skip:tok + BW]
                                dst = Ks[first:first + DH, n, :, skip:]
                            stacked[w].by(sp.dma_start(words(dst), src.rearrange("h d t -> d h t")))
                if kind == "maxT":
                    maxT_ready.wait(sp, B, i + 1)
                    placed[i % 2].by(sp.dma_start(words(Qs[SHIFT_ROW:SHIFT_ROW + 1, n, :, P * i:P * i + P]),
                                              words(maxT[:, i % 2, :])))
                if kind == "normalise":
                    wait_alone(sp, ln.normed, ln.done(B, 0))
                    stored.by(sp.dma_start(block_of(y_out, b, n), total[:, n, :, :]))

            pipeline.loop(sp, NSEQ, piece)
            stored.wait(sp, 2 * NSEQ - 1)

        @block.gpsimd
        def _(pool):
            for s in (biased, rot_ready, lo_ready):
                s.start(pool)
            pool.memset(Qs[:, 1, :, :].bitcast(f32), 0.0).then_inc(cleared_too, 1)
            pool.wait_ge(cleared_too, 1)
            pool.memset(Ks[SHIFT_ROW:P, :, :, :].bitcast(f32), -1.0).then_inc(cleared_too, 1)
            pool.wait_ge(cleared_too, 2)
            pool.wait_ge(setup, NSETUP)
            pool.wait_ge(consts, 16 * NCONST)

            def piece(step, B, b, n, when, next_too):
                kind, i = step
                if kind == "bias":
                    x_loaded.wait(pool, B)
                    stored.wait(pool, B - 2)
                    biased.by(pool.tensor_tensor(total[:, n, :, :], x[:, :, :], each_tile(bo, BT), ALU.add))
                if kind in ("q", "k"):
                    i = "qk".index(kind)
                    turned_ready.wait(pool, B, 4 * i + 2)
                    rot_ready.by(pool.tensor_tensor(rot[:, 0, :], turned[:, 0, :], turned[:, 1, :], ALU.subtract))
                    turned_ready.wait(pool, B, 4 * i + 4)
                    rot_ready.by(pool.tensor_tensor(rot[:, 1, :], turned[:, 2, :], turned[:, 3, :], ALU.add))
                if kind in ("split q", "split k"):
                    i = "qk".index(kind[-1])
                    hi_ready.wait(pool, B, i + 1)
                    rot_ready.wait(pool, B, 2 * i + 2)
                    other = bounced["k" if i == 0 else "q"]
                    other.wait(pool, B - 1 if i == 0 else B)
                    lo_ready.by(pool.tensor_tensor(lo[:, :, :], rot[:, :, :], hi[:, :, :].bitcast(f32), ALU.subtract))
                if kind == "statistics":
                    ln.reciprocal_root(pool, B, 0)

            pipeline.loop(pool, NSEQ, piece)

        @block.scalar
        def _(act):
            for s in (xT_ready, hi_ready, v_carried, exp_ready, oT_ready, aoT_ready):
                s.start(act)
            act.wait_ge(setup, NSETUP)
            act.wait_ge(consts, 16 * NCONST)

            def piece(step, B, b, n, when, next_too):
                kind, i = step
                if kind == "xT":
                    xT_ready.by(act.copy(xT[:, i, :], arrived(act, B, step)[:, 0:BW]))
                if kind in ("split q", "split k"):
                    i = "qk".index(kind[-1])
                    rot_ready.wait(act, B, 2 * i + 2)
                    other = bounced["k" if i == 0 else "q"]
                    other.wait(act, B - 1 if i == 0 else B)
                    hi_ready.by(act.copy(hi[:, :, :], rot[:, :, :]))
                if kind == "v":
                    v_ready.wait(act, B - 1)
                    pv_done.wait(act, B - 2)
                    if n:
                        v_carried.by(act.copy(V[:, 1, 0, :, :], V[:, 0, BT, :, :]))
                    else:
                        v_carried.by(act.copy(V[:, 0, 0, :, :], V[:, 1, BT, :, :]))
                if kind == "tr":
                    t, g = i // NHG, i % NHG
                    s = arrived(act, B, step)[:, :].rearrange("p (h a q) -> p h a q", h=HG, a=2)
                    pv_done.wait(act, B if t else B - 1, NHG * ((t - 1) % BT) + g + 1)
                    first = 0 if n or t else 1
                    exp_ready.by(act.activation(probs[:, HG * g:HG * g + HG, first:2, :], s[:, :, first:2, :],
                                                ACT.Exp, scale=SCALE))
                if kind == "pv" and i % NHG == NHG - 1:
                    t = i // NHG
                    pv_done.wait(act, B, i + 1)
                    filled.wait(act, B - (t == 0), pipeline.rest_at[("back", (t - 1) % BT)] + 1)
                    oT_ready.by(act.copy(oT[:, :, :], O[t % 2][:, :, :]))
                if kind == "aoT":
                    s = arrived(act, B, step)[:, 0:2 * CH * P].rearrange("p (c n) -> p c n", c=CH)
                    aoT_ready.by(act.copy(aoT[:, :, 2 * P * i:2 * P * i + 2 * P], s))

            pipeline.loop(act, NSEQ, piece)

        @block.vector
        def _(dve):
            dve.memset(V[:, :, :, :, :], 1.0).then_inc(setup, 1)
            dve.memset(ln.half[:, :], -0.5).then_inc(setup, 1)
            dve.memset(maxT[:, :, :].bitcast(f32), 0.0).then_inc(setup, 1)
            dve.memset(Qs[:, 0, :, :].bitcast(f32), 0.0).then_inc(cleared, 1)
            for s in (turned_ready, v_ready, max_ready, maxT_ready, recip_ready, ao_ready, summed):
                s.start(dve)
            dve.wait_ge(consts, 16 * NCONST)

            def piece(step, B, b, n, when, next_too):
                kind, i = step
                cols = slice(BW * n, BW * n + BW)
                if kind in ("q", "k"):
                    i = "qk".index(kind)
                    bias = (bq, bk)[i]
                    s = arrived(dve, B, step)
                    hi_ready.wait(dve, B if i else B - 1, 1 if i else 2)
                    lo_ready.wait(dve, B if i else B - 1, 1 if i else 2)
                    for j, (r, table) in enumerate(((0, cos), (1, sin), (0, sin), (1, cos))):
                        turned_ready.by(dve.scalar_tensor_tensor(turned[:, j, :], s[:, BW * r:BW * r + BW],
                                                                 bias[:, r:r + 1], table[:, cols], ALU.add, ALU.mult))
                if kind == "v":
                    s = arrived(dve, B, step)
                    pv_done.wait(dve, B - 2)
                    v_carried.wait(dve, B - 1)
                    for t in range(BT):
                        last = dve.tensor_tensor(V[:, n, t + 1, :, 0:DH],
                                                 s[:, D * t:D * t + D].rearrange("p (h d) -> p h d", h=H),
                                                 bv[:, :].rearrange("p (h d) -> p h d", h=H), ALU.add)
                    v_ready.by(last)
                if kind == "nat":
                    t, g = i // NHG, i % NHG
                    s = arrived(dve, B, step)[:, :].rearrange("p (h k) -> p h k", h=HG)
                    first = 0 if n or t else P
                    max_ready.by(dve.reduce_max(rowmax[:, t, HG * g:HG * g + HG], s[:, :, first:2 * P], AX))
                if kind == "maxT":
                    s = arrived(dve, B, step)
                    placed[i % 2].wait(dve, B - (i < 2), (i - 2) % BT // 2 + 1)
                    maxT_ready.by(dve.tensor_copy(maxT[:, i % 2, :], s[0:H, 0:P]))
                if kind == "back":
                    s = arrived(dve, B, step)[:, 0:512].rearrange("p (h d) -> p h d", h=H)
                    recip_ready.by(dve.reciprocal(recip[:, i, :], s[:, :, DH]))
                    recip_ready.wait(dve, B, i + 1)
                    ao_ready.by(dve.tensor_tensor(ao[:, i, :].rearrange("p (h d) -> p h d", h=H), s[:, :, 0:DH],
                                                  recip[:, i, :].unsqueeze(2).broadcast_to([P, H, DH]), ALU.mult))
                if kind == "proj":
                    s = arrived(dve, B, step)
                    biased.wait(dve, B)
                    summed.by(dve.tensor_tensor(total[:, n, :, :], s[:, :].rearrange("p (t n) -> p t n", t=BT),
                                                total[:, n, :, :], ALU.add))
                if kind == "statistics":
                    summed.wait(dve, B)
                    ln.statistics(dve, total[:, n, :, :], B, 0)
                if kind == "normalise":
                    ln.normalise(dve, total[:, n, :, :], total[:, n, :, :], B, 0)

            pipeline.loop(dve, NSEQ, piece)

        @block.tensor
        def _(pe):
            mm = nc.tensor.matmul
            for s in (lead_filled, filled, pv_done):
                s.start(pe)
            pe.wait_ge(setup, NSETUP)
            pe.wait_ge(consts, 16 * NCONST)

            def piece(step, B, b, n, when, next_too):
                kind, i = step
                t, g = i // NHG, i % NHG
                if kind == "pv":
                    exp_ready.wait(pe, B, i + 1)
                    if i == 0:
                        v_ready.wait(pe, B)
                        v_carried.wait(pe, B)
                    if g == 0:
                        oT_ready.wait(pe, B if t >= 2 else B - 1, (t - 2) % BT + 1)
                    first = 0 if n or t else 1
                    for a in range(first, 2):
                        for j in range(HG):
                            h = HG * g + j
                            last = mm(O[t % 2][32 * j:32 * j + 32, g, :], V[:, n, t + a, h, :], probs[:, h, a, :],
                                      start=a == first, stop=a == 1, tile_position=(0, 32 * j))
                    pv_done.by(last)
                if kind in unslotted:
                    return
                if kind == "xT":
                    x_loaded.wait(pe, B)
                if kind == "q":
                    xT_ready.wait(pe, B)
                if step == ("nat", 0):
                    stacked["q"].wait(pe, B)
                    stacked["k"].wait(pe, B)
                if kind == "maxT":
                    max_ready.wait(pe, B, NHG * i + NHG)
                if kind == "tr" and g == 0:
                    placed[t % 2].wait(pe, B, t // 2 + 1)
                if kind == "back":
                    oT_ready.wait(pe, B, i + 1)
                if kind == "aoT":
                    ao_ready.wait(pe, B, 2 * i + 2)
                if kind == "proj":
                    aoT_ready.wait(pe, B)
                s = pipeline.use(pe, B, step, when)
                if kind == "xT":
                    for tt in range(BT):
                        last = nc.tensor.transpose(s[:, P * tt:P * tt + P], x[:, tt, P * i:P * i + P], ident[:, :])
                if kind in ("q", "k"):
                    w = wq if kind == "q" else wk
                    for r in range(2):
                        for c in range(CH):
                            last = mm(s[:, BW * r:BW * r + BW], w[:, c, P * r:P * r + P], xT[:, c, :],
                                      start=c == 0, stop=c == CH - 1)
                if kind == "v":
                    for tt in range(BT):
                        for c in range(CH):
                            last = mm(s[:, D * tt:D * tt + D], xT[:, c, P * tt:P * tt + P], wv[:, c, :],
                                      start=c == 0, stop=c == CH - 1)
                if kind == "nat":
                    first = 0 if n or t else 1
                    for k in range(HG // 2):
                        o = s[:, 512 * k:512 * k + 512].rearrange("p (h a n) -> p h a n", h=2, a=2)[:, :, first:2, :]
                        mm(o, ident16[:, :], mask[:, first:2, :].unsqueeze(1).broadcast_to([P, 2, 2 - first, P]),
                           start=True, stop=False, skip_group_check=True)
                        for m in range(2):
                            h = HG * g + 2 * k + m
                            last = mm(o[:, m, :, :].rearrange("p a n -> p (a n)"), Qs[0:96, n, h, P * t:P * t + P],
                                      Ks[0:96, n, h // 2, P * (t + first):P * (t + 2)], start=False, stop=True,
                                      skip_group_check=True)
                if kind == "maxT":
                    last = nc.tensor.transpose(s[0:H, 0:P], rowmax[:, i, :], ident[:, :])
                if kind == "tr":
                    first = 0 if n or t else 1
                    for k in range(HG // 2):
                        o = s[:, 512 * k:512 * k + 512].rearrange("p (h a n) -> p h a n", h=2, a=2)
                        mm(o[:, :, first:2, :], ident16[:, :],
                           maskT[:, first:2, :].unsqueeze(1).broadcast_to([P, 2, 2 - first, P]),
                           start=True, stop=False, skip_group_check=True)
                        for m in range(2):
                            h = HG * g + 2 * k + m
                            for a in range(first, 2):
                                last = mm(o[:, m, a, :], Ks[:, n, h // 2, P * (t + a):P * (t + a + 1)],
                                          Qs[:, n, h, P * t:P * t + P], start=False, stop=True, skip_group_check=True)
                if kind == "back":
                    for gg in range(NHG):
                        last = nc.tensor.transpose(s[:, P * gg:P * gg + P], oT[:, gg, :], ident[:, :])
                if kind == "aoT":
                    for c in range(CH):
                        for tt in range(2):
                            last = nc.tensor.transpose(s[:, P * (2 * c + tt):P * (2 * c + tt) + P],
                                                       ao[:, 2 * i + tt, P * c:P * c + P], ident[:, :])
                if kind == "proj":
                    for tt in range(BT):
                        for c in range(CH):
                            last = mm(s[:, D * tt:D * tt + D], aoT[:, c, P * tt:P * tt + P], wo[:, c, :],
                                      start=c == 0, stop=c == CH - 1)
                pipeline.put(step, last)

            pipeline.loop(pe, NSEQ, piece)


def token_choice_layer(nc, x_in, y_out, controller, f1_in, f2_in, f1_bias, tie_in, ident_in, scratch):
    G = 16
    E, F = 64, 64
    EH = E // 2
    TT = 2 * NT
    NG = TT * P // G
    J = P // EH
    NQ = NG // J
    CH = D // P
    TP = TT // 2
    PAIRS = EH // 2
    HB = 8
    IN = PAIRS // 2
    NC = TT // 4

    plan = [("xT", n) for n in range(2 * CH)] + [("logits", 0)]

    def selection(half):
        out = [("pT", half * TP)]
        for tp in range(TP):
            if tp + 1 < TP:
                out.append(("pT", half * TP + tp + 1))
            out.append(("sel", half * TP + tp))
        return out

    def experts(half):
        h, o = [("h", 2 * half + n) for n in range(2)], [("inter", IN * half + n) for n in range(IN)]
        return [h[0], o[0], o[1], h[1]] + o[2:]

    def combination(half):
        return [("out", NC * half + n) for n in range(NC)]

    plan += selection(0) + experts(0) + selection(1) + combination(0) + experts(1) + combination(1)

    with ExitStack() as ctx:
        sb, ps, sem = allocators(nc, ctx, "l0f")
        consts = sem("consts"); setup = sem("setup")
        ident = sb("ident", [P, P])
        ctrl = sb("ctrl", [P, CH, E])
        f1 = sb("f1", [P, CH, E, F])
        f2 = sb("f2", [P, PAIRS, D])
        b1 = sb("b1", [P, E // 2])
        tie = sb("tie", [P, G])
        turned = sb("turned", [P, CH * EH * NG])
        sel = turned[:, :].rearrange("p (c e n) -> p c e n", c=CH, e=EH)
        xT = turned[:, 0:CH * TT * P].rearrange("p (c t) -> p c t", c=CH)
        wide = sb("wide", [P, 2 * TT, D])
        x, inter2, y = wide[:, 0:TT, :], wide, wide[:, TT:2 * TT, :]
        hi = sb("hi", [P, TT, D], f32r); lo = sb("lo", [P, TT, D], f32r)
        total = sb("total", [P, TT, D])
        hidden = sb("hidden", [P, 8, 2, NG])
        inter = sb("inter", [P, 2, 4, D])
        choice = sb("choice", [P, 2, NQ, G])
        spread = sb("spread", [P, 2, NQ, J, G])
        chosen = sb("chosen", [P, 2, 2, 2, P], f32r)
        best = sb("best", [P, 2, NQ])
        ln = LayerNorm(sb, sem, "ln", setup, 1, TT)
        slots = [ps(f"slot{i}", [P, 1024]) for i in range(4)]

        f1_loaded = sem("f1_loaded"); f2_loaded = sem("f2_loaded")
        x_loaded = sem("x_loaded"); x_again = sem("x_again"); stored = sem("stored")
        filled = sem("filled"); xT_ready = sem("xT_ready"); hi_ready = sem("hi_ready"); lo_ready = sem("lo_ready")
        rated = sem("rated"); best_ready = sem("best_ready"); choice_ready = sem("choice_ready"); spread_ready = [sem(f"spread_ready{half}") for half in range(2)]
        chosen_ready = sem("chosen_ready"); sel_even = sem("sel_even"); sel_odd = sem("sel_odd")
        hidden_even = sem("hidden_even"); hidden_odd = sem("hidden_odd")
        inter_even = sem("inter_even"); inter_odd = sem("inter_odd")
        left = [sem(f"left{i}") for i in range(2)]
        back = [sem(f"back{i}") for i in range(NC)]
        summed = sem("summed")

        def emptied(key):
            kind, i = key
            return {"xT": [(xT_ready, 2 * CH, i + 1)], "logits": [(rated, 2, 2)],
                    "pT": [(chosen_ready, 4 * TP, 2 * i + 2)],
                    "sel": [(sel_even, 2 * TP, i + 1), (sel_odd, 2 * TP, i + 1)],
                    "h": [(hidden_even, 2 * PAIRS, HB * (i + 1)), (hidden_odd, 2 * PAIRS, HB * (i + 1))],
                    "inter": [(inter_even, 2 * IN, i + 1), (inter_odd, 2 * IN, i + 1)],
                    "out": [(summed, 2 * NC, 2 * NC + i + 1)]}[kind]

        ring = Ring(plan, 4, emptied)

        def arrived(eng, b, key):
            eng.wait_ge(filled, ring.count(b, key))
            return slots[ring.slot(key)]

        NCONST = 4
        NSETUP = 4
        block = ctx.enter_context(nc.Block())
        f2_rows = f2_in.rearrange("(p e) f d -> (e f) p d", e=2)

        def hidden_free(eng, b, p):
            if p >= 8:
                eng.wait_ge(filled, ring.count(b, ("inter", (p - 8) // 2)))

        def inter_free(eng, b, i):
            if i >= 2:
                eng.wait_ge(left[i % 2], 16 * (IN * b + (i - 2) // 2 + 1))

        @block.sync
        def _(sp):
            sp.dma_start(ident[:, :], ident_in).then_inc(consts, 16)
            sp.dma_start(ctrl[:, :, :], controller.rearrange("(c p) e -> p c e", p=P)).then_inc(consts, 16)
            sp.dma_start(b1[:, :], f1_bias).then_inc(consts, 16)
            sp.dma_start(tie[:, :], on_all_partitions(tie_in, G)).then_inc(consts, 16)

            def load(b, s):
                sp.dma_start(wide[:, NT * s:NT * s + NT, :], tokens(x_in, 2 * b + s)).then_inc(x_loaded, 16)

            def turn(b, last):
                for half in range(2):
                    if half:
                        sp.wait_ge(filled, ring.count(b, ("inter", IN - 1)))
                    sp.dma_start(f2[:, :, :], f2_rows[:, PAIRS * half:PAIRS * half + PAIRS, :]).then_inc(f2_loaded, 16)
                    if half == 0:
                        for s in range(2):
                            sp.dma_start(total[:, NT * s:NT * s + NT, :], tokens(x_in, 2 * b + s)).then_inc(x_again, 16)
                    for n in range(IN):
                        i = IN * half + n
                        sp.wait_ge(inter_even, 2 * IN * b + i + 1)
                        sp.wait_ge(inter_odd, 2 * IN * b + i + 1)
                        sp.dma_start(scratch[half, :, 4 * n:4 * n + 4, :], inter[:, i % 2, :, :]).then_inc(left[i % 2], 16)
                    for i in range(2):
                        wait_alone(sp, left[i], 16 * (IN * b + IN // 2 * (half + 1)))
                    if half:
                        sp.wait_ge(filled, ring.count(b, ("out", NC - 1)))
                    rows = scratch[half, :, :, :].rearrange("(q j) e d -> (j e) q d", j=J)
                    for n in range(NC):
                        q = slice(NQ // NC * n, NQ // NC * (n + 1))
                        sp.dma_start(inter2[:, q, :], rows[:, q, :]).then_inc(back[n], 16)
                if not last:
                    for s in range(2):
                        wait_alone(sp, filled, ring.count(b, ("out", NC + (s + 1) * NC // 4)))
                        load(b + 1, s)
                wait_alone(sp, ln.normed, ln.done(b, 0))
                for s in range(2):
                    sp.dma_start(tokens(y_out, 2 * b + s), wide[:, TT + NT * s:TT + NT * s + NT, :]).then_inc(stored, 16)

            for s in range(2):
                load(0, s)
            for c in range(CH):
                sp.dma_start(f1[:, c, :, :], f1_in.rearrange("(c p) e f -> p c e f", p=P)[:, c, :, :]).then_inc(f1_loaded, 16)
            with sp.Fori(0, NSEQ // 2 - 1) as b:
                turn(b, False)
            turn(NSEQ // 2 - 1, True)
            sp.wait_ge(stored, 16 * NSEQ)

        @block.gpsimd
        def _(pool):
            pool.wait_ge(setup, NSETUP)
            pool.wait_ge(consts, 16 * NCONST)
            with pool.Fori(0, NSEQ // 2) as b:
                for n in range(2):
                    pool.wait_ge(hi_ready, 2 * b + n + 1)
                    part = slice(NT * n, NT * n + NT)
                    pool.tensor_tensor(lo[:, part, :], x[:, part, :], hi[:, part, :].bitcast(f32), ALU.subtract).then_inc(lo_ready, 1)
                pool.wait_ge(choice_ready, 2 * b + 2)
                wait_alone(pool, lo_ready, 2 * b + 2)
                for j in range(J):
                    if j:
                        wait_alone(pool, spread_ready[1], J * b + j)
                    rows = slice(EH * j, EH * j + EH)
                    pool.tensor_copy(spread[rows, 1, :, j, :], choice[rows, 1, :, :]).then_inc(spread_ready[1], 1)
                pool.wait_ge(spread_ready[1], J * (b + 1))
                ln.reciprocal_root(pool, b, 0)

        @block.scalar
        def _(act):
            act.wait_ge(setup, NSETUP)
            act.wait_ge(consts, 16 * NCONST)
            with act.Fori(0, NSEQ // 2) as b:
                act.wait_ge(x_loaded, 32 * b + 32)
                for n in range(2):
                    act.copy(hi[:, NT * n:NT * n + NT, :], x[:, NT * n:NT * n + NT, :]).then_inc(hi_ready, 1)
                for n in range(2 * CH):
                    c, s = n % CH, n // CH
                    act.copy(xT[:, c, T * s:T * s + T], arrived(act, b, ("xT", n))[:, :]).then_inc(xT_ready, 1)

                def take_choice(i):
                    if i % TP >= 2:
                        act.wait_ge(filled, ring.count(b, ("sel", i - 2)))
                    s = arrived(act, b, ("pT", i))[:, 0:2 * P].rearrange("p (t n) -> p t n", t=2)
                    for q in range(2):
                        rows = slice(64 * q, 64 * q + 64)
                        act.copy(chosen[rows, i % 2, :, q, :], s[rows, :, :]).then_inc(chosen_ready, 1)

                for half in range(2):
                    take_choice(half * TP)
                    for tp in range(TP):
                        i = half * TP + tp
                        if tp + 1 < TP:
                            take_choice(i + 1)
                        s = arrived(act, b, ("sel", i))[:, 0:512].rearrange("p (g e) -> p e g", e=EH)
                        act.copy(sel[:, 0, :, 16 * tp:16 * tp + 16], s).then_inc(sel_even, 1)
                    for key in experts(half):
                        s = arrived(act, b, key)
                        if key[0] == "h":
                            for n in range(HB):
                                p = HB * key[1] + n
                                hidden_free(act, b, p)
                                act.activation(hidden[0:64, p % 8, 0, :], s[0:64, NG * n:NG * n + NG], ACT.Relu,
                                               bias=b1[0:64, p:p + 1]).then_inc(hidden_even, 1)
                        else:
                            i = key[1]
                            inter_free(act, b, i)
                            act.copy(inter[:, i % 2, 0:2, :], s[:, 0:512].rearrange("p (e d) -> p e d", e=2)).then_inc(inter_even, 1)

        def combine(dve, b, half):
            if half == 0:
                dve.wait_ge(x_again, 32 * b + 32)
            else:
                dve.wait_ge(summed, 2 * NC * b + 3 * NC)
            for n in range(NC):
                s = arrived(dve, b, ("out", NC * half + n))[:, :].rearrange("p (t d) -> p t d", t=4)
                part = total[:, 4 * n:4 * n + 4, :]
                dve.tensor_tensor(part, s, part, ALU.add).then_inc(summed, 1)

        @block.vector
        def _(dve):
            dve.memset(spread[:, :, :, :, :], 0.0).then_inc(setup, 1)
            dve.memset(chosen[:, :, :, :, :].bitcast(f32), 0.0).then_inc(setup, 1)
            dve.memset(hidden[:, :, :, :], 0.0).then_inc(setup, 1)
            dve.memset(ln.half[:, :], -0.5).then_inc(setup, 1)
            dve.sem_inc(summed, 2 * NC)
            dve.wait_ge(consts, 16 * NCONST)
            with dve.Fori(0, NSEQ // 2) as b:
                s = arrived(dve, b, ("logits", 0))[:, :].rearrange("p (h q t) -> p h q t", h=2, t=G)
                for half in range(2):
                    marks, top = choice[:, half, :, :], best[:, half, :]
                    dve.tensor_tensor(marks, s[:, half, :, :], tie[:, :].unsqueeze(1).broadcast_to([P, NQ, G]), ALU.add)\
                        .then_inc(rated, 1)
                    dve.wait_ge(rated, 2 * b + half + 1)
                    dve.reduce_max(top, marks, AX).then_inc(best_ready, 1)
                    dve.wait_ge(best_ready, 2 * b + half + 1)
                    dve.tensor_tensor(marks, marks, top.unsqueeze(2).broadcast_to([P, NQ, G]), ALU.is_equal)\
                        .then_inc(choice_ready, 1)
                    if half == 0:
                        dve.wait_ge(choice_ready, 2 * b + 1)
                        for j in range(J):
                            rows = slice(EH * j, EH * j + EH)
                            dve.tensor_copy(spread[rows, 0, :, j, :], choice[rows, 0, :, :]).then_inc(spread_ready[0], 1)
                for half in range(2):
                    for tp in range(TP):
                        i = half * TP + tp
                        s = arrived(dve, b, ("sel", i))[:, 512:1024].rearrange("p (g e) -> p e g", e=EH)
                        dve.tensor_copy(sel[:, 1, :, 16 * tp:16 * tp + 16], s).then_inc(sel_odd, 1)
                    if half:
                        combine(dve, b, 0)
                    for key in experts(half):
                        s = arrived(dve, b, key)
                        if key[0] == "h":
                            for n in range(HB):
                                p = HB * key[1] + n
                                hidden_free(dve, b, p)
                                dve.tensor_scalar(hidden[64:128, p % 8, 1, :], s[64:128, NG * n:NG * n + NG],
                                                  b1[64:128, p:p + 1], 0.0, ALU.add, ALU.max).then_inc(hidden_odd, 1)
                        else:
                            i = key[1]
                            inter_free(dve, b, i)
                            dve.tensor_copy(inter[:, i % 2, 2:4, :], s[:, 512:1024].rearrange("p (e d) -> p e d", e=2))\
                                .then_inc(inter_odd, 1)
                combine(dve, b, 1)
                dve.wait_ge(summed, 2 * NC * (b + 2))
                ln.statistics(dve, total, b, 0)
                ln.normalise(dve, y, total, b, 0)

        @block.tensor
        def _(pe):
            mm = nc.tensor.matmul
            pe.wait_ge(setup, NSETUP)
            pe.wait_ge(consts, 16 * NCONST)
            with pe.Fori(0, NSEQ // 2) as b:
                def use(key):
                    ring.wait_free(pe, b, key)
                    return slots[ring.slot(key)]

                def transpose_choice(i):
                    half, tp = i // TP, i % TP
                    s = use(("pT", i))
                    if tp == 0:
                        pe.wait_ge(spread_ready[half], J * (b + 1))
                    for t in range(2):
                        q = 2 * (2 * tp + t)
                        last = nc.tensor.transpose(s[:, P * t:P * t + P],
                                                   spread[:, half, q:q + 2, :, :].rearrange("p q j t -> p (q j t)"), ident[:, :])
                    last.then_inc(filled, 1)

                def select(i):
                    tp = i % TP
                    s = use(("sel", i))
                    pe.wait_ge(chosen_ready, 4 * TP * b + 2 * i + 2)
                    for c in range(CH):
                        for t in range(2):
                            o = s[:, 512 * c + 256 * t:512 * c + 256 * t + 256]
                            rhs = chosen[:, i % 2, t, :, :].rearrange("p q n -> p (q n)")
                            for part in (hi, lo):
                                last = mm(o, part[:, 2 * tp + t, P * c:P * c + P], rhs, start=part is hi, stop=part is lo)
                    last.then_inc(filled, 1)

                def expert(key):
                    s = use(key)
                    i = key[1]
                    if key[0] == "h":
                        if i % 2 == 0:
                            pe.wait_ge(f1_loaded, 16 * CH)
                            pe.wait_ge(sel_even, 2 * TP * b + TP * (i // 2 + 1))
                            pe.wait_ge(sel_odd, 2 * TP * b + TP * (i // 2 + 1))
                        for n in range(HB):
                            e0 = 2 * (HB * i + n)
                            for c in range(CH):
                                for k in range(2):
                                    last = mm(s[64 * k:64 * k + 64, NG * n:NG * n + NG], f1[:, c, e0 + k, :],
                                              sel[:, c, (e0 + k) % EH, :], start=c == 0, stop=c == CH - 1)
                    else:
                        for n in range(2):
                            p = 2 * i + n
                            pe.wait_ge(hidden_even, 2 * PAIRS * b + p + 1)
                            pe.wait_ge(hidden_odd, 2 * PAIRS * b + p + 1)
                            if i % IN == 0 and n == 0:
                                pe.wait_ge(f2_loaded, 16 * (2 * b + i // IN + 1))
                            for k in range(2):
                                last = mm(s[:, D * (2 * n + k):D * (2 * n + k + 1)], hidden[:, p % 8, k, :], f2[:, p % PAIRS, :],
                                          start=True, stop=True)
                    last.then_inc(filled, 1)

                def combine_on_pe(half):
                    for n in range(NC):
                        s = use(("out", NC * half + n))
                        pe.wait_ge(back[n], 16 * (2 * b + half + 1))
                        for t in range(4):
                            for k in range(2):
                                q = 2 * (4 * n + t) + k
                                last = mm(s[64 * k:64 * k + 64, D * t:D * t + D],
                                          spread[:, half, q, :, :].rearrange("p j t -> p (j t)"), inter2[:, q, :],
                                          start=True, stop=True)
                        last.then_inc(filled, 1)

                pe.wait_ge(summed, 2 * NC * (b + 1))
                pe.wait_ge(x_loaded, 32 * b + 32)
                for n in range(2 * CH):
                    c, sq = n % CH, n // CH
                    s = use(("xT", n))
                    for t in range(NT):
                        last = nc.tensor.transpose(s[:, P * t:P * t + P], x[:, NT * sq + t, P * c:P * c + P], ident[:, :])
                    last.then_inc(filled, 1)
                s = use(("logits", 0))
                pe.wait_ge(xT_ready, 2 * CH * (b + 1))
                for half in range(2):
                    for c in range(CH):
                        by_quad = xT[:, c, :].rearrange("p (q j t) -> p q j t", j=J, t=G)
                        for j in range(J):
                            last = mm(s[EH * j:EH * j + EH, 512 * half:512 * half + 512], ctrl[:, c, EH * half:EH * half + EH],
                                      by_quad[:, :, j, :], start=c == 0, stop=c == CH - 1, tile_position=(0, EH * j))
                last.then_inc(filled, 1)
                for half in range(2):
                    if half == 0:
                        pe.wait_ge(lo_ready, 2 * b + 2)
                    for kind, i in selection(half):
                        (transpose_choice if kind == "pT" else select)(i)
                    if half:
                        combine_on_pe(0)
                    for key in experts(half):
                        expert(key)
                combine_on_pe(1)


def linear_attention_layer(nc, x_in, y_out, wqkvT, wprojT, bproj, ident_in, head_blocks_in):
    DH = 16
    HC = P // DH
    CH = D // P
    EPS = 1e-6
    W1 = P + HC
    PAIRS = NT // 2

    plan = [("xT", c) for c in range(CH)] + [("q", c) for c in range(CH)] + [("kv", g) for g in range(PAIRS)]
    plan += ["state"] + [("mix", g) for g in range(PAIRS)] + [("aoT", c) for c in range(CH)] + [("proj", g) for g in range(2)]

    with ExitStack() as ctx:
        sb, ps, sem = allocators(nc, ctx, "l1a")
        wqkv = sb("wqkv", [P, CH, 3 * D]); wproj = sb("wproj", [P, CH, D])
        bias = sb("bias", [P, D])
        ident = sb("ident", [P, P])
        head_blocks = sb("head_blocks", [P, W1])
        consts = sem("consts"); setup = sem("setup")

        class Stream:
            def __init__(self, s):
                def buf(name, shape):
                    return sb(f"{name}{s}", shape)

                def sig(name):
                    return sem(f"{name}{s}")

                self.s = s
                self.x = buf("x", [P, NT, D])
                self.sum = buf("sum", [P, NT, D])
                self.y = buf("y", [P, NT, D])
                self.xT = buf("xT", [P, CH, T])
                self.exp_q = buf("exp_q", [P, CH, T]); self.exp_k = buf("exp_k", [P, NT, D])
                self.qT = buf("qT", [P, CH, T]); self.k = buf("k", [P, NT, D])
                self.v1 = buf("v1", [P, NT, CH, P + 1])
                self.state = buf("state", [P, CH, W1])
                self.z = buf("z", [P, PAIRS, 2, CH, HC])
                self.ao = buf("ao", [P, NT, D]); self.aoT = buf("aoT", [P, CH, T])
                self.ln = LayerNorm(sb, sem, f"ln{s}", setup, 1)
                self.slots = [ps(f"slot{s}{i}", [P, 1024]) for i in range(2)]
                self.x_loaded = sig("x_loaded"); self.stored = sig("stored")
                self.filled = sig("filled"); self.xT_ready = sig("xT_ready"); self.v_ready = sig("v_ready")
                self.exp_ready = sig("exp_ready"); self.clipped = sig("clipped"); self.features = sig("features")
                self.state_ready = sig("state_ready"); self.den_ready = sig("den_ready"); self.z_ready = sig("z_ready")
                self.mixed = sig("mixed"); self.aoT_ready = sig("aoT_ready"); self.biased = sig("biased")
                self.summed = sig("summed")
                self.ring = Ring(plan, 2, self.emptied)

            def emptied(self, key):
                if key == "state":
                    return [(self.state_ready, 2 * CH, 2 * CH)]
                kind, i = key
                return [{"xT": (self.xT_ready, CH, i + 1), "q": (self.features, CH + PAIRS, i + 1),
                        "kv": (self.features, CH + PAIRS, CH + i + 1), "mix": (self.mixed, PAIRS, i + 1),
                        "aoT": (self.aoT_ready, CH, i + 1)}[kind]]

            def slot(self, key):
                return self.slots[self.ring.slot(key)]

        streams = [Stream(s) for s in range(2)]
        block = ctx.enter_context(nc.Block())

        def arrived(eng, st, b, key):
            eng.wait_ge(st.filled, st.ring.count(b, key))
            return st.slot(key)

        def run(steps, b):
            for step in steps:
                for st in streams:
                    step(st, b)

        NCONST = 5

        @block.sync
        def _(sp):
            sp.dma_start(ident[:, :], ident_in).then_inc(consts, 16)
            sp.dma_start(wqkv[:, :, :], wqkvT.rearrange("(c p) n -> p c n", p=P)).then_inc(consts, 16)
            sp.dma_start(wproj[:, :, :], wprojT.rearrange("(c p) n -> p c n", p=P)).then_inc(consts, 16)
            sp.dma_start(bias[:, :], on_all_partitions(bproj, D)).then_inc(consts, 16)
            sp.dma_start(head_blocks[:, :], head_blocks_in).then_inc(consts, 16)

            def load(st, b):
                sp.dma_start(st.x[:, :, :], tokens(x_in, 2 * b + st.s)).then_inc(st.x_loaded, 16)

            def load_next(st, b):
                wait_alone(sp, st.xT_ready, CH * b + CH)
                wait_alone(sp, st.biased, b + 1)
                load(st, b + 1)

            def store(st, b):
                wait_alone(sp, st.ln.normed, st.ln.done(b, 0))
                sp.dma_start(tokens(y_out, 2 * b + st.s), st.y[:, :, :]).then_inc(st.stored, 16)

            run([load], 0)
            with sp.Fori(0, NSEQ // 2 - 1) as b:
                run([load_next, store], b)
            run([store], NSEQ // 2 - 1)
            for st in streams:
                sp.wait_ge(st.stored, 16 * (NSEQ // 2) + 16)

        @block.gpsimd
        def _(pool):
            pool.wait_ge(setup, 4)
            pool.wait_ge(consts, 16 * NCONST)

            def clip(st, b):
                for i in range(CH + PAIRS - 1):
                    wait_alone(pool, st.exp_ready, b * (CH + PAIRS) + i + 1)
                    part = st.exp_q[:, i, :] if i < CH else st.exp_k[:, 2 * (i - CH):2 * (i - CH) + 2, :]
                    pool.tensor_scalar(part, part, 1.0, None, ALU.min).then_inc(st.clipped, 1)

            def bias_x(st, b):
                pool.wait_ge(st.x_loaded, 16 * b + 16)
                pool.wait_ge(st.features, b * (CH + PAIRS) + 1)
                pool.tensor_tensor(st.sum[:, :, :], st.x[:, :, :], each_tile(bias), ALU.add).then_inc(st.biased, 1)

            def norm(st, b):
                st.ln.reciprocal_root(pool, b, 0)

            with pool.Fori(0, NSEQ // 2) as b:
                run([clip, bias_x, norm], b)

        @block.scalar
        def _(act):
            act.wait_ge(setup, 4)
            act.wait_ge(consts, 16 * NCONST)

            def copy_xT(st, b):
                for c in range(CH):
                    act.copy(st.xT[:, c, :], arrived(act, st, b, ("xT", c))[:, :]).then_inc(st.xT_ready, 1)

            def exp_q(st, b):
                for c in range(CH):
                    act.activation(st.exp_q[:, c, :], arrived(act, st, b, ("q", c))[:, :], ACT.Exp).then_inc(st.exp_ready, 1)

            def exp_k(st, b):
                for g in range(PAIRS):
                    kv = arrived(act, st, b, ("kv", g))[:, :].rearrange("p (t n) -> p t n", t=2)
                    for t in range(2):
                        act.copy(st.v1[:, 2 * g + t, :, 0:P], kv[:, t, D:2 * D].rearrange("p (c n) -> p c n", c=CH))\
                            .then_inc(st.v_ready, 1)
                    act.activation(st.exp_k[:, 2 * g:2 * g + 2, :], kv[:, :, 0:D], ACT.Exp).then_inc(st.exp_ready, 1)

            def copy_aoT(st, b):
                for c in range(CH):
                    act.copy(st.aoT[:, c, :], arrived(act, st, b, ("aoT", c))[:, :]).then_inc(st.aoT_ready, 1)

            with act.Fori(0, NSEQ // 2) as b:
                run([copy_xT, exp_q, exp_k, copy_aoT], b)

        @block.vector
        def _(dve):
            for st in streams:
                dve.memset(st.v1[:, :, :, P:P + 1], 1.0).then_inc(setup, 1)
                dve.memset(st.ln.half[:, :], -0.5).then_inc(setup, 1)
            for st in streams:
                dve.sem_inc(st.stored, 16)
                dve.sem_inc(st.summed, 2)
            dve.wait_ge(consts, 16 * NCONST)

            def features(st, b):
                for i in range(CH + PAIRS):
                    if i < CH:
                        x, e, o = arrived(dve, st, b, ("q", i))[:, :], st.exp_q[:, i, :], st.qT[:, i, :]
                    else:
                        g = i - CH
                        x = arrived(dve, st, b, ("kv", g))[:, :].rearrange("p (t n) -> p t n", t=2)[:, :, 0:D]
                        e, o = st.exp_k[:, 2 * g:2 * g + 2, :], st.k[:, 2 * g:2 * g + 2, :]
                    if i == CH + PAIRS - 1:
                        dve.wait_ge(st.exp_ready, (b + 1) * (CH + PAIRS))
                        dve.tensor_scalar(e, e, 1.0, None, ALU.min).then_inc(st.clipped, 1)
                    dve.wait_ge(st.clipped, b * (CH + PAIRS) + i + 1)
                    dve.scalar_tensor_tensor(o, x, 0.0, e, ALU.max, ALU.add).then_inc(st.features, 1)

            def state(st, b):
                s = arrived(dve, st, b, "state")
                for c in range(CH):
                    dve.tensor_tensor(st.state[:, c, 0:P], s[:, 512 * c:512 * c + P], head_blocks[:, 0:P], ALU.mult)\
                        .then_inc(st.state_ready, 1)
                    dve.tensor_scalar(st.state[:, c, P:W1], head_blocks[:, P:W1], s[:, 512 * c + P:512 * c + P + 1], None,
                                      ALU.mult).then_inc(st.state_ready, 1)

            def mix(st, b):
                for g in range(PAIRS):
                    s = arrived(dve, st, b, ("mix", g))[:, :].rearrange("p (t n) -> p t n", t=2)[:, :, 0:CH * W1]\
                        .rearrange("p t (c n) -> p t c n", c=CH)
                    z = st.z[:, g, :, :, :]
                    dve.tensor_scalar(z, s[:, :, :, P:W1], EPS, None, ALU.add).then_inc(st.den_ready, 1)
                    dve.wait_ge(st.den_ready, PAIRS * b + g + 1)
                    dve.reciprocal(z, z).then_inc(st.z_ready, 1)
                    dve.wait_ge(st.z_ready, PAIRS * b + g + 1)
                    for t in range(2):
                        for c in range(CH):
                            ins = dve.tensor_tensor(
                                st.ao[:, 2 * g + t, P * c:P * c + P].rearrange("p (h n) -> p h n", h=HC),
                                s[:, t, c, 0:P].rearrange("p (h n) -> p h n", h=HC),
                                z[:, t, c, :].unsqueeze(2).broadcast_to([P, HC, DH]), ALU.mult)
                    ins.then_inc(st.mixed, 1)

            def residual(st, b):
                for g in range(2):
                    s = arrived(dve, st, b, ("proj", g))[:, :].rearrange("p (t n) -> p t n", t=4)
                    dve.wait_ge(st.biased, b + 1)
                    part = st.sum[:, 4 * g:4 * g + 4, :]
                    dve.tensor_tensor(part, s, part, ALU.add).then_inc(st.summed, 1)
                dve.wait_ge(st.summed, 2 * b + 4)
                st.ln.statistics(dve, st.sum, b, 0)

            def norm(st, b):
                dve.wait_ge(st.stored, 16 * b + 16)
                st.ln.normalise(dve, st.y, st.sum, b, 0)

            with dve.Fori(0, NSEQ // 2) as b:
                run([features, state, mix, residual, norm], b)

        @block.tensor
        def _(pe):
            mm = nc.tensor.matmul
            pe.wait_ge(setup, 4)
            pe.wait_ge(consts, 16 * NCONST)

            def use(st, b, key):
                st.ring.wait_free(pe, b, key)
                return st.slot(key)

            def transpose_x(st, b):
                pe.wait_ge(st.x_loaded, 16 * b + 16)
                pe.wait_ge(st.summed, 2 * b + 2)
                for c in range(CH):
                    s = use(st, b, ("xT", c))
                    for t in range(NT):
                        last = nc.tensor.transpose(s[:, P * t:P * t + P], st.x[:, t, P * c:P * c + P], ident[:, :])
                    last.then_inc(st.filled, 1)

            def project_q(st, b):
                pe.wait_ge(st.xT_ready, CH * b + CH)
                for c in range(CH):
                    s = use(st, b, ("q", c))
                    for half in range(2):
                        cols = slice(512 * half, 512 * half + 512)
                        for k in range(CH):
                            last = mm(s[:, cols], wqkv[:, k, P * c:P * c + P], st.xT[:, k, cols], start=k == 0, stop=k == CH - 1)
                    last.then_inc(st.filled, 1)

            def project_kv(st, b):
                for g in range(PAIRS):
                    s = use(st, b, ("kv", g))
                    for t in range(2):
                        tok = P * (2 * g + t)
                        for k in range(CH):
                            last = mm(s[:, 512 * t:512 * t + 512], st.xT[:, k, tok:tok + P], wqkv[:, k, D:3 * D],
                                      start=k == 0, stop=k == CH - 1)
                    last.then_inc(st.filled, 1)

            def sum_state(st, b):
                s = use(st, b, "state")
                pe.wait_ge(st.v_ready, NT * b + NT)
                pe.wait_ge(st.features, (b + 1) * (CH + PAIRS))
                for c in range(CH):
                    for t in range(NT):
                        last = mm(s[:, 512 * c:512 * c + P + 1], st.k[:, t, P * c:P * c + P], st.v1[:, t, c, :],
                                  start=t == 0, stop=t == NT - 1)
                last.then_inc(st.filled, 1)

            def mix(st, b):
                pe.wait_ge(st.state_ready, (b + 1) * 2 * CH)
                for g in range(PAIRS):
                    s = use(st, b, ("mix", g))
                    for t in range(2):
                        tok = P * (2 * g + t)
                        for c in range(CH):
                            at = 512 * t + W1 * c
                            last = mm(s[:, at:at + W1], st.qT[:, c, tok:tok + P], st.state[:, c, :], start=True, stop=True)
                    last.then_inc(st.filled, 1)

            def transpose_ao(st, b):
                pe.wait_ge(st.mixed, PAIRS * (b + 1))
                for c in range(CH):
                    s = use(st, b, ("aoT", c))
                    for t in range(NT):
                        last = nc.tensor.transpose(s[:, P * t:P * t + P], st.ao[:, t, P * c:P * c + P], ident[:, :])
                    last.then_inc(st.filled, 1)

            def project_out(st, b):
                pe.wait_ge(st.aoT_ready, CH * (b + 1))
                for g in range(2):
                    s = use(st, b, ("proj", g))
                    for t in range(4):
                        tok = P * (4 * g + t)
                        for k in range(CH):
                            last = mm(s[:, D * t:D * t + D], st.aoT[:, k, tok:tok + P], wproj[:, k, :], start=k == 0, stop=k == CH - 1)
                    last.then_inc(st.filled, 1)

            with pe.Fori(0, NSEQ // 2) as b:
                run([transpose_x, project_q, project_kv, sum_state, mix, transpose_ao, project_out], b)
def nested_width_attention_layer(nc, x_in, y_out, q_wT, q_b, k_wT, k_b, v_wT, v_b, o_wT, o_b, norm_w, norm_b, ident_in, scratch):
    H, DH = 8, 32
    NE = 4
    QW = T // NE
    SCALE = float(D) ** -0.5
    width = [D >> e for e in range(NE)]
    BATCHES = [[(h, 0) for h in range(4)], [(h, 0) for h in range(4, 8)], [(h, 1) for h in range(4)],
               [(0, 2), (1, 2), (0, 3)]]
    UNITS = [u for batch in BATCHES for u in batch]
    FIRST = [sum(len(b) for b in BATCHES[:i]) for i in range(len(BATCHES))]
    NB = len(BATCHES)

    USED = {(c, "k"): T for c in range(2)} | {(0, "q"): T, (1, "q"): QW}
    PROJECTIONS = [("k", 0), ("q", 0), ("k", 1), ("q", 1)]

    def nat(i):
        return [("nat", FIRST[i] + u, t) for u in range(len(BATCHES[i])) for t in range(2)]

    def tr(i):
        return [("tr", FIRST[i] + u, half) for half in range(2) for u in range(len(BATCHES[i]))]

    def pv(i, half):
        return [("pv", i, NT // 2 * half + j) for j in range(NT // 2)]

    def ahead(steps):
        return [("ahead",) + s for s in steps]

    def merged(*streams):
        keyed = [((j + 0.5) / len(s), i, step) for i, s in enumerate(streams) for j, step in enumerate(s)]
        return [step for _, _, step in sorted(keyed, key=lambda k: k[:2])]

    front = [("xT", 0), ("xT", 1), ("xT", 2), ("load",), ("k", 0), ("q", 0), ("k", 1), ("q", 1), ("statistics",), ("v", 0), ("v", 1), ("rest of q",), ("normalise",)]
    steps = [("again",)]
    steps += merged(tr(1)[:4], nat(3)[:2], pv(0, 1), ahead(front[:4]))
    steps += merged(tr(1)[4:], nat(3)[2:], pv(1, 0), ahead(front[4:6]))
    steps += merged(tr(2)[:4], pv(1, 1), ahead(front[6:9])) + [("mT", 3)]
    steps += merged(tr(2)[4:], pv(2, 0), ahead(front[9:12]), ahead(nat(0)[:3]))
    steps += merged(tr(3)[:3], ahead(nat(0)[3:6]), pv(2, 1))
    steps += merged(tr(3)[3:], ahead(nat(0)[6:] + nat(1)[:1])) + ahead([("mT", 0)]) + pv(3, 0)[:2] + ahead(nat(1)[1:2])
    steps += pv(3, 0)[2:] + ahead(nat(1)[2:4]) + pv(3, 1)[:2] + ahead(nat(1)[4:5]) + pv(3, 1)[2:] + ahead(nat(1)[5:])
    steps += [("out", 0), ("out", 1)] + ahead([("mT", 1)])
    steps += ahead(tr(0)[:1] + nat(2)[:1] + tr(0)[1:3]) + [("finish",)] + ahead(tr(0)[3:4] + nat(2)[1:2])
    steps += ahead(merged(tr(0)[4:], nat(2)[2:5], front[12:])) + ahead(merged(nat(2)[5:], pv(0, 0)) + [("mT", 2)])
    lead = [s[1:] for s in steps if s[0] == "ahead"]

    unslotted = ("statistics", "normalise", "load", "again", "pv", "rest of q", "finish")
    plan = [s for s in steps if s[0] not in unslotted and s[1] not in unslotted]
    NSLOT = 3
    assert len(plan) % NSLOT == 0
    assert all(key[0] == "ahead" for key in plan[-NSLOT:])
    at = {key: i for i, key in enumerate(plan)}
    lead_at = {key[1:]: i for i, key in enumerate(k for k in plan if k[0] == "ahead")}
    rest_at = {key: i for i, key in enumerate(k for k in plan if k[0] != "ahead")}
    max_at = {s[1:]: i for i, s in enumerate(nat(0) + nat(1) + nat(2) + nat(3))}
    exp_at = {s[1:]: i for i, s in enumerate(tr(0) + tr(1) + tr(2) + tr(3))}

    with ExitStack() as ctx:
        sb, ps, sem = allocators(nc, ctx, "l1f")
        consts = sem("consts"); setup = sem("setup"); cleared = sem("cleared"); cleared_too = sem("cleared_too")
        xn = sb("xn", [P, NT, D])
        total = sb("total", [P, NT, D])
        xT = [sb("xT0", [P, T]), sb("xT1", [P, QW])]
        hi = sb("hi", [P, 2, T], f32r); lo = sb("lo", [P, 2, T], f32r)
        Qs = sb("Qs", [P, 2, len(UNITS), QW], f32r)
        Ks = sb("Ks", [P, 2, H, T], f32r)
        V = sb("V", [P, 2, NT, D])
        probs = sb("probs", [P, 2, 4, NT // 2 * QW])
        recip = sb("recip", [P, 2, QW])
        aoT = [sb("aoT0", [P, T]), sb("aoT1", [P, QW])]
        wq = sb("wq", [P, 2, D]); wk = sb("wk", [P, 2, D]); wv = sb("wv", [P, 2, D]); wo = sb("wo", [P, 2, D])
        qb = sb("qb", [P, 2]); kb = sb("kb", [P, 2]); vb = sb("vb", [P, D]); nw = sb("nw", [P, 2]); nb = sb("nb", [P, 2])
        ob = sb("ob", [P, NE, D])
        ident = sb("ident", [P, P])
        ones = sb("ones", [P, DH])
        rowmax = sb("rowmax", [P, 2 * len(UNITS)])
        maxT = sb("maxT", [8, 2, P], f32r)
        first_ln = LayerNorm(sb, sem, "first", setup, 1)
        own_ln = LayerNorm(sb, sem, "own", setup, 1)
        slots = [ps(f"slot{i}", [P, 1024]) for i in range(NSLOT)]
        OS = [ps(f"os{i}", [P, 2, QW]) for i in range(2)]
        SHIFT_ROW = 3 * DH

        def signal(name, per, step=1):
            return Signal(sem(name), per, step)

        x_loaded = signal("x_loaded", 1, 16); x_again = signal("x_again", 1, 16); stored = signal("stored", 1, 16)
        doubled = sem("doubled"); x2_ready = signal("x2_ready", NE)
        xT_ready = [signal(f"xT{i}_ready", n) for i, n in enumerate((1, 2, 1))]
        lead_filled = signal("lead_filled", len(lead_at)); filled = signal("filled", len(rest_at))
        hi_ready = signal("hi_ready", 4); lo_ready = signal("lo_ready", 4); v_ready = signal("v_ready", 2)
        bounced = {p: signal(f"bounced_{p[0]}{p[1]}", 2, 16) for p in PROJECTIONS}
        stacked = [signal(f"stacked{c}", 6, 16) for c in range(2)]
        rest_stacked = signal("rest_stacked", 9, 16)
        max_done = signal("max_done", len(max_at)); maxT_ready = signal("maxT_ready", NB)
        placed = [signal(f"placed{i}", NB // 2, 16) for i in range(2)]
        exp_done = signal("exp_done", len(exp_at)); pv_done = signal("pv_done", 2 * NB)
        recip_ready = signal("recip_ready", NB); ao_ready = signal("ao_ready", NB + 1)
        summed = signal("summed", NE)

        def arrived(eng, B, key, is_ahead):
            if is_ahead:
                lead_filled.wait(eng, B, lead_at[key] + 1)
                return slots[at[("ahead",) + key] % NSLOT]
            filled.wait(eng, B, rest_at[key] + 1)
            return slots[at[key] % NSLOT]

        def runs(key, is_ahead):
            return {"alone": key[0] == "ahead", None: key[0] != "ahead"}.get(is_ahead, True)

        def use(pe, B, key, is_ahead):
            i = at[("ahead",) + key if is_ahead else key]
            R = B - 1 if is_ahead else B
            here = [j for j in range(i) if j % NSLOT == i % NSLOT and runs(plan[j], is_ahead)]
            if here:
                old = here[-1]
            elif is_ahead == "alone":
                return slots[i % NSLOT]
            else:
                old, R = len(plan) - NSLOT + i % NSLOT, R - 1
            was = plan[old]
            if was[0] == "ahead":
                was, R = was[1:], R + 1
            kind = was[0]
            read, count = {"nat": lambda: (max_done, max_at[was[1:]] + 1), "tr": lambda: (exp_done, exp_at[was[1:]] + 1),
                           "mT": lambda: (maxT_ready, was[1] + 1), "out": lambda: (summed, (1, NE)[was[1]]),
                           "xT": lambda: (xT_ready[was[1]], None), "v": lambda: (v_ready, was[1] + 1),
                           "k": lambda: (lo_ready, 2 * was[1] + 1), "q": lambda: (lo_ready, 2 * was[1] + 2)}[kind]()
            read.wait(pe, R, count)
            return slots[i % NSLOT]

        def loop(eng, piece):
            def body(b, last):
                for n in range(2):
                    for step in steps:
                        if step[0] == "ahead":
                            if not (last and n == 1):
                                piece(step[1:], 2 * b + n + 1, 1 - n, not last, True)
                        else:
                            piece(step, 2 * b + n, n, True, None if last and n == 1 else False)

            for step in lead:
                piece(step, 0, 0, True, "alone")
            with eng.Fori(0, NSEQ // 2 - 1) as b:
                body(b, False)
            body(NSEQ // 2 - 1, True)

        NCONST = 14
        NSETUP = 5
        block = ctx.enter_context(nc.Block())

        @block.sync
        def _(sp):
            sp.dma_start(xn[:, :, :], tokens(x_in, 0)).then_inc(x_loaded.sem, 16)
            for w, src in ((wk, k_wT), (wq, q_wT), (wv, v_wT), (wo, o_wT)):
                sp.dma_start(w[:, :, :], src.rearrange("(c p) n -> p c n", p=P)).then_inc(consts, 16)
            for v, src in ((qb, q_b), (kb, k_b), (nw, norm_w), (nb, norm_b), (ident, ident_in)):
                sp.dma_start(v[:, :], src).then_inc(consts, 16)
            sp.dma_start(vb[:, :], on_all_partitions(v_b, D)).then_inc(consts, 16)
            sp.wait_ge(setup, NSETUP)
            for e in range(NE):
                sp.dma_start(ob[:, e, 0:width[e]], on_all_partitions(o_b, width[e])).then_inc(consts, 16)
            for s in (x_again, stored, x_loaded, *bounced.values(), *stacked, rest_stacked):
                s.start(sp)

            def piece(step, B, parity, next_too, is_ahead):
                kind = step[0]
                if kind == "load" and next_too:
                    for r in xT_ready:
                        r.wait(sp, B)
                    alone(sp)
                    x_loaded.by(sp.dma_start(xn[:, :, :], tokens(x_in, B + 1)))
                if kind == "again":
                    stored.wait(sp, B - 1)
                    alone(sp)
                    x_again.by(sp.dma_start(total[:, :, :], tokens(x_in, B)))
                if kind in ("k", "q"):
                    p = step
                    j, c = "kq".index(kind), step[1]
                    used = USED[(c, kind)]
                    stacked[c].wait(sp, B - 1)
                    if p == ("q", 0):
                        rest_stacked.wait(sp, B - 1)
                    alone(sp)
                    lo_ready.wait(sp, B, PROJECTIONS.index(p) + 1)
                    for part, source in enumerate((hi, lo)):
                        bounced[p].by(sp.dma_start(scratch[j, part, P * c:P * c + P, 0:used], words(source[:, j, 0:used])))
                    bounced[p].wait(sp, B)
                    exp_done.wait(sp, B - 2)
                    alone(sp)
                    for r in range(3):
                        rows = slice(DH * r, DH * r + DH)
                        if kind == "k":
                            src = scratch[0, (0, 0, 1)[r], P * c:P * c + P, :]
                            stacked[c].by(sp.dma_start(words(Ks[rows, parity, 4 * c:4 * c + 4, :]),
                                                       src.rearrange("(h d) t -> d h t", d=DH)))
                        else:
                            src = scratch[1, (0, 1, 0)[r], P * c:P * c + P, :]
                            u = FIRST[c]
                            stacked[c].by(sp.dma_start(words(Qs[rows, parity, u:u + 4, :]),
                                                       src[:, 0:QW].rearrange("(h d) t -> d h t", d=DH)))
                if kind == "rest of q":
                    for u, n, e in ((8, 4, 1), (12, 2, 2), (14, 1, 3)):
                        for r in range(3):
                            src = scratch[1, (0, 1, 0)[r], 0:DH * n, QW * e:QW * e + QW]
                            rest_stacked.by(sp.dma_start(words(Qs[DH * r:DH * r + DH, parity, u:u + n, :]),
                                                         src.rearrange("(h d) t -> d h t", d=DH)))
                if kind == "mT":
                    i = step[1]
                    if is_ahead == "alone" and i == 0:
                        sp.wait_ge(cleared, 1); sp.wait_ge(cleared_too, 2)
                    maxT_ready.wait(sp, B, i + 1)
                    n = len(BATCHES[i])
                    placed[i % 2].by(sp.dma_start(
                        words(Qs[SHIFT_ROW:SHIFT_ROW + 1, parity, FIRST[i]:FIRST[i] + n, :])
                        .rearrange("o u (t q) -> o (u t) q", q=P), words(maxT[0:2 * n, i % 2, :])))
                if kind == "finish":
                    wait_alone(sp, own_ln.normed, own_ln.done(B, 0))
                    stored.by(sp.dma_start(tokens(y_out, B), total[:, :, :]))

            for s in placed:
                s.start(sp)
            loop(sp, piece)
            stored.wait(sp, NSEQ - 1)

        @block.gpsimd
        def _(pool):
            x2_ready.start(pool)
            pool.memset(Ks[96:128, 1, :, :].bitcast(f32), -1.0).then_inc(cleared_too, 1)
            pool.wait_ge(cleared_too, 1)
            pool.wait_ge(setup, NSETUP)
            pool.wait_ge(consts, 16 * NCONST)

            def piece(step, B, parity, next_too, is_ahead):
                if step[0] == "statistics" and next_too:
                    first_ln.reciprocal_root(pool, B + 1, 0)
                if step[0] == "again":
                    x_again.wait(pool, B)
                    pool.tensor_tensor(total[:, :, :], total[:, :, :], total[:, :, :], ALU.add).then_inc(doubled, 1)
                    pool.wait_ge(doubled, B + 1)
                    for e in range(NE):
                        x2_ready.by(pool.tensor_tensor(total[:, 2 * e:2 * e + 2, :], total[:, 2 * e:2 * e + 2, :],
                                                       ob[:, e:e + 1, :].broadcast_to([P, 2, D]), ALU.add))
                if step[0] == "finish":
                    own_ln.reciprocal_root(pool, B, 0)
                    own_ln.normalise(pool, total, total, B, 0)

            first_ln.reciprocal_root(pool, 0, 0)
            pool.wait_ge(first_ln.rstd_ready, 1)
            pool.memset(Qs[96:128, :, :, :].bitcast(f32), 0.0).then_inc(cleared_too, 1)
            pool.wait_ge(cleared_too, 2)
            loop(pool, piece)

        @block.scalar
        def _(act):
            for s in (xT_ready[0], xT_ready[1], hi_ready, exp_done):
                s.start(act)
            act.wait_ge(setup, NSETUP)
            act.wait_ge(consts, 16 * NCONST)

            def piece(step, B, parity, next_too, is_ahead):
                kind = step[0]
                if kind == "xT" and step[1] < 2:
                    s = arrived(act, B, step, is_ahead)
                    v_ready.wait(act, B - 1)
                    for rows, to, col in (((P, 0, 0), ) if step[1] == 0 else ((64, 512, 0), (32, 768, 256))):
                        n = 512 if rows == P else 256
                        xT_ready[step[1]].by(act.activation(xT[0][0:rows, to:to + n], s[0:rows, col:col + n], ACT.Identity,
                                                            bias=nb[0:rows, 0:1], scale=nw[0:rows, 0:1]))
                if kind in ("k", "q"):
                    c = step[1]
                    used = USED[(c, kind)]
                    bias = kb if kind == "k" else qb
                    s = arrived(act, B, step, is_ahead)
                    before = (kind, 1 - c)
                    bounced[before].wait(act, B - (c == 0))
                    hi_ready.by(act.activation(hi[:, "kq".index(kind), 0:used], s[:, 0:used], ACT.Identity,
                                               bias=bias[:, c:c + 1]))
                if kind == "tr":
                    _, u, half = step
                    i = max(i for i in range(NB) if FIRST[i] <= u)
                    s = arrived(act, B, step, is_ahead)
                    if u == FIRST[i]:
                        if i:
                            pv_done.wait(act, B, 2 * (i - 1) + half + 1)
                        else:
                            pv_done.wait(act, B - 1, 2 * (NB - 1) + half + 1)
                    exp_done.by(act.activation(probs[:, half, u - FIRST[i], :], s[:, :], ACT.Exp, scale=SCALE))

            loop(act, piece)

        @block.vector
        def _(dve):
            for s in (xT_ready[2], lo_ready, v_ready, max_done, maxT_ready, recip_ready, ao_ready, summed):
                s.start(dve)
            dve.memset(ob[:, :, :], 0.0).then_inc(setup, 1)
            dve.memset(ones[:, :], 1.0).then_inc(setup, 1)
            dve.memset(first_ln.half[:, :], -0.5).then_inc(setup, 1)
            dve.memset(own_ln.half[:, :], -0.5).then_inc(setup, 1)
            dve.memset(xT[0][:, :], 0.0).then_inc(setup, 1)
            dve.memset(Ks[96:128, 0, :, :].bitcast(f32), -1.0).then_inc(cleared, 1)

            def statistics(B):
                x_loaded.wait(dve, B)
                first_ln.statistics(dve, xn, B, 0)

            statistics(0)
            first_ln.normalise(dve, xn, xn, 0, 0)
            dve.wait_ge(consts, 16 * NCONST)

            def norms(B, i):
                pv_done.wait(dve, B, 2 * i + 2)
                os = OS[i % 2]
                rows = DH * len(BATCHES[i])
                recip_ready.by(dve.reciprocal(recip[0:rows, i % 2, :], os[0:rows, 1, :]))
                recip_ready.wait(dve, B, i + 1)
                for dst, rows in (((aoT[i % 2][:, QW * (i // 2):QW * (i // 2) + QW], slice(0, P)),) if i < 3 else
                                  ((aoT[0][0:64, 2 * QW:3 * QW], slice(0, 64)), (aoT[0][0:32, 3 * QW:4 * QW], slice(64, 96)))):
                    ao_ready.by(dve.tensor_tensor(dst, os[rows, 0, :], recip[rows, i % 2, :], ALU.mult))

            def piece(step, B, parity, next_too, is_ahead):
                kind = step[0]
                if kind == "statistics" and next_too:
                    statistics(B + 1)
                if kind == "normalise" and next_too:
                    first_ln.normalise(dve, xn, xn, B + 1, 0)
                if step == ("xT", 2):
                    s = arrived(dve, B, step, is_ahead)
                    v_ready.wait(dve, B - 1)
                    xT_ready[2].by(dve.tensor_scalar(xT[1][:, :], s[:, 0:QW], nw[:, 1:2], nb[:, 1:2], ALU.mult, ALU.add))
                if kind in ("k", "q"):
                    c = step[1]
                    used = USED[(c, kind)]
                    bias = kb if kind == "k" else qb
                    j = "kq".index(kind)
                    before = (kind, 1 - c)
                    bounced[before].wait(dve, B - (c == 0))
                    hi_ready.wait(dve, B, PROJECTIONS.index(step) + 1)
                    s = slots[at[("ahead",) + step] % NSLOT]
                    lo_ready.by(dve.scalar_tensor_tensor(lo[:, j, 0:used], s[:, 0:used], bias[:, c:c + 1],
                                                         hi[:, j, 0:used], ALU.add, ALU.subtract))
                if kind == "v":
                    g = step[1]
                    s = arrived(dve, B, step, is_ahead)
                    v_ready.by(dve.tensor_tensor(V[:, parity, 4 * g:4 * g + 4, :],
                                                 s[:, :].rearrange("p (t n) -> p t n", t=4), each_tile(vb, 4), ALU.add))
                if kind == "nat":
                    _, u, t = step
                    s = arrived(dve, B, step, is_ahead)
                    max_done.by(dve.reduce_max(rowmax[:, 2 * u + t:2 * u + t + 1], s[:, :], AX))
                if kind == "mT":
                    i = step[1]
                    n = 2 * len(BATCHES[i])
                    s = arrived(dve, B, step, is_ahead)
                    placed[i % 2].wait(dve, B - (i < 2), (i + 2) % NB // 2 + 1)
                    maxT_ready.by(dve.tensor_copy(maxT[0:n, i % 2, :], s[0:n, 0:P]))
                if kind == "pv" and step[2] == NT - 1:
                    norms(B, step[1])
                if step == ("out", 0):
                    s = arrived(dve, B, step, is_ahead)
                    x2_ready.wait(dve, B)
                    summed.by(dve.tensor_tensor(total[:, 0:2, :], s[:, 0:2 * D].rearrange("p (t n) -> p t n", t=2),
                                                total[:, 0:2, :], ALU.add))
                if step == ("out", 1):
                    s = arrived(dve, B, step, is_ahead)
                    col = 0
                    for e in range(1, NE):
                        w = width[e]
                        o = s[:, col:col + 2 * w].rearrange("p (t n) -> p t n", t=2)
                        col += 2 * w
                        summed.by(dve.tensor_tensor(total[:, 2 * e:2 * e + 2, 0:w], o, total[:, 2 * e:2 * e + 2, 0:w], ALU.add))
                if kind == "finish":
                    summed.wait(dve, B)
                    own_ln.statistics(dve, total, B, 0)

            loop(dve, piece)

        @block.tensor
        def _(pe):
            for s in (lead_filled, filled, pv_done):
                s.start(pe)
            pe.wait_ge(setup, NSETUP)
            pe.wait_ge(consts, 16 * NCONST)
            mm = nc.tensor.matmul

            def piece(step, B, parity, next_too, is_ahead):
                kind = step[0]
                if kind != "pv" and kind in unslotted:
                    return
                if kind == "pv":
                    _, i, kt = step
                    n = len(BATCHES[i])
                    half, j = divmod(kt, NT // 2)
                    if j == 0:
                        exp_done.wait(pe, B, 2 * FIRST[i] + n * (half + 1))
                    if kt == 0:
                        ao_ready.wait(pe, B - (i < 2), (3, NB + 1, 1, 2)[i])
                        v_ready.wait(pe, B)
                    os = OS[i % 2]
                    for what in range(2):
                        for u in range(n):
                            h = BATCHES[i][u][0]
                            lhsT = ones[:, :] if what else V[:, parity, kt, DH * h:DH * h + DH]
                            last = mm(os[DH * u:DH * u + DH, what, :], lhsT, probs[:, half, u, QW * j:QW * j + QW],
                                      start=kt == 0 and what == 0, stop=kt == NT - 1, skip_group_check=True,
                                      tile_position=(0, DH * u))
                    if j == NT // 2 - 1:
                        pv_done.by(last)
                    return
                s = use(pe, B, step, is_ahead)
                if kind == "xT":
                    if step[1] == 0:
                        pe.wait_ge(first_ln.normed, first_ln.done(B, 0))
                    first, n, c = ((0, 4, 0), (4, 4, 0), (0, 2, 1))[step[1]]
                    for t in range(n):
                        last = nc.tensor.transpose(s[:, P * t:P * t + P], xn[:, first + t, P * c:P * c + P], ident[:, :])
                if kind in ("k", "q"):
                    c = step[1]
                    w = wk if kind == "k" else wq
                    if step == ("k", 0):
                        for r in xT_ready:
                            r.wait(pe, B)
                    cols = slice(P * c, P * c + P)
                    mm(s[:, 0:QW], w[:, 0, cols], xT[0][:, 0:QW], start=True, stop=False)
                    last = mm(s[:, 0:QW], w[:, 1, cols], xT[1][:, :], start=False, stop=True)
                    if kind == "k" or c == 0:
                        mm(s[:, QW:2 * QW], w[:, 0, cols], xT[0][:, QW:2 * QW], start=True, stop=True)
                        last = mm(s[:, 2 * QW:T], w[:, 0, cols], xT[0][:, 2 * QW:T], start=True, stop=True)
                if kind == "v":
                    for t in range(4):
                        tok = 4 * step[1] + t
                        o = s[:, D * t:D * t + D]
                        last = mm(o, xT[0][:, P * tok:P * tok + P], wv[:, 0, :], start=True, stop=tok >= 2)
                        if tok < 2:
                            last = mm(o, xT[1][:, P * tok:P * tok + P], wv[:, 1, :], start=False, stop=True)
                if kind == "nat":
                    _, u, t = step
                    if u == 0 and t == 0:
                        stacked[0].wait(pe, B)
                    if u == FIRST[1] and t == 0:
                        stacked[1].wait(pe, B)
                    if u == FIRST[2] and t == 0:
                        rest_stacked.wait(pe, B)
                    for half in range(2):
                        last = mm(s[:, 512 * half:512 * half + 512], Qs[0:96, parity, u, P * t:P * t + P],
                                  Ks[0:96, parity, UNITS[u][0], 512 * half:512 * half + 512], start=True, stop=True)
                if kind == "mT":
                    i = step[1]
                    n = 2 * len(BATCHES[i])
                    max_done.wait(pe, B, 2 * FIRST[i] + n)
                    last = nc.tensor.transpose(s[0:n, 0:P], rowmax[:, 2 * FIRST[i]:2 * FIRST[i] + n], ident[:, :])
                if kind == "tr":
                    _, u, half = step
                    if half == 0 and u in FIRST:
                        i = FIRST.index(u)
                        placed[i % 2].wait(pe, B, i // 2 + 1)
                    for j in range(4):
                        kt = 4 * half + j
                        last = mm(s[:, QW * j:QW * j + QW], Ks[:, parity, UNITS[u][0], P * kt:P * kt + P], Qs[:, parity, u, :],
                                  start=True, stop=True)
                if kind == "out":
                    if step[1] == 0:
                        ao_ready.wait(pe, B)
                    col = 0
                    for e in ((0,), range(1, NE))[step[1]]:
                        w = width[e]
                        for t in (2 * e, 2 * e + 1):
                            k = min(w, P)
                            last = mm(s[:, col:col + w], aoT[0][0:k, P * t:P * t + P], wo[0:k, 0, 0:w], start=True, stop=w <= P)
                            if w > P:
                                last = mm(s[:, col:col + w], aoT[1][:, P * t:P * t + P], wo[:, 1, 0:w], start=False, stop=True)
                            col += w
                (lead_filled if is_ahead else filled).by(last)

            loop(pe, piece)


def four_layers(nc, x, wq, wk, bq, bk, wv, bv, wo, bo, cos, sin, mask, maskT, ident, ident16,
                controller, f1, f2, f1_bias, tie, wqkv, wproj, bproj, head_blocks,
                q_w, q_b, k_w, k_b, v_w, v_b, o_w, o_b, norm_w, norm_b, out):
    def dram(name, shape):
        return nc.dram_tensor(name, shape, f32, kind="Internal").ap()

    x1, x2, x3 = (dram(f"x{i}", (NSEQ, T, D)) for i in (1, 2, 3))
    window_attention_layer(nc, x, x1, wq, wk, bq, bk, wv, bv, wo, bo, cos, sin, mask, maskT, ident, ident16,
                           dram("qk_rows", (2, 2, 16, 16, T)))
    token_choice_layer(nc, x1, x2, controller, f1, f2, f1_bias, tie, ident, dram("expert_outputs", (2, 128, 32, D)))
    linear_attention_layer(nc, x2, x3, wqkv, wproj, bproj, ident, head_blocks)
    nested_width_attention_layer(nc, x3, out, q_w, q_b, k_w, k_b, v_w, v_b, o_w, o_b, norm_w, norm_b, ident, dram("kq_rows", (2, 2, D, T)))


def shape_constants():
    import numpy as np

    half, blocked = 8, -1e30
    inv_freq = (np.float32(1.0) / np.float32(10000.0) ** (np.arange(half, dtype=np.float32) / np.float32(half))).astype(np.float32)
    ang = np.arange(T, dtype=np.float32)[:, None] * inv_freq[None, :]
    i = np.arange(P)
    before = lambda key, query: np.where(key >= query, 0.0, blocked)
    own = lambda key, query: np.where(key <= query, 0.0, blocked)
    heads = np.zeros((P, P + 8), np.float32)
    heads[:, :P] = i[:, None] // 16 == i[None, :] // 16
    heads[:, P:] = i[:, None] // 16 == np.arange(8)[None, :]
    bf = mybir.dt.np(bf16)
    return {
        "cos": np.ascontiguousarray(np.tile(np.cos(ang).astype(np.float32).T, (16, 1))),
        "sin": np.ascontiguousarray(np.tile(np.sin(ang).astype(np.float32).T, (16, 1))),
        "mask": np.concatenate([before(i[None, :], i[:, None]), own(i[None, :], i[:, None])], 1).astype(bf),
        "maskT": np.concatenate([before(i[:, None], i[None, :]), own(i[:, None], i[None, :])], 1).astype(bf),
        "ident": np.eye(P, dtype=np.float32), "ident16": np.eye(P, dtype=np.float32).astype(bf),
        "tie": np.linspace(0.0, 1e-6, 16, dtype=np.float32), "heads": heads,
    }


def kernel(**inputs):
    import numpy as np
    import concourse.bacc as bacc
    from concourse.bass_utils import run_bass_kernel_spmd as run

    a = {k: np.asarray(v) for k, v in inputs.items()}
    c = shape_constants()
    order = np.arange(D).reshape(16, 2, 8).transpose(1, 0, 2).reshape(D)
    column = lambda v: v.reshape(-1, P).T
    wqkv = a["L1_attn_Wqkv"].T
    args = [
        a["L0_attn_x"], a["L0_attn_Wq"][order].T, a["L0_attn_Wk"][order].T, column(a["L0_attn_bq"][order]),
        column(a["L0_attn_bk"][order]), a["L0_attn_Wv"].T, a["L0_attn_bv"], a["L0_attn_Wo"].T, a["L0_attn_bo"],
        c["cos"], c["sin"], c["mask"], c["maskT"], c["ident"], c["ident16"],
        a["L0_ffn_controller"].reshape(D, 64), a["L0_ffn_f1"].reshape(D, 64, 64), a["L0_ffn_f2"].reshape(64, 64, D),
        column(a["L0_ffn_bias"]), c["tie"],
        wqkv, a["L1_attn_Wproj"].T, a["L1_attn_bproj"], c["heads"],
        a["L1_ffn_q_w"].T, column(a["L1_ffn_q_b"]), a["L1_ffn_k_w"].T, column(a["L1_ffn_k_b"]), a["L1_ffn_v_w"].T,
        a["L1_ffn_v_b"], a["L1_ffn_o_w"].T, a["L1_ffn_o_b"], column(a["L1_ffn_norm_w"]), column(a["L1_ffn_norm_b"]),
    ]
    nc = bacc.Bacc("TRN2", target_bir_lowering=False, num_devices=1)
    arrays, aps = {}, []
    for i, v in enumerate(args):
        v = np.ascontiguousarray(v)
        arrays[f"in_{i}_dram"] = v
        aps.append(nc.dram_tensor(f"in_{i}_dram", v.shape, mybir.dt.from_np(v.dtype), kind="ExternalInput").ap())
    out = nc.dram_tensor("out_dram", (NSEQ, T, D), f32, kind="ExternalOutput").ap()
    four_layers(nc, *aps, out)
    r = run(nc, [arrays], core_ids=[0])
    return r.results[0]["out_dram"]
```
